# Optimizing a Trainium2 kernel written in Bass

```python
import numpy as np
import jax
import jax.numpy as jnp

def _softmax(x, axis=-1):
    return jax.nn.softmax(x, axis=axis)

def _gelu(x):
    return jax.nn.gelu(x, approximate=True)

def _silu(x):
    return jax.nn.silu(x)

def _sigmoid(x):
    return jax.nn.sigmoid(x)

def _layernorm(x, axis=-1, eps=1e-05):
    m = jnp.mean(x, axis=axis, keepdims=True)
    v = jnp.var(x, axis=axis, keepdims=True)
    return (x - m) / jnp.sqrt(v + eps)

def _scatter_add(tgt, idx, src, axis=0):
    return tgt.at[idx].add(src)

def _segment_sum(src, seg, n):
    return jax.ops.segment_sum(src, seg, n)
kernel_name = 'mk_flamingo_gated_d2_seqx_r8_d09d7f'

def setup_inputs(seed: int=0):
    np.random.seed(seed)
    _w = jnp.asarray

    def _rec_inputs():
        import jax
        import jax.numpy as jnp
        _rk = jax.random.key(seed)
        x = -0.0002928 + 1 * jax.random.normal(jax.random.fold_in(_rk, 1), (8, 128, 256), jnp.float32)
        _lenS = 128 - jax.random.randint(jax.random.fold_in(_rk, 7), (8,), 0, max(1, 128 // 4) + 1, jnp.int32)
        _lenS2 = 128 - jax.random.randint(jax.random.fold_in(_rk, 8), (8,), 0, max(1, 128 // 4) + 1, jnp.int32)
        _ctx_2048P = jax.random.normal(jax.random.fold_in(_rk, 11), (8, 16, 256), jnp.float32)
        _ctx_2048c = jax.random.dirichlet(jax.random.fold_in(_rk, 511), 0.3 * jnp.ones((16,), jnp.float32), (8, 128))
        _ctx_2048t = jnp.einsum('bsk,bkd->bsd', _ctx_2048c, _ctx_2048P)
        _ctx_2048t = _ctx_2048t * jax.lax.rsqrt(jnp.mean(jnp.square(_ctx_2048t)) + 1e-12) * 0.953939
        ctx_2048 = -1.39393e-06 + 0.999914 * (_ctx_2048t + 0.3 * jax.random.normal(jax.random.fold_in(_rk, 611), (8, 128, 256), jnp.float32))
        _validS = jnp.arange(128)[None, :] < _lenS[:, None]
        _validS2 = jnp.arange(128)[None, :] < _lenS2[:, None]
        _causal = jnp.tril(jnp.ones((128, 128), dtype=bool))
        mask_Bx1x2048_fk1 = jnp.where(jnp.ones((8, 1, 256), dtype=bool), 1.0, 0.0).astype(jnp.float32)
        _g = jax.random.normal(jax.random.fold_in(_rk, 9001), (2, 2), jnp.float32)
        _g = jnp.sign(_g) * jnp.maximum(jnp.abs(_g), 1.0) + (_g == 0) * 1.0
        g_xattn = _g[0]
        g_ffn = _g[1]
        return (x, ctx_2048, mask_Bx1x2048_fk1, g_xattn, g_ffn)
    x, ctx_2048, mask_Bx1x2048_fk1, g_xattn, g_ffn = _rec_inputs()

    def _L0_xattn_setup():
        import math
        import jax, jax.numpy as jnp
        import numpy as np
        SIZE = 128
        HEADS = 16
        HEAD_DIM = SIZE // HEADS
        B, T, S = (2, 256, 256)
        NEG = 1000000.0
        key = jax.random.key(seed)
        ks = jax.random.split(key, 10)
        target = jax.random.normal(ks[0], (B, SIZE, T), dtype=jnp.float32)
        source = jax.random.normal(ks[1], (B, SIZE, S), dtype=jnp.float32)
        target_mask = (jax.random.uniform(ks[2], (B, 1, T)) > 0.1).astype(jnp.float32)
        source_mask = (jax.random.uniform(ks[3], (B, 1, S)) > 0.1).astype(jnp.float32)
        scale = 1.0 / math.sqrt(SIZE)
        Wq = jax.random.normal(ks[4], (SIZE, SIZE), dtype=jnp.float32) * scale
        Wk = jax.random.normal(ks[5], (SIZE, SIZE), dtype=jnp.float32) * scale
        Wv = jax.random.normal(ks[6], (SIZE, SIZE), dtype=jnp.float32) * scale
        bq = jax.random.normal(ks[7], (SIZE,), dtype=jnp.float32) * 0.01
        bk = jax.random.normal(ks[8], (SIZE,), dtype=jnp.float32) * 0.01
        bv = jax.random.normal(ks[9], (SIZE,), dtype=jnp.float32) * 0.01
        return {'target': target, 'source': source, 'target_mask': target_mask, 'source_mask': source_mask, 'Wq': Wq, 'bq': bq, 'Wk': Wk, 'bk': bk, 'Wv': Wv, 'bv': bv}
    _L0_xattn_all = _L0_xattn_setup()
    _L0_xattn_in = {k: v for k, v in _L0_xattn_all.items() if k in ('Wq', 'bq', 'Wk', 'bk', 'Wv', 'bv')}
    del _L0_xattn_all

    def _L0_ffn_setup():
        import jax, jax.numpy as jnp
        import numpy as np
        MIN_EXPERTS = 2
        NEG_INF = -1000000000.0

        def _l2norm(x, axis):
            return x / jnp.maximum(jnp.linalg.norm(x, axis=axis, keepdims=True), 1e-12)

        def _ste(x):
            return x + jax.lax.stop_gradient((x > 0).astype(x.dtype) - x)

        def _forward(hidden_states, sim_matrix, gates, q_proj, k_proj, v_proj, o_proj):
            B, T, C = hidden_states.shape
            E = gates.shape[0]
            H = q_proj.shape[-1]
            x = hidden_states.reshape(B * T, C)
            logits = _l2norm(x, -1) @ _l2norm(sim_matrix, 0) - jax.nn.sigmoid(gates)
            gated = jax.nn.relu(logits)
            mask = _ste(gated)
            inactive = jnp.sum(mask, axis=1) == 0
            fb_idx = jax.lax.top_k(logits, MIN_EXPERTS)[1]
            fb_mask = jnp.max(jax.nn.one_hot(fb_idx, E, dtype=mask.dtype), axis=1)
            mask = jnp.where(inactive[:, None] & (fb_mask > 0), jnp.ones_like(mask), mask)
            masked_logits = jnp.where(mask > 0, gated, jnp.full_like(gated, NEG_INF))
            probs = jax.nn.softmax(masked_logits, axis=-1)
            w = probs * (mask > 0)

            def mix(proj):
                pe = jnp.einsum('nc,ech->neh', x, proj)
                return jnp.einsum('ne,neh->nh', w, pe).reshape(B, T, H)
            q, k, v = (mix(q_proj), mix(k_proj), mix(v_proj))
            scale = 1.0 / jnp.sqrt(jnp.asarray(H, dtype=q.dtype))
            scores = jnp.einsum('bqh,bkh->bqk', q, k) * scale
            causal = jnp.tril(jnp.ones((T, T), dtype=bool))
            scores = jnp.where(causal[None], scores, jnp.full_like(scores, NEG_INF))
            attn = jax.nn.softmax(scores, axis=-1)
            ao = jnp.einsum('bqk,bkh->bqh', attn, v).reshape(B * T, H)
            wa = jnp.einsum('ne,nh->enh', w, ao)
            out = jnp.einsum('enh,ehc->nc', wa, o_proj)
            return out.reshape(B, T, C)
        key = jax.random.key(seed)
        ks = jax.random.split(key, 6)
        B, T, C, H, E = (4, 256, 256, 128, 16)
        xavier_qkv = float(np.sqrt(2.0 / (C + H)))
        return {'hidden_states': jax.random.normal(ks[0], (B, T, C), dtype=jnp.float32), 'sim_matrix': jax.random.normal(ks[1], (C, E), dtype=jnp.float32), 'gates': jnp.full((E,), -6.0, dtype=jnp.float32), 'q_proj': jax.random.normal(ks[2], (E, C, H), dtype=jnp.float32) * xavier_qkv, 'k_proj': jax.random.normal(ks[3], (E, C, H), dtype=jnp.float32) * xavier_qkv, 'v_proj': jax.random.normal(ks[4], (E, C, H), dtype=jnp.float32) * xavier_qkv, 'o_proj': jax.random.normal(ks[5], (E, H, C), dtype=jnp.float32) * xavier_qkv}
    _L0_ffn_all = _L0_ffn_setup()
    _L0_ffn_in = {k: v for k, v in _L0_ffn_all.items() if k in ('sim_matrix', 'gates', 'q_proj', 'k_proj', 'v_proj', 'o_proj')}
    del _L0_ffn_all

    def _L1_xattn_setup():
        import jax, jax.numpy as jnp
        import numpy as np
        B_DIM, T_DIM, C_DIM = (16, 128, 256)

        def _wkv(w, u, k, v):
            Bn, Tn, Cn = k.shape
            NEG_INF = jnp.float32(-1e+38)

            def step(carry, kv_t):
                p, q, o = carry
                kt, vt = kv_t
                no = jnp.maximum(o, u + kt)
                A = jnp.exp(o - no)
                E = jnp.exp(u + kt - no)
                y = (A * p + E * vt) / (A * q + E)
                no2 = jnp.maximum(w + o, kt)
                A2 = jnp.exp(w + o - no2)
                E2 = jnp.exp(kt - no2)
                return ((A2 * p + E2 * vt, A2 * q + E2, no2), y)
            init = (jnp.zeros((Bn, Cn), k.dtype), jnp.zeros((Bn, Cn), k.dtype), jnp.full((Bn, Cn), NEG_INF, k.dtype))
            kT = jnp.moveaxis(k, 1, 0)
            vT = jnp.moveaxis(v, 1, 0)
            _, yT = jax.lax.scan(step, init, (kT, vT))
            return jnp.moveaxis(yT, 0, 1)
        key = jax.random.key(seed)
        k1, k2, k3, k4 = jax.random.split(key, 4)
        w = -jnp.exp(jax.random.normal(k1, (C_DIM,), jnp.float32))
        u = jax.random.normal(k2, (C_DIM,), jnp.float32)
        k = jax.random.normal(k3, (B_DIM, T_DIM, C_DIM), jnp.float32)
        v = jax.random.normal(k4, (B_DIM, T_DIM, C_DIM), jnp.float32)
        return {'B': B_DIM, 'T': T_DIM, 'C': C_DIM, 'w': w, 'u': u, 'k': k, 'v': v}
    _L1_xattn_all = _L1_xattn_setup()
    _L1_xattn_in = {k: v for k, v in _L1_xattn_all.items() if k in ('w', 'u')}
    del _L1_xattn_all

    def _L1_ffn_setup():
        import jax, jax.numpy as jnp
        import numpy as np
        B, S, H, E = (4, 256, 256, 8)
        key = jax.random.key(seed)
        k_x, k_wg, k_w, k_b = jax.random.split(key, 4)
        x = jax.random.normal(k_x, (B, S, H), dtype=jnp.float32)
        wg = jax.random.normal(k_wg, (H, E), dtype=jnp.float32) * (1.0 / np.sqrt(H))
        W = jax.random.normal(k_w, (E, H, H), dtype=jnp.float32) * (1.0 / np.sqrt(H))
        b = jax.random.normal(k_b, (E, H), dtype=jnp.float32) * 0.01
        return {'x': x, 'wg': wg, 'W': W, 'b': b}
    _L1_ffn_all = _L1_ffn_setup()
    _L1_ffn_in = {k: v for k, v in _L1_ffn_all.items() if k in ('wg', 'W', 'b')}
    del _L1_ffn_all
    return {'x': x, 'ctx_2048': ctx_2048, 'mask_Bx1x2048_fk1': mask_Bx1x2048_fk1, 'g_xattn': g_xattn, 'g_ffn': g_ffn, 'L0_xattn_Wq': _L0_xattn_in['Wq'], 'L0_xattn_bq': _L0_xattn_in['bq'], 'L0_xattn_Wk': _L0_xattn_in['Wk'], 'L0_xattn_bk': _L0_xattn_in['bk'], 'L0_xattn_Wv': _L0_xattn_in['Wv'], 'L0_xattn_bv': _L0_xattn_in['bv'], 'L0_ffn_sim_matrix': _L0_ffn_in['sim_matrix'], 'L0_ffn_gates': _L0_ffn_in['gates'], 'L0_ffn_q_proj': _L0_ffn_in['q_proj'], 'L0_ffn_k_proj': _L0_ffn_in['k_proj'], 'L0_ffn_v_proj': _L0_ffn_in['v_proj'], 'L0_ffn_o_proj': _L0_ffn_in['o_proj'], 'L1_xattn_w': _L1_xattn_in['w'], 'L1_xattn_u': _L1_xattn_in['u'], 'L1_ffn_wg': _L1_ffn_in['wg'], 'L1_ffn_W': _L1_ffn_in['W'], 'L1_ffn_b': _L1_ffn_in['b']}

def reference(x, ctx_2048, mask_Bx1x2048_fk1, g_xattn, g_ffn, L0_xattn_Wq, L0_xattn_bq, L0_xattn_Wk, L0_xattn_bk, L0_xattn_Wv, L0_xattn_bv, L0_ffn_sim_matrix, L0_ffn_gates, L0_ffn_q_proj, L0_ffn_k_proj, L0_ffn_v_proj, L0_ffn_o_proj, L1_xattn_w, L1_xattn_u, L1_ffn_wg, L1_ffn_W, L1_ffn_b):
    import jax
    import jax.numpy as jnp

    def _L0_xattn_ref(target, source, target_mask, source_mask, Wq, bq, Wk, bk, Wv, bv):
        import math
        import jax, jax.numpy as jnp
        import numpy as np
        SIZE = 128
        HEADS = 16
        HEAD_DIM = SIZE // HEADS
        B, T, S = (2, 256, 256)
        NEG = 1000000.0
        b, _, t = target.shape
        s = source.shape[-1]
        q = jnp.einsum('oc,bct->bot', Wq, target) + bq[None, :, None]
        k = jnp.einsum('oc,bcs->bos', Wk, source) + bk[None, :, None]
        v = jnp.einsum('oc,bcs->bos', Wv, source) + bv[None, :, None]
        q = q.reshape(b, HEADS, HEAD_DIM, t)
        k = k.reshape(b, HEADS, HEAD_DIM, s)
        v = v.reshape(b, HEADS, HEAD_DIM, s)
        dot = jnp.einsum('bhdt,bhds->bhts', q, k) / math.sqrt(HEAD_DIM)
        mask = target_mask[:, :, :, None] * source_mask[:, :, None, :]
        dot = mask * dot - (1.0 - mask) * NEG
        amap = jax.nn.softmax(dot, axis=-1) * mask
        out = jnp.einsum('bhts,bhds->bhdt', amap, v)
        return out.reshape(b, HEADS * HEAD_DIM, t)

    def _L0_ffn_ref(hidden_states, sim_matrix, gates, q_proj, k_proj, v_proj, o_proj):
        import jax, jax.numpy as jnp
        import numpy as np
        MIN_EXPERTS = 2
        NEG_INF = -1000000000.0

        def _l2norm(x, axis):
            return x / jnp.maximum(jnp.linalg.norm(x, axis=axis, keepdims=True), 1e-12)

        def _ste(x):
            return x + jax.lax.stop_gradient((x > 0).astype(x.dtype) - x)

        def _forward(hidden_states, sim_matrix, gates, q_proj, k_proj, v_proj, o_proj):
            B, T, C = hidden_states.shape
            E = gates.shape[0]
            H = q_proj.shape[-1]
            x = hidden_states.reshape(B * T, C)
            logits = _l2norm(x, -1) @ _l2norm(sim_matrix, 0) - jax.nn.sigmoid(gates)
            gated = jax.nn.relu(logits)
            mask = _ste(gated)
            inactive = jnp.sum(mask, axis=1) == 0
            fb_idx = jax.lax.top_k(logits, MIN_EXPERTS)[1]
            fb_mask = jnp.max(jax.nn.one_hot(fb_idx, E, dtype=mask.dtype), axis=1)
            mask = jnp.where(inactive[:, None] & (fb_mask > 0), jnp.ones_like(mask), mask)
            masked_logits = jnp.where(mask > 0, gated, jnp.full_like(gated, NEG_INF))
            probs = jax.nn.softmax(masked_logits, axis=-1)
            w = probs * (mask > 0)

            def mix(proj):
                pe = jnp.einsum('nc,ech->neh', x, proj)
                return jnp.einsum('ne,neh->nh', w, pe).reshape(B, T, H)
            q, k, v = (mix(q_proj), mix(k_proj), mix(v_proj))
            scale = 1.0 / jnp.sqrt(jnp.asarray(H, dtype=q.dtype))
            scores = jnp.einsum('bqh,bkh->bqk', q, k) * scale
            causal = jnp.tril(jnp.ones((T, T), dtype=bool))
            scores = jnp.where(causal[None], scores, jnp.full_like(scores, NEG_INF))
            attn = jax.nn.softmax(scores, axis=-1)
            ao = jnp.einsum('bqk,bkh->bqh', attn, v).reshape(B * T, H)
            wa = jnp.einsum('ne,nh->enh', w, ao)
            out = jnp.einsum('enh,ehc->nc', wa, o_proj)
            return out.reshape(B, T, C)
        return _forward(hidden_states, sim_matrix, gates, q_proj, k_proj, v_proj, o_proj)

    def _L1_xattn_ref(B, T, C, w, u, k, v):
        import jax, jax.numpy as jnp
        import numpy as np
        B_DIM, T_DIM, C_DIM = (16, 128, 256)

        def _wkv(w, u, k, v):
            Bn, Tn, Cn = k.shape
            NEG_INF = jnp.float32(-1e+38)

            def step(carry, kv_t):
                p, q, o = carry
                kt, vt = kv_t
                no = jnp.maximum(o, u + kt)
                A = jnp.exp(o - no)
                E = jnp.exp(u + kt - no)
                y = (A * p + E * vt) / (A * q + E)
                no2 = jnp.maximum(w + o, kt)
                A2 = jnp.exp(w + o - no2)
                E2 = jnp.exp(kt - no2)
                return ((A2 * p + E2 * vt, A2 * q + E2, no2), y)
            init = (jnp.zeros((Bn, Cn), k.dtype), jnp.zeros((Bn, Cn), k.dtype), jnp.full((Bn, Cn), NEG_INF, k.dtype))
            kT = jnp.moveaxis(k, 1, 0)
            vT = jnp.moveaxis(v, 1, 0)
            _, yT = jax.lax.scan(step, init, (kT, vT))
            return jnp.moveaxis(yT, 0, 1)
        return _wkv(w, u, k, v)

    def _L1_ffn_ref(x, wg, W, b):
        import jax, jax.numpy as jnp
        import numpy as np
        B, S, H, E = (4, 256, 256, 8)
        Bv, Sv, Hv = x.shape
        Ev = W.shape[0]
        xt = x.reshape(-1, Hv)
        logits = xt @ wg
        probs = jax.nn.softmax(logits, axis=-1)
        idx = jnp.argmax(probs, axis=-1)
        gate = jnp.take_along_axis(probs, idx[:, None], axis=1)
        onehot = jax.nn.one_hot(idx, Ev, dtype=x.dtype)
        expert_out = jnp.einsum('nh,eoh->neo', xt, W) + b[None, :, :]
        combine = onehot * gate
        out = jnp.einsum('ne,neo->no', combine, expert_out)
        return out.reshape(Bv, Sv, Hv)
    x = x + jnp.tanh(g_xattn[0]) * _L0_xattn_ref(_layernorm(x, axis=-1), ctx_2048, mask_Bx1x2048_fk1, mask_Bx1x2048_fk1, L0_xattn_Wq, L0_xattn_bq, L0_xattn_Wk, L0_xattn_bk, L0_xattn_Wv, L0_xattn_bv)
    x = x + jnp.tanh(g_ffn[0]) * _L0_ffn_ref(_layernorm(x, axis=-1), L0_ffn_sim_matrix, L0_ffn_gates, L0_ffn_q_proj, L0_ffn_k_proj, L0_ffn_v_proj, L0_ffn_o_proj)
    x = x + jnp.tanh(g_xattn[1]) * _L1_xattn_ref(8, 128, 256, L1_xattn_w, L1_xattn_u, _layernorm(x, axis=-1), ctx_2048)
    x = x + jnp.tanh(g_ffn[1]) * _L1_ffn_ref(_layernorm(x, axis=-1), L1_ffn_wg, L1_ffn_W, L1_ffn_b)
    return x

_drawn_inputs = setup_inputs


def setup_inputs(seed=0):
    import zlib

    import numpy as np

    out = dict(_drawn_inputs(seed))
    spreads = {'g_ffn': (-1.0, 0.6), 'L0_ffn_gates': (-6.0, 0.6)}
    factors = {'L0_xattn_bq': 8.0,
     'L0_xattn_bk': 64.0,
     'L0_xattn_bv': 8.0,
     'L0_ffn_q_proj': 4.56,
     'L0_ffn_k_proj': 6.798,
     'L1_ffn_b': 22.214}
    for name, (base, spread) in spreads.items():
        noise = np.random.default_rng([zlib.crc32(name.encode()), seed]).standard_normal(out[name].shape)
        drawn = base * np.exp(spread * noise) if base else spread * noise
        out[name] = jnp.asarray(drawn.astype(out[name].dtype))
    for name, factor in factors.items():
        out[name] = (out[name] * factor).astype(out[name].dtype)
    return out
```

```python
from contextlib import ExitStack

import concourse.bass as bass
from concourse import mybir

ALU = mybir.AluOpType
ACT = mybir.ActivationFunctionType
AX = mybir.AxisListType
F32 = mybir.dt.float32
F32R = mybir.dt.float32r
U32 = mybir.dt.uint32

P = 128
NH = 16
HD = P // NH
QUADS = NH // 4
NEG_MASK = 1.0e6
NEG_CAUSAL = 1.0e9
NEG_START = -1.0e38
EPS = 1.0e-5


def head_of(quad, j):
    return 8 * (quad // 2) + 2 * j + quad % 2


class Tally:

    def __init__(self, sem):
        self.sem, self.n = sem, 0

    def step(self, instruction):
        instruction.then_inc(self.sem, 1)
        self.n += 1
        return self.n


class Bank:

    def __init__(self, psum):
        self.psum, self.reader = psum, None

    def take(self, engine, sem, value):
        if self.reader is not None:
            engine.wait_ge(*self.reader)
        self.reader = (sem, value)
        return self.psum


def flamingo_two_layers(nc, x, ctx, ctxT, mask, maskT, g_xattn, g_ffn, wqT, wkT, wvT, bq, bk, bv, sim, gates,
                        wqkv, wo, wkv_w, wkv_u, wg, w1T, b1, out):
    NB, _, T = x.shape
    CC = T // P
    NE = wqkv.shape[0]
    QKV = wqkv.shape[2]
    HID = QKV // 3
    NE1 = w1T.shape[0]
    XATTN_SCALE = float(HD) ** -0.5
    FFN_SCALE = float(HID) ** -0.5

    es = ExitStack()
    with es:
        def sb(name, shape, dt=F32):
            return es.enter_context(nc.sbuf_tensor(name, shape, dt))

        def sem(name):
            return es.enter_context(nc.semaphore(name))

        x_sb = sb("x_sb", [P, NB, T])
        mask_bc = sb("mask_bc", [P, NB, T])
        mask_col = sb("mask_col", [P, CC, NB])
        ctx_b = [sb(f"ctx_b{i}", [P, T]) for i in range(2)]
        ctxT_sb = sb("ctxT_sb", [P, CC, NB, P])
        wqT_sb, wkT_sb, wvT_sb = (sb(n, [P, P]) for n in ("wqT_sb", "wkT_sb", "wvT_sb"))
        bq_sb, bk_sb = sb("bq_sb", [P, 1]), sb("bk_sb", [P, 1])
        bv_sb = sb("bv_sb", [1, P])
        gx_sb, gf_sb = sb("gx_sb", [P, 2]), sb("gf_sb", [P, 2])
        tgx, tgf = sb("tgx", [P, 2]), sb("tgf", [P, 2])
        sim_sb = sb("sim_sb", [P, CC, NE])
        gates_sb = sb("gates_sb", [P, NE])
        wg_sb = sb("wg_sb", [P, CC, NE1])
        b1_sb = sb("b1_sb", [NE1, T])
        w_sb, u_sb = sb("w_sb", [P, CC]), sb("u_sb", [P, CC])
        ident = sb("ident", [P, P])
        ones = sb("ones", [P, P])
        zeros = sb("zeros", [P, P])
        minus_half = sb("minus_half", [P, NE])
        iota_e = sb("iota_e", [P, NE])
        causal = sb("causal", [P, P])
        causal_neg = sb("causal_neg", [P, P])
        arena = sb("arena", [P, 8 * QUADS * T], F32R)
        sel_q_hi, sel_q_lo, sel_k_hi, sel_k_lo = (
            arena[:, n * QUADS * P:(n + 1) * QUADS * P].rearrange("p (q n) -> p q n", q=QUADS) for n in range(4))
        sel_aux_q, sel_aux_k = (
            arena[:, (2 + n) * NB * P:(3 + n) * NB * P].rearrange("p (b n) -> p b n", b=NB) for n in range(2))
        q_stack0, q_stack1, q_stack_max, k_stack = (
            arena[:, (4 + n) * QUADS * T:(5 + n) * QUADS * T].rearrange("p (q t) -> p q t", q=QUADS)
            for n in range(4))
        q_stack = [q_stack0, q_stack1]
        sel_max = sb("sel_max", [2 * NH, QUADS, P], F32R)
        row_q, row_k = sb("row_q", [P, P]), sb("row_k", [P, P])
        batch_row = sb("batch_row", [P, NB])
        mask8 = sb("mask8", [P, T])
        aux_f = sb("aux_f", [P, 2, T])
        aux_q, aux_k = sb("aux_q", [P, T], F32R), sb("aux_k", [P, T], F32R)
        bn6 = sb("bn6", [P, NB, 6])
        mv = sb("mv", [P, NB, 2])
        var_eps, rstd = sb("var_eps", [P, NB]), sb("rstd", [P, NB])
        xn = sb("xn", [P, T])
        q_f, k_f = sb("q_f", [P, T]), sb("k_f", [P, T])
        q_hi, q_lo, k_hi, k_lo = (sb(n, [P, T], F32R) for n in ("q_hi", "q_lo", "k_hi", "k_lo"))
        k_pad = [sb(f"k_pad{i}", [P, 4, QUADS, T], F32R) for i in range(2)]
        v_pad = [sb(f"v_pad{i}", [P, CC, NH, 32]) for i in range(2)]
        mx = sb("mx", [P, CC, NH])
        neg_max = sb("neg_max", [P, CC, 2, NH], F32R)
        max_rows = sb("max_rows", [2 * NH, T], F32R)
        probs = sb("probs", [P, 8, CC, T])
        o_raw = sb("o_raw", [P, 2, T])
        o_den = sb("o_den", [P, CC, 2 * NH // 2])
        o_tok = sb("o_tok", [P, CC, P])
        bn6f, mvf = sb("bn6f", [P, 6]), sb("mvf", [P, 2])
        vef, rstdf = sb("vef", [P, 1]), sb("rstdf", [P, 1])
        xn_f = sb("xn_f", [P, T])
        sq_junk = sb("sq_junk", [P, T])
        nsq, rnorm = sb("nsq", [P, NB]), sb("rnorm", [P, NB])
        xT_hi, xT_lo = (sb(n, [P, NB, CC, P], F32R) for n in ("xT_hi", "xT_lo"))
        simn = sb("simn", [P, CC, NE])
        sim_sq = sb("sim_sq", [P, CC, NE])
        sim_r = sb("sim_r", [P, NE])
        sim_hi, sim_lo = sb("sim_hi", [P, CC, NE], F32R), sb("sim_lo", [P, CC, NE], F32R)
        sgate = sb("sgate", [P, NE])
        lg, gated, pos, fb = (sb(n, [P, NB, NE]) for n in ("lg", "gated", "pos", "fb"))
        top8, topi_f = sb("top8", [P, NB, 8]), sb("topi_f", [P, NB, 8])
        topi = sb("topi", [P, NB, 8], U32)
        inact, gmax, esum, ersum = (sb(n, [P, NB]) for n in ("inact", "gmax", "esum", "ersum"))
        w_e, w_et = sb("w_e", [P, NB, NE]), sb("w_et", [P, NB, NE])
        w_raw, w_hi, w_lo = ([sb(f"{n}{i}", [P, CC, QKV], d) for i in range(2)]
                             for n, d in (("w_raw", F32), ("w_hi", F32R), ("w_lo", F32R)))
        s_raw = [sb(f"s_raw{i}", [P, 2 * T]) for i in range(2)]
        qkv = probs[:].rearrange("p s c t -> p (s c t)")[:, 0:NB * QKV].rearrange("p (b n) -> p b n", b=NB)
        o_hi = k_pad[0][:].rearrange("p j q t -> p (j q) t")
        o_lo = k_pad[1][:].rearrange("p j q t -> p (j q) t")
        w1_hi, w1_lo = (arena[:, n * CC * NE1 * T:(n + 1) * CC * NE1 * T].rearrange("p (c e t) -> p c e t", c=CC, e=NE1)
                        for n in range(2))
        qkT = sb("qkT", [P, 2, P])
        scr, pat, patT = sb("scr", [P, P]), sb("pat", [P, P]), sb("patT", [P, P])
        row_m, row_nm, row_s, row_r = (sb(n, [P, 1]) for n in ("row_m", "row_nm", "row_s", "row_r"))
        ao_hi, ao_lo = sb("ao_hi", [P, P], F32R), sb("ao_lo", [P, P], F32R)
        acc_odd = q_f
        w_full, u_full = sb("w_full", [P, CC, P]), sb("u_full", [P, CC, P])
        kn = ctx_b[0]
        kT = sb("kT", [P, CC, P])
        o_ext = sb("o_ext", [P, CC, P + 1])
        uk, no, ow = sb("uk", [P, CC, P]), sb("no", [P, CC, P]), sb("ow", [P, CC, P])
        arg1, arg2, e1, e2 = (mask_bc[:, 2 * n:2 * n + 2, :] for n in range(4))
        ev, e2v = sb("ev", [P, T]), sb("e2v", [P, T])
        pq = sb("pq", [P, 2, T + 1])
        num, den, yT = ctx_b[1], xn, sb("yT", [P, CC, P])
        xn_1 = sb("xn_1", [P, T])
        x1_hi, x1_lo = sb("x1_hi", [P, CC, P], F32R), sb("x1_lo", [P, CC, P], F32R)
        wg_hi, wg_lo = sb("wg_hi", [P, CC, NE1], F32R), sb("wg_lo", [P, CC, NE1], F32R)
        lg1, ex1, comb = sb("lg1", [P, NE1]), sb("ex1", [P, NE1]), sb("comb", [P, NE1])
        m8, i8f = sb("m8", [P, 8]), sb("i8f", [P, 8])
        i8 = sb("i8", [P, 8], U32)
        nm1, s1, r1 = sb("nm1", [P, 1]), sb("s1", [P, 1]), sb("r1", [P, 1])
        combT = sb("combT", [NE1, P])
        acc1 = k_f

        bank = [es.enter_context(nc.psum_tensor(f"bank{i}", [P, 512], F32)) for i in range(8)]

        ld_x, ld_mask, ld_mask8, ld_wts, ld_small, ld_late = (
            sem(n) for n in ("ld_x", "ld_mask", "ld_mask8", "ld_wts", "ld_small", "ld_late"))
        ctx_in = [sem("ctx_in0"), sem("ctx_in1")]
        kpad_in = sem("kpad_in")
        w_in, s_in = [sem("w_in0"), sem("w_in1")], [sem("s_in0"), sem("s_in1")]
        out_done = sem("out_done")
        consts, dve, setup_done, tanh_done = sem("consts"), sem("dve"), sem("setup_done"), sem("tanh_done")
        vef_ready, rstd_ready, xn_ready, qk_mm, v_mm = (
            sem(n) for n in ("vef_ready", "rstd_ready", "xn_ready", "qk_mm", "v_mm"))
        kf_ready, qk_split, v_ready, q_mm, k_mm, q_stacked, k_stacked = (
            sem(n) for n in ("kf_ready", "qk_split", "v_ready", "q_mm", "k_mm", "q_stacked", "k_stacked"))
        p1_done, p1_read, negmax_ready, max_T, max_copied, max_mm, q_max_ready = (
            sem(n) for n in ("p1_done", "p1_read", "negmax_ready", "max_T", "max_copied", "max_mm", "q_max_ready"))
        p2_done, exp_done, av_done, o_read, o_T, otok_ready, o_back, x1_ready = (
            sem(n) for n in ("p2_done", "exp_done", "av_done", "o_read", "o_T", "otok_ready", "o_back", "x1_ready"))
        ve2_ready, rstd2_ready, xn2_ready, xn2_T, xT_ready, sq_done = (
            sem(n) for n in ("ve2_ready", "rstd2_ready", "xn2_ready", "xn2_T", "xT_ready", "sq_done"))
        simsq_ready, simsum_mm, simsum_ready, simr_ready, sg_exp = (
            sem(n) for n in ("simsq_ready", "simsum_mm", "simsum_ready", "simr_ready", "sg_exp"))
        routed, nsq_ready, rnorm_ready, gated_ready, exp_w, lg_read = (
            sem(n) for n in ("routed", "nsq_ready", "rnorm_ready", "gated_ready", "exp_w", "lg_read"))
        whi_ready, wlo_ready, shi_ready, slo_ready, moe_mm, moe_read = (
            sem(n) for n in ("whi_ready", "wlo_ready", "shi_ready", "slo_ready", "moe_mm", "moe_read"))
        qk_T, qkT_ready, scored, scr_ready, pat_exp, pat_ready, pat_T, patT_ready, ao_mm, ao_ready = (
            sem(n) for n in ("qk_T", "qkT_ready", "scored", "scr_ready", "pat_exp", "pat_ready", "pat_T",
                             "patT_ready", "ao_mm", "ao_ready"))
        oproj_mm, oproj_read, ve3_ready, rstd3_ready, kn_ready, kn_T, kT_ready = (
            sem(n) for n in ("oproj_mm", "oproj_read", "ve3_ready", "rstd3_ready", "kn_ready", "kn_T", "kT_ready"))
        arg1_ready, e1_ready, arg2_ready, e2_ready, ev_ready, e2v_ready, y_ready, y_T, x3_ready = (
            sem(n) for n in ("arg1_ready", "e1_ready", "arg2_ready", "e2_ready", "ev_ready", "e2v_ready", "y_ready",
                             "y_T", "x3_ready"))
        ve4_ready, rstd4_ready, xn4_ready, xn4_T, x4_split, lg4_mm, nm4_ready, ex4_ready, comb_ready = (
            sem(n) for n in ("ve4_ready", "rstd4_ready", "xn4_ready", "xn4_T", "x4_split", "lg4_mm", "nm4_ready",
                             "ex4_ready", "comb_ready"))
        comb_T, combT_ready, bias_mm, acc4_ready, l1_mm, l1_read, xout_ready, wkv_used = (
            sem(n) for n in ("comb_T", "combT_ready", "bias_mm", "acc4_ready", "l1_mm", "l1_read", "xout_ready",
                             "wkv_used"))

        block = es.enter_context(nc.Block())

        def valid(*batches):
            return tuple(b if 0 <= b < NB else None for b in batches)

        ATTENTION = [valid(i + 2, i + 1, i, i - 1) for i in range(-2, NB + 1)]
        TAIL = [valid(i, i - 1, i - 2, i - 3) for i in range(NB + 3)]

        ST_PARITY = {}
        for prep, peak, _, _ in ATTENTION:
            for use in ([(prep, u) for u in range(1, 5)] if prep is not None else []) + (
                    [(peak + 1, u) for u in (5, 6)] if peak is not None else []) + (
                    [(prep, 0)] if prep is not None else []):
                ST_PARITY[use] = len(ST_PARITY) % 2

        def st_bank(b, use):
            return bank[6 + ST_PARITY[(b, use)]][:]

        def side_part(n):
            if n % 2 == 0:
                k = n // 2
                return (o_hi[:, 2 * k:2 * k + 2, :], o_lo[:, 2 * k:2 * k + 2, :],
                        wo[2 * k:2 * k + 2].rearrange("e h c -> h e c"))
            c, k = divmod(n // 2, NE1 // 2)
            return (w1_hi[:, c, 2 * k:2 * k + 2, :], w1_lo[:, c, 2 * k:2 * k + 2, :],
                    w1T[2 * k:2 * k + 2, c * P:(c + 1) * P, :].rearrange("e h o -> h e o"))

        def pairs(tile):
            return tile.rearrange("p (e c) -> p e c", e=2)

        @block.sync
        def _(sp):
            def load_side(n):
                sp.dma_start(pairs(s_raw[n % 2][:]), side_part(n)[2]).then_inc(s_in[n % 2], 16)

            def load_expert(e):
                sp.dma_start(w_raw[e % 2][:], wqkv[e].rearrange("(c p) n -> p c n", p=P)).then_inc(w_in[e % 2], 16)

            sp.dma_start(x_sb[:], x.rearrange("b p t -> p b t")).then_inc(ld_x, 16)
            sp.dma_start(ctx_b[0][:], ctx[0]).then_inc(ctx_in[0], 16)
            for dst, src in ((wqT_sb, wqT), (wkT_sb, wkT), (wvT_sb, wvT)):
                sp.dma_start(dst[:], src).then_inc(ld_wts, 16)
            for dst, src in ((bq_sb, bq), (bk_sb, bk), (bv_sb, bv)):
                sp.dma_start(dst[:], src).then_inc(ld_wts, 16)
            sp.wait_ge(consts, 1)
            for s in range(4):
                sp.dma_start(mask8[32 * s:32 * s + NB, :], mask).then_inc(ld_mask8, 16)
            sp.dma_start(mask_bc[:], mask.partition_broadcast(P)).then_inc(ld_mask, 16)
            sp.dma_start(mask_col[:], maskT.rearrange("(c p) b -> p c b", p=P)).then_inc(ld_mask, 16)
            for dst, src in ((gx_sb[:], g_xattn.partition_broadcast(P)), (gf_sb[:], g_ffn.partition_broadcast(P)),
                             (gates_sb[:], gates.partition_broadcast(P)),
                             (sim_sb[:], sim.rearrange("(c p) e -> p c e", p=P))):
                sp.dma_start(dst, src).then_inc(ld_small, 16)
            sp.dma_start(ctx_b[1][:], ctx[1]).then_inc(ctx_in[1], 16)
            for dst, src in ((wg_sb[:], wg.rearrange("(c p) e -> p c e", p=P)), (b1_sb[:], b1),
                             (w_sb[:], wkv_w),
                             (u_sb[:], wkv_u),
                             (ctxT_sb[:], ctxT.rearrange("(c p) b t -> p c b t", p=P))):
                sp.dma_start(dst, src).then_inc(ld_late, 16)
            for n in range(2):
                load_expert(n)
                load_side(n)
            for prep, _, _, _ in ATTENTION:
                if prep is None:
                    continue
                sp.wait_ge(k_stacked, 2 * (prep + 1))
                if prep >= 2:
                    sp.wait_ge(p2_done, NH * (prep - 1))
                else:
                    sp.wait_ge(setup_done, 1)
                for j in range(4):
                    sp.dma_start(k_pad[prep % 2][32 * j:32 * j + 32, j, :, :].bitcast(F32),
                                 k_stack[32 * j:32 * j + 32, :, :].bitcast(F32)).then_inc(kpad_in, 16)
                if prep + 2 < NB:
                    sp.wait_ge(v_mm, prep + 1)
                    sp.dma_start(ctx_b[prep % 2][:], ctx[prep + 2]).then_inc(ctx_in[prep % 2], 16)
            for e in range(2, NE):
                sp.wait_ge(whi_ready, e - 1)
                sp.wait_ge(wlo_ready, e - 1)
                load_expert(e)
                sp.wait_ge(shi_ready, e - 1)
                sp.wait_ge(slo_ready, e - 1)
                load_side(e)
            for b in range(NB):
                sp.wait_ge(xout_ready, b + 1)
                sp.dma_start(out[b], x_sb[:, b, :]).then_inc(out_done, 16)
            sp.wait_ge(out_done, 16 * NB)

        @block.gpsimd
        def _(eng):
            g = nc.gpsimd
            made = Tally(consts)
            made.step(g.memset(mask8[:], 0.0))
            made.step(g.memset(ones[:], 1.0))
            made.step(g.memset(zeros[:], 0.0))
            made.step(g.memset(minus_half[:], -0.5))
            eng.wait_ge(consts, made.n)
            made.step(g.affine_select(out=ident[:], in_=ones[:], compare_op=ALU.is_equal, fill=0.0, base=0,
                                      pattern=[[-1, P]], channel_multiplier=1))
            made.step(g.affine_select(out=causal[:], in_=ones[:], compare_op=ALU.is_ge, fill=0.0, base=0,
                                      pattern=[[-1, P]], channel_multiplier=1))
            made.step(g.affine_select(out=causal_neg[:], in_=zeros[:], compare_op=ALU.is_ge, fill=-NEG_CAUSAL,
                                      base=0, pattern=[[-1, P]], channel_multiplier=1))
            made.step(g.iota(iota_e[:], pattern=[[1, NE]], base=0, channel_multiplier=0,
                             allow_small_or_imprecise_dtypes=True))
            for i in range(2):
                made.step(g.memset(v_pad[i][:], 0.0))
            eng.wait_ge(consts, made.n)
            for i in range(2):
                by_pair = v_pad[i][:].rearrange("p c (g i) n -> p (c g) i n", i=2)
                for k in range(2):
                    made.step(g.memset(by_pair[:, :, k, 16 + k:17 + k], 1.0))
            for i in range(2):
                made.step(g.memset(k_pad[i][:].bitcast(F32), 0.0))
            eng.wait_ge(vef_ready, 1)
            g.tensor_tensor(rstd[:], var_eps[:], minus_half[:, 0:NB], ALU.pow).then_inc(rstd_ready, 1)
            eng.wait_ge(simsum_ready, 1)
            g.tensor_tensor(sim_r[:], sim_sq[:, 0, :], minus_half[:], ALU.pow).then_inc(simr_ready, 1)

            def expert_lo(e):
                eng.wait_ge(w_in[e % 2], 16 * (e // 2 + 1))
                eng.wait_ge(whi_ready, e + 1)
                if e >= 2:
                    eng.wait_ge(moe_mm, NB * (e - 1))
                g.tensor_tensor(w_lo[e % 2][:], w_raw[e % 2][:], w_hi[e % 2][:].bitcast(F32),
                                ALU.subtract).then_inc(wlo_ready, 1)

            def side_lo(n):
                eng.wait_ge(s_in[n % 2], 16 * (n // 2 + 1))
                eng.wait_ge(shi_ready, n + 1)
                hi, lo, _ = side_part(n)
                g.tensor_tensor(lo, pairs(s_raw[n % 2][:]), hi.bitcast(F32), ALU.subtract).then_inc(slo_ready, 1)

            for prep, peak, main, fin in ATTENTION:
                if fin is not None:
                    eng.wait_ge(ve2_ready, fin + 1)
                    g.tensor_tensor(rstdf[:], vef[:], minus_half[:, 0:1], ALU.pow).then_inc(rstd2_ready, 1)
                if main in (1, 2):
                    expert_lo(main - 1)
            eng.wait_ge(nsq_ready, 1)
            g.tensor_tensor(rnorm[:], nsq[:], minus_half[:, 0:NB], ALU.pow).then_inc(rnorm_ready, 1)
            for e in range(NE):
                if e >= 2:
                    expert_lo(e)
                side_lo(e)
            for _, proj, wkv, last in TAIL:
                if wkv is not None:
                    eng.wait_ge(e2_ready, wkv + 1)
                    g.tensor_tensor(e2v[:].rearrange("p (c t) -> p c t", c=CC),
                                    e2[:, 1, :].rearrange("p (c t) -> p c t", c=CC), ctxT_sb[:, :, wkv, :],
                                    ALU.mult).then_inc(e2v_ready, 1)
                    eng.wait_ge(e1_ready, wkv + 1)
                    g.tensor_tensor(ev[:].rearrange("p (c t) -> p c t", c=CC),
                                    e1[:, 1, :].rearrange("p (c t) -> p c t", c=CC), ctxT_sb[:, :, wkv, :],
                                    ALU.mult).then_inc(ev_ready, 1)
                if proj is not None:
                    eng.wait_ge(ve3_ready, proj + 1)
                    g.tensor_tensor(rstd[:, 0:1], var_eps[:, 0:1], minus_half[:, 0:1], ALU.pow).then_inc(rstd3_ready, 1)
                if wkv is not None:
                    eng.wait_ge(ve4_ready, wkv + 1)
                    g.tensor_tensor(rstd[:, 1:2], var_eps[:, 1:2], minus_half[:, 0:1], ALU.pow).then_inc(rstd4_ready, 1)

        @block.scalar
        def _(act):
            a = nc.scalar
            act.wait_ge(ld_small, 64)
            a.activation(tgx[:], gx_sb[:], ACT.Tanh).then_inc(tanh_done, 1)
            a.activation(tgf[:], gf_sb[:], ACT.Tanh).then_inc(tanh_done, 1)
            a.activation(sgate[:], gates_sb[:], ACT.Exp, scale=-1.0).then_inc(sg_exp, 1)

            def expert_hi(e):
                act.wait_ge(w_in[e % 2], 16 * (e // 2 + 1))
                if e >= 2:
                    act.wait_ge(moe_mm, NB * (e - 1))
                a.activation(w_hi[e % 2][:], w_raw[e % 2][:], ACT.Copy).then_inc(whi_ready, 1)

            def side_hi(n):
                act.wait_ge(s_in[n % 2], 16 * (n // 2 + 1))
                a.activation(side_part(n)[0], pairs(s_raw[n % 2][:]), ACT.Copy).then_inc(shi_ready, 1)

            def exponentials(b, quad):
                if 4 * b + quad >= 2:
                    act.wait_ge(av_done, 4 * b + quad - 1)
                for j in range(4):
                    n = NH * b + 4 * quad + j
                    act.wait_ge(p2_done, n + 1)
                    a.activation(probs[:, n % 8, :, :], bank[2 + n % 2][:].rearrange("p (c t) -> p c t", c=CC),
                                 ACT.Exp).then_inc(exp_done, 1)

            def stack_copies(b, which):
                done, stacked = (q_mm, q_stacked) if which == 0 else (k_mm, k_stacked)
                dst = q_stack[b % 2] if which == 0 else k_stack
                if which == 0 and b >= 2:
                    act.wait_ge(q_max_ready, 2 * (b - 1))
                if which == 1 and b >= 1:
                    act.wait_ge(kpad_in, 64 * b)
                for half in range(2):
                    act.wait_ge(done, 2 * b + half + 1)
                    a.activation(dst[:, 2 * half:2 * half + 2, :],
                                 st_bank(b, 1 + 2 * which + half).rearrange("p (q t) -> p q t", q=2),
                                 ACT.Copy).then_inc(stacked, 1)

            for prep, peak, main, fin in ATTENTION:
                if fin is not None:
                    act.wait_ge(av_done, 4 * (fin + 1))
                    if fin >= 1:
                        act.wait_ge(o_T, fin)
                    a.activation(o_raw[:], bank[4][:].rearrange("p (f t) -> p f t", f=2), ACT.Copy).then_inc(o_read, 1)
                for quad in range(QUADS):
                    if main is not None:
                        exponentials(main, quad)
                    if prep is not None and quad in (1, 2):
                        stack_copies(prep, quad - 1)
                if fin is not None:
                    act.wait_ge(xn2_ready, fin + 1)
                    a.activation(sq_junk[:], xn_f[:], ACT.Square, accum_out=nsq[:, fin:fin + 1]).then_inc(sq_done, 1)
                if peak is not None:
                    act.wait_ge(max_T, peak + 1)
                    if peak >= 1:
                        act.wait_ge(max_mm, 2 * peak)
                    a.activation(max_rows[:], bank[5][0:2 * NH, 0:T], ACT.Copy).then_inc(max_copied, 1)
                if main in (0, 1):
                    expert_hi(main)
            act.wait_ge(gated_ready, 1)
            a.activation(w_e[:], gated[:], ACT.Exp).then_inc(exp_w, 1)
            for e in range(NE):
                if e >= 2:
                    expert_hi(e)
                side_hi(e)

            for att, proj, wkv, last in TAIL:
                if wkv is not None:
                    act.wait_ge(kn_T, wkv + 1)
                    if wkv >= 1:
                        act.wait_ge(wkv_used, wkv)
                    a.activation(kT[:], bank[6][:, 0:T].rearrange("p (c t) -> p c t", c=CC), ACT.Copy).then_inc(kT_ready, 1)
                if att is not None:
                    act.wait_ge(qk_T, att + 1)
                    if att >= 1:
                        act.wait_ge(scored, att)
                    a.activation(qkT[:], bank[4][:, 0:2 * P].rearrange("p (c t) -> p c t", c=2),
                                 ACT.Copy).then_inc(qkT_ready, 1)
                if wkv is not None:
                    act.wait_ge(arg2_ready, wkv + 1)
                    a.activation(e2[:], arg2[:], ACT.Exp).then_inc(e2_ready, 1)
                    act.wait_ge(arg1_ready, wkv + 1)
                    a.activation(e1[:], arg1[:], ACT.Exp).then_inc(e1_ready, 1)
                if last is not None:
                    act.wait_ge(nm4_ready, last + 1)
                    a.activation(ex1[:], lg1[:], ACT.Exp, bias=nm1[:], accum_out=s1[:]).then_inc(ex4_ready, 1)
                if att is not None:
                    act.wait_ge(scr_ready, att + 1)
                    a.activation(pat[:], scr[:], ACT.Exp, bias=row_nm[:], accum_out=row_s[:]).then_inc(pat_exp, 1)
                    act.wait_ge(pat_T, att + 1)
                    if att >= 1:
                        act.wait_ge(ao_mm, att)
                    a.activation(patT[:], bank[5][:, 0:P], ACT.Copy).then_inc(patT_ready, 1)
                if last is not None:
                    act.wait_ge(comb_T, last + 1)
                    if last >= 1:
                        act.wait_ge(bias_mm, last)
                    a.activation(combT[:], bank[7][0:NE1, 0:P], ACT.Copy).then_inc(combT_ready, 1)

        @block.vector
        def _(eng):
            v = nc.vector
            d = Tally(dve)

            def then(instruction):
                eng.wait_ge(dve, d.step(instruction))

            eng.wait_ge(ld_x, 16)
            for b in range(NB):
                n = d.step(v.bn_stats(bn6[:, b, :], x_sb[:, b, :]))
            eng.wait_ge(dve, n)
            for b in range(NB):
                n = d.step(v.bn_aggr(mv[:, b, :], bn6[:, b, :]))
            eng.wait_ge(dve, n)
            v.tensor_scalar(var_eps[:], mv[:, :, 1], EPS, None, ALU.add).then_inc(vef_ready, 1)

            for t in (sel_q_hi, sel_q_lo, sel_k_hi, sel_k_lo, sel_max):
                n = d.step(v.memset(t[:].bitcast(F32), 0.0))
            for t in (row_q, row_k):
                n = d.step(v.memset(t[:], 0.0))
            eng.wait_ge(dve, n)
            eng.wait_ge(consts, 8)
            for t, parts in ((sel_q_hi, (0, 1)), (sel_q_lo, (2,)), (sel_k_hi, (0, 2)), (sel_k_lo, (1,))):
                for quad in range(QUADS):
                    half, odd = divmod(quad, 2)
                    src = ident[:, 64 * half:64 * half + 64].rearrange("p (j n) -> p j n", n=16)[
                        :, :, HD * odd:HD * (odd + 1)]
                    dst = t[:, quad, :].rearrange("p (j n) -> p j n", j=4)
                    for part in parts:
                        n = d.step(v.tensor_copy(dst[:, :, HD * part:HD * (part + 1)], src))
            for quad in range(QUADS):
                for part in range(2):
                    h0 = NH * part + head_of(quad, 0)
                    n = d.step(v.tensor_copy(sel_max[:, quad, 29 + part::32], ident[0:2 * NH, h0:h0 + 7:2]))
            by_head_q = row_q[:].rearrange("p (j n) -> p j n", j=4)
            by_head_k = row_k[:].rearrange("p (j n) -> p j n", j=4)
            for s, row, end in ((0, 24, 26), (1, 26, 27), (2, 27, 28), (3, 28, 29)):
                n = d.step(v.memset(by_head_q[32 * s:32 * s + 32, :, row:end], 1.0))
            for s, row, end in ((0, 24, 25), (0, 26, 27), (1, 25, 26), (2, 27, 31)):
                n = d.step(v.memset(by_head_k[32 * s:32 * s + 32, :, row:end], 1.0))
            for s in range(4):
                n = d.step(v.tensor_copy(batch_row[32 * s:32 * s + 32, :], ident[32 * s:32 * s + 32, 32 * s:32 * s + NB]))
            eng.wait_ge(ld_mask8, 64)
            n = d.step(v.tensor_scalar(aux_f[0:64, 0, :], mask8[0:64, :], -NEG_MASK, None, ALU.mult))
            n = d.step(v.tensor_scalar(aux_f[64:128, 0, :], mask8[64:128, :], 1.0, NEG_MASK, ALU.subtract, ALU.mult))
            n = d.step(v.tensor_scalar(aux_f[:, 1, :], mask8[:], -1.0, 1.0, ALU.mult, ALU.add))
            eng.wait_ge(dve, n)
            for dst, k in ((aux_q, 0), (aux_k, 1)):
                n = d.step(v.tensor_copy(dst[:], aux_f[:, k, :]))
            eng.wait_ge(dve, n)
            for p0, dst, k in ((32, aux_q, 0), (96, aux_q, 0), (32, aux_k, 1)):
                n = d.step(v.tensor_tensor(dst[p0:p0 + 32, :], aux_f[p0:p0 + 32, k, :],
                                           dst[p0:p0 + 32, :].bitcast(F32), ALU.subtract))
            n = d.step(v.tensor_scalar(aux_k[64:96, :], aux_f[64:96, 1, :], 0.0, 1.0, ALU.mult, ALU.add))
            n = d.step(v.tensor_scalar(aux_k[96:128, :], aux_f[96:128, 1, :], 0.0, None, ALU.mult))
            for dst, rows in ((sel_aux_q, row_q), (sel_aux_k, row_k)):
                n = d.step(v.tensor_tensor(dst[:], batch_row[:].unsqueeze(2).to_broadcast([P, NB, P]),
                                           rows[:].unsqueeze(1).to_broadcast([P, NB, P]), ALU.mult))
            eng.wait_ge(ld_mask, 32)
            eng.wait_ge(ld_wts, 96)
            n = d.step(v.tensor_scalar(wqT_sb[:], wqT_sb[:], XATTN_SCALE, None, ALU.mult))
            n = d.step(v.tensor_scalar(bq_sb[:], bq_sb[:], XATTN_SCALE, None, ALU.mult))
            eng.wait_ge(dve, n)
            eng.wait_ge(consts, 16)
            v.memset(pq[:, :, 0:1], 0.0).then_inc(setup_done, 1)

            def prepare(b):
                if b == 0:
                    eng.wait_ge(rstd_ready, 1)
                else:
                    eng.wait_ge(qk_mm, b)
                v.tensor_scalar(xn[:], x_sb[:, b, :], mv[:, b, 0:1], rstd[:, b:b + 1], ALU.subtract,
                                ALU.mult).then_inc(xn_ready, 1)

            def project(b):
                eng.wait_ge(ld_wts, 96)
                eng.wait_ge(qk_mm, b + 1)
                v.scalar_tensor_tensor(q_f[:], bank[5][:, 0:T], bq_sb[:], mask_bc[:, b, :], ALU.add,
                                       ALU.mult).then_inc(dve, 1)
                d.n += 1
                nq = d.n
                v.scalar_tensor_tensor(k_f[:], bank[5][:, T:2 * T], bk_sb[:], mask_bc[:, b, :], ALU.add,
                                       ALU.mult).then_inc(kf_ready, 1)
                if b >= 1:
                    eng.wait_ge(k_mm, 2 * b)
                eng.wait_ge(dve, nq)
                nq = d.step(v.tensor_copy(q_hi[:], q_f[:]))
                eng.wait_ge(kf_ready, b + 1)
                nk = d.step(v.tensor_copy(k_hi[:], k_f[:]))
                eng.wait_ge(dve, nq)
                d.step(v.tensor_tensor(q_lo[:], q_f[:], q_hi[:].bitcast(F32), ALU.subtract))
                eng.wait_ge(dve, nk)
                v.tensor_tensor(k_lo[:], k_f[:], k_hi[:].bitcast(F32), ALU.subtract).then_inc(qk_split, 1)

            def spread_values(b):
                eng.wait_ge(v_mm, b + 1)
                if b >= 2:
                    eng.wait_ge(av_done, 4 * (b - 1))
                vp = v_pad[b % 2][:].rearrange("p c (g i) n -> p c g i n", i=2)
                src = st_bank(b, 0)[:, 0:CC * P].rearrange("p (c g i n) -> p c g i n", c=CC, i=2, n=HD)
                for c in range(CC):
                    for i in range(2):
                        v.tensor_scalar(vp[:, c, :, i, HD * i:HD * (i + 1)], src[:, c, :, i, :],
                                        mask_col[:, c, b:b + 1], None, ALU.mult).then_inc(v_ready, 1)

            def maxima(b, quad):
                for j in range(4):
                    n = NH * b + 4 * quad + j
                    h = head_of(quad, j)
                    eng.wait_ge(p1_done, n + 1)
                    v.tensor_reduce(mx[:, :, h], bank[n % 2][:].rearrange("p (c s) -> p c s", c=CC), axis=AX.X,
                                    op=ALU.max).then_inc(p1_read, 1)

            def negate_maxima(b):
                eng.wait_ge(p1_read, NH * (b + 1))
                if b >= 1:
                    eng.wait_ge(max_T, b)
                then(v.tensor_scalar(neg_max[:, :, 0, :], mx[:], -1.0, None, ALU.mult))
                v.scalar_tensor_tensor(neg_max[:, :, 1, :], mx[:], -1.0, neg_max[:, :, 0, :].bitcast(F32), ALU.mult,
                                       ALU.subtract).then_inc(negmax_ready, 1)

            def add_maxima(b):
                if b >= 1:
                    eng.wait_ge(p2_done, NH * b)
                eng.wait_ge(q_stacked, 2 * (b + 1))
                for half in range(2):
                    eng.wait_ge(max_mm, 2 * b + half + 1)
                    s = slice(2 * half, 2 * half + 2)
                    v.tensor_tensor(q_stack_max[:, s, :],
                                    st_bank(b + 1, 5 + half).rearrange("p (q t) -> p q t", q=2),
                                    q_stack[b % 2][:, s, :].bitcast(F32), ALU.add).then_inc(q_max_ready, 1)

            def normalise_heads(b):
                eng.wait_ge(o_T, b + 1)
                cols = bank[5][:].rearrange("p (g n) -> p g n", n=32)
                then(v.reciprocal(o_den[:].rearrange("p c (g i) -> p (c g) i", i=2), cols[:, :, 16:18]))
                then(v.tensor_tensor(o_den[:], o_den[:], mask_col[:, :, b:b + 1].to_broadcast([P, CC, NH]), ALU.mult))
                if b >= 1:
                    eng.wait_ge(o_back, b)
                v.tensor_tensor(o_tok[:].rearrange("p c (g i n) -> p (c g) i n", i=2, n=HD),
                                cols[:, :, 0:16].rearrange("p g (i n) -> p g i n", i=2),
                                o_den[:].rearrange("p c (g i) -> p (c g) i", i=2).unsqueeze(3).to_broadcast(
                                    [P, CC * NH // 2, 2, HD]), ALU.mult).then_inc(otok_ready, 1)

            def add_attention(b):
                eng.wait_ge(tanh_done, 2)
                eng.wait_ge(o_back, b + 1)
                v.scalar_tensor_tensor(x_sb[:, b, :], bank[5][:, 0:T], tgx[:, 0:1], x_sb[:, b, :], ALU.mult,
                                       ALU.add).then_inc(x1_ready, 1)
                eng.wait_ge(x1_ready, b + 1)
                then(v.bn_stats(bn6f[:], x_sb[:, b, :]))
                then(v.bn_aggr(mvf[:], bn6f[:]))
                if b >= 1:
                    eng.wait_ge(rstd2_ready, b)
                v.tensor_scalar(vef[:], mvf[:, 1:2], EPS, None, ALU.add).then_inc(ve2_ready, 1)

            def normalise_second(b):
                eng.wait_ge(rstd2_ready, b + 1)
                if b >= 1:
                    eng.wait_ge(xn2_T, b)
                    eng.wait_ge(sq_done, b)
                v.tensor_scalar(xn_f[:], x_sb[:, b, :], mvf[:, 0:1], rstdf[:], ALU.subtract,
                                ALU.mult).then_inc(xn2_ready, 1)

            def split_second(b):
                eng.wait_ge(xn2_T, b + 1)
                src = bank[5][:, 0:T].rearrange("p (c n) -> p c n", c=CC)
                then(v.tensor_copy(xT_hi[:, b, :, :], src))
                v.tensor_tensor(xT_lo[:, b, :, :], src, xT_hi[:, b, :, :].bitcast(F32),
                                ALU.subtract).then_inc(xT_ready, 1)

            def other_constants():
                eng.wait_ge(ld_small, 64)
                v.tensor_tensor(sim_sq[:], sim_sb[:], sim_sb[:], ALU.mult).then_inc(simsq_ready, 1)
                eng.wait_ge(sg_exp, 1)
                then(v.tensor_scalar(sgate[:], sgate[:], 1.0, None, ALU.add))
                then(v.reciprocal(sgate[:], sgate[:]))
                eng.wait_ge(ld_late, 80)
                for c in range(CC):
                    d.step(v.tensor_scalar(w_full[:, c, :], ones[:], w_sb[:, c:c + 1], None, ALU.mult))
                    d.step(v.tensor_scalar(u_full[:, c, :], ones[:], u_sb[:, c:c + 1], None, ALU.mult))
                d.step(v.memset(o_ext[:, :, 0:1], NEG_START))
                then(v.tensor_copy(wg_hi[:], wg_sb[:]))
                then(v.tensor_tensor(wg_lo[:], wg_sb[:], wg_hi[:].bitcast(F32), ALU.subtract))

            def router_sums():
                eng.wait_ge(simsum_mm, 1)
                v.tensor_scalar(sim_sq[:, 0, :], bank[5][:, 0:NE], 1e-24, None, ALU.max).then_inc(simsum_ready, 1)

            def router_columns():
                eng.wait_ge(simr_ready, 1)
                then(v.tensor_tensor(simn[:], sim_sb[:], sim_r[:].unsqueeze(1).to_broadcast([P, CC, NE]), ALU.mult))
                then(v.tensor_copy(sim_hi[:], simn[:]))
                v.tensor_tensor(sim_lo[:], simn[:], sim_hi[:].bitcast(F32), ALU.subtract).then_inc(simsum_ready, 1)

            for prep, peak, main, fin in ATTENTION:
                if prep is not None:
                    prepare(prep)
                for quad in range(QUADS):
                    if peak is not None:
                        maxima(peak, quad)
                    if quad == 0 and prep is not None:
                        project(prep)
                    if fin is not None:
                        if quad < 3:
                            (normalise_heads, add_attention, normalise_second)[quad](fin)
                if peak is not None:
                    negate_maxima(peak)
                if fin is not None:
                    split_second(fin)
                if peak is not None:
                    add_maxima(peak)
                if prep is not None:
                    spread_values(prep)
                if main == 0:
                    other_constants()
                    router_sums()
                if main == 1:
                    router_columns()

            eng.wait_ge(sq_done, NB)
            v.tensor_scalar(nsq[:], nsq[:], 1e-24, None, ALU.max).then_inc(nsq_ready, 1)
            eng.wait_ge(rnorm_ready, 1)
            eng.wait_ge(routed, 1)
            v.tensor_tensor(lg[:], bank[5][:, 0:NB * NE].rearrange("p (b e) -> p b e", b=NB),
                            rnorm[:].unsqueeze(2).to_broadcast([P, NB, NE]), ALU.mult).then_inc(lg_read, 1)
            eng.wait_ge(lg_read, 1)
            then(v.tensor_tensor(lg[:], lg[:], sgate[:].unsqueeze(1).to_broadcast([P, NB, NE]), ALU.subtract))
            for b in range(NB):
                n = d.step(v.max(top8[:, b, :], lg[:, b, :]))
            eng.wait_ge(dve, n)
            for b in range(NB):
                n = d.step(v.max_index(topi[:, b, :], top8[:, b, :], lg[:, b, :]))
            then(v.tensor_scalar(gmax[:], top8[:, :, 0], 0.0, None, ALU.max))
            then(v.tensor_scalar(gated[:], lg[:], 0.0, None, ALU.max))
            v.tensor_tensor(gated[:], gated[:], gmax[:].unsqueeze(2).to_broadcast([P, NB, NE]),
                            ALU.subtract).then_inc(gated_ready, 1)
            then(v.tensor_copy(topi_f[:], topi[:]))
            iota_b = iota_e[:].unsqueeze(1).to_broadcast([P, NB, NE])
            then(v.tensor_tensor(fb[:], iota_b, topi_f[:, :, 0:1].to_broadcast([P, NB, NE]), ALU.is_equal))
            then(v.tensor_tensor(pos[:], iota_b, topi_f[:, :, 1:2].to_broadcast([P, NB, NE]), ALU.is_equal))
            then(v.tensor_tensor(fb[:], fb[:], pos[:], ALU.add))
            then(v.tensor_scalar(inact[:], top8[:, :, 0], 0.0, None, ALU.is_le))
            then(v.tensor_tensor(fb[:], fb[:], inact[:].unsqueeze(2).to_broadcast([P, NB, NE]), ALU.mult))
            then(v.tensor_scalar(pos[:], lg[:], 0.0, None, ALU.is_gt))
            then(v.tensor_tensor(pos[:], pos[:], fb[:], ALU.add))
            eng.wait_ge(exp_w, 1)
            then(v.tensor_tensor(w_e[:], w_e[:], pos[:], ALU.mult))
            then(v.tensor_reduce(esum[:], w_e[:], axis=AX.X, op=ALU.add))
            then(v.reciprocal(ersum[:], esum[:]))
            then(v.tensor_tensor(w_e[:], w_e[:], ersum[:].unsqueeze(2).to_broadcast([P, NB, NE]), ALU.mult))
            then(v.tensor_scalar(w_et[:], w_e[:], tgf[:, 0:1], None, ALU.mult))

            for e in range(NE):
                for b in range(NB):
                    n = NB * e + b
                    eng.wait_ge(moe_mm, n + 1)
                    src = bank[n % 8][:, 0:QKV]
                    if e == 0:
                        v.tensor_scalar(qkv[:, b, :], src, w_e[:, b, e:e + 1], None, ALU.mult).then_inc(moe_read, 1)
                    else:
                        eng.wait_ge(moe_read, n - NB + 1)
                        v.scalar_tensor_tensor(qkv[:, b, :], src, w_e[:, b, e:e + 1], qkv[:, b, :], ALU.mult,
                                               ALU.add).then_inc(moe_read, 1)

            def flat(tile):
                return tile.rearrange("p (c t) -> p c t", c=CC)

            def output_experts(b, ks):
                for k in ks:
                    n = NE // 2 * b + k
                    eng.wait_ge(oproj_mm, n + 1)
                    src = bank[n % 2]
                    even, odd = w_et[:, b, 2 * k:2 * k + 1], w_et[:, b, 2 * k + 1:2 * k + 2]
                    if k:
                        eng.wait_ge(oproj_read, n)
                        eng.wait_ge(dve, d.n)
                    d.step(v.scalar_tensor_tensor(x_sb[:, b, :], src[:, 0:T], even, x_sb[:, b, :], ALU.mult, ALU.add))
                    if k == 0:
                        v.tensor_scalar(acc_odd[:], src[:, T:2 * T], odd, None, ALU.mult).then_inc(oproj_read, 1)
                    else:
                        v.scalar_tensor_tensor(acc_odd[:], src[:, T:2 * T], odd, acc_odd[:], ALU.mult,
                                               ALU.add).then_inc(oproj_read, 1)

            def statistics(b, col, ready):
                then(v.bn_stats(bn6f[:], x_sb[:, b, :]))
                then(v.bn_aggr(mv[:, col, :], bn6f[:]))
                v.tensor_scalar(var_eps[:, col:col + 1], mv[:, col, 1:2], EPS, None, ALU.add).then_inc(ready, 1)

            def experts_done(b):
                eng.wait_ge(oproj_read, NE // 2 * (b + 1))
                eng.wait_ge(dve, d.n)
                then(v.tensor_tensor(x_sb[:, b, :], x_sb[:, b, :], acc_odd[:], ALU.add))
                statistics(b, 0, ve3_ready)

            def keys(b):
                eng.wait_ge(rstd3_ready, b + 1)
                if b >= 1:
                    eng.wait_ge(kn_T, b)
                v.tensor_scalar(kn[:], x_sb[:, b, :], mv[:, 0, 0:1], rstd[:, 0:1], ALU.subtract,
                                ALU.mult).then_inc(kn_ready, 1)

            def wkv_exponents(b):
                o_prev, o_next = o_ext[:, :, 0:P], o_ext[:, :, 1:P + 1]
                eng.wait_ge(kT_ready, b + 1)
                for c in range(CC):
                    d.step(v.tensor_tensor_scan(o_ext[:, c, 1:P + 1], w_full[:, c, :], kT[:, c, :], NEG_START,
                                                op0=ALU.add, op1=ALU.max))
                d.step(v.tensor_tensor(uk[:], kT[:], u_full[:], ALU.add))
                eng.wait_ge(dve, d.n)
                n_ow = d.step(v.tensor_tensor(ow[:], o_prev, w_full[:], ALU.add))
                n_no = d.step(v.tensor_tensor(no[:], o_prev, uk[:], ALU.max))
                eng.wait_ge(dve, n_ow)
                d.step(v.tensor_tensor(flat(arg2[:, 0, :]), ow[:], o_next, ALU.subtract))
                if b >= 1:
                    eng.wait_ge(e2_ready, b)
                v.tensor_tensor(flat(arg2[:, 1, :]), kT[:], o_next, ALU.subtract).then_inc(arg2_ready, 1)
                eng.wait_ge(dve, d.n)
                d.step(v.tensor_tensor(flat(arg1[:, 0, :]), o_prev, no[:], ALU.subtract))
                v.tensor_tensor(flat(arg1[:, 1, :]), uk[:], no[:], ALU.subtract).then_inc(arg1_ready, 1)
                eng.wait_ge(arg2_ready, b + 1)

            def wkv_sums(b):
                eng.wait_ge(e2v_ready, b + 1)
                eng.wait_ge(e2_ready, b + 1)
                d.step(v.tensor_tensor_scan(pq[:, 0, 1:T + 1], e2[:, 0, :], e2v[:], 0.0, op0=ALU.mult, op1=ALU.add))
                then(v.tensor_tensor_scan(pq[:, 1, 1:T + 1], e2[:, 0, :], e2[:, 1, :], 0.0, op0=ALU.mult,
                                          op1=ALU.add))
                eng.wait_ge(e1_ready, b + 1)
                n_num = d.step(v.tensor_tensor(num[:], e1[:, 0, :], pq[:, 0, 0:T], ALU.mult))
                n_den = d.step(v.tensor_tensor(den[:], e1[:, 0, :], pq[:, 1, 0:T], ALU.mult))
                eng.wait_ge(dve, n_den)
                then(v.tensor_tensor(den[:], den[:], e1[:, 1, :], ALU.add))
                n_den = d.step(v.reciprocal(den[:], den[:]))
                eng.wait_ge(ev_ready, b + 1)
                n_num = d.step(v.tensor_tensor(num[:], num[:], ev[:], ALU.add))
                eng.wait_ge(dve, n_num)
                if b >= 1:
                    eng.wait_ge(y_T, b)
                v.tensor_tensor(yT[:], flat(num[:]), flat(den[:]), ALU.mult).then_inc(y_ready, 1)
                eng.wait_ge(y_ready, b + 1)
                v.memset(row_m[:, 0:1], 0.0).then_inc(wkv_used, 1)

            def add_wkv(b):
                eng.wait_ge(y_T, b + 1)
                v.scalar_tensor_tensor(x_sb[:, b, :], bank[6][:, 0:T], tgx[:, 1:2], x_sb[:, b, :], ALU.mult,
                                       ALU.add).then_inc(x3_ready, 1)
                eng.wait_ge(x3_ready, b + 1)
                statistics(b, 1, ve4_ready)

            def normalise_last(b):
                eng.wait_ge(rstd4_ready, b + 1)
                v.tensor_scalar(xn_1[:], x_sb[:, b, :], mv[:, 1, 0:1], rstd[:, 1:2], ALU.subtract,
                                ALU.mult).then_inc(xn4_ready, 1)

            def split_last(b):
                eng.wait_ge(xn4_T, b + 1)
                src = flat(bank[7][:, 0:T])
                if b >= 1:
                    eng.wait_ge(l1_mm, NE1 // 2 * b)
                then(v.tensor_copy(x1_hi[:], src))
                v.tensor_tensor(x1_lo[:], src, x1_hi[:].bitcast(F32), ALU.subtract).then_inc(x4_split, 1)

            def gate_last(b):
                eng.wait_ge(lg4_mm, b + 1)
                then(v.tensor_copy(lg1[:], bank[7][:, 0:NE1]))
                then(v.max(m8[:], lg1[:]))
                d.step(v.max_index(i8[:], m8[:], lg1[:]))
                v.tensor_scalar(nm1[:], m8[:, 0:1], -1.0, None, ALU.mult).then_inc(nm4_ready, 1)

            def combine_last(b):
                eng.wait_ge(dve, d.n)
                then(v.tensor_copy(i8f[:], i8[:]))
                then(v.tensor_scalar(comb[:], iota_e[:, 0:NE1], i8f[:, 0:1], None, ALU.is_equal))
                eng.wait_ge(ex4_ready, b + 1)
                then(v.reciprocal(r1[:], s1[:]))
                then(v.tensor_tensor(r1[:], r1[:], tgf[:, 1:2], ALU.mult))
                v.tensor_scalar(comb[:], comb[:], r1[:], None, ALU.mult).then_inc(comb_ready, 1)

            def last_experts(b):
                eng.wait_ge(comb_ready, b + 1)
                eng.wait_ge(bias_mm, b + 1)
                v.tensor_tensor(x_sb[:, b, :], bank[7][:, 0:T], x_sb[:, b, :], ALU.add).then_inc(acc4_ready, 1)
                eng.wait_ge(acc4_ready, b + 1)
                for k in range(NE1 // 2):
                    n = NE1 // 2 * b + k
                    eng.wait_ge(l1_mm, n + 1)
                    src = bank[2 + n % 2]
                    even, odd = comb[:, 2 * k:2 * k + 1], comb[:, 2 * k + 1:2 * k + 2]
                    if k:
                        eng.wait_ge(l1_read, n)
                        eng.wait_ge(dve, d.n)
                    d.step(v.scalar_tensor_tensor(x_sb[:, b, :], src[:, 0:T], even, x_sb[:, b, :], ALU.mult, ALU.add))
                    if k == 0:
                        v.tensor_scalar(acc1[:], src[:, T:2 * T], odd, None, ALU.mult).then_inc(l1_read, 1)
                    else:
                        v.scalar_tensor_tensor(acc1[:], src[:, T:2 * T], odd, acc1[:], ALU.mult,
                                               ALU.add).then_inc(l1_read, 1)
                eng.wait_ge(l1_read, NE1 // 2 * (b + 1))
                eng.wait_ge(dve, d.n)
                v.tensor_tensor(x_sb[:, b, :], x_sb[:, b, :], acc1[:], ALU.add).then_inc(xout_ready, 1)

            def mask_scores(b):
                eng.wait_ge(scored, b + 1)
                then(v.scalar_tensor_tensor(scr[:], bank[5][:, 0:P], FFN_SCALE, causal[:], ALU.mult, ALU.mult))
                then(v.tensor_tensor_reduce(out=scr[:], in0=scr[:], in1=causal_neg[:], scale=1.0, scalar=-3.0e38,
                                            op0=ALU.add, op1=ALU.max, accum_out=row_m[:]))
                v.tensor_scalar(row_nm[:], row_m[:], -1.0, None, ALU.mult).then_inc(scr_ready, 1)

            def normalise_rows(b):
                eng.wait_ge(pat_exp, b + 1)
                then(v.reciprocal(row_r[:], row_s[:]))
                v.tensor_scalar(pat[:], pat[:], row_r[:], None, ALU.mult).then_inc(pat_ready, 1)

            def split_attention(b):
                eng.wait_ge(ao_mm, b + 1)
                if b >= 1:
                    eng.wait_ge(oproj_mm, NE // 2 * b)
                then(v.tensor_copy(ao_hi[:], bank[4][:, 0:P]))
                v.tensor_tensor(ao_lo[:], bank[4][:, 0:P], ao_hi[:].bitcast(F32), ALU.subtract).then_inc(ao_ready, 1)

            for att, proj, wkv, last in TAIL:
                if last is not None:
                    split_last(last)
                if wkv is not None:
                    wkv_exponents(wkv)
                if proj is not None:
                    output_experts(proj, (0, 1))
                if last is not None:
                    gate_last(last)
                if att is not None:
                    mask_scores(att)
                if proj is not None:
                    output_experts(proj, (2, 3, 4))
                if att is not None:
                    normalise_rows(att)
                if last is not None:
                    combine_last(last)
                if wkv is not None:
                    wkv_sums(wkv)
                if proj is not None:
                    output_experts(proj, (5, 6, 7))
                    experts_done(proj)
                if att is not None:
                    split_attention(att)
                if last is not None:
                    last_experts(last)
                if proj is not None:
                    keys(proj)
                if wkv is not None:
                    add_wkv(wkv)
                    normalise_last(wkv)

        @block.tensor
        def _(pe):
            banks = [Bank(b) for b in bank]
            stack_uses = [0]

            def stack_bank(b, use, reader, value):
                assert ST_PARITY[(b, use)] == stack_uses[0] % 2
                stack_uses[0] += 1
                return banks[6 + ST_PARITY[(b, use)]].take(pe, reader, value)

            def mm(out_, lhsT, rhs, start, stop):
                return nc.tensor.matmul(out_, lhsT, rhs, start=start, stop=stop)

            def split_product(out_, terms):
                steps = [s for lh, ll, rh, rl in terms for s in ((lh, rh), (lh, rl), (ll, rh))]
                for n, (l, r) in enumerate(steps):
                    last = mm(out_, l, r, n == 0, n == len(steps) - 1)
                return last

            def project(b):
                pe.wait_ge(setup_done, 1)
                pe.wait_ge(xn_ready, b + 1)
                pe.wait_ge(ctx_in[b % 2], 16 * (b // 2 + 1))
                ps = banks[5].take(pe, kf_ready, b + 1)
                mm(ps[:, 0:T], wqT_sb[:], xn[:], True, True)
                mm(ps[:, T:2 * T], wkT_sb[:], ctx_b[b % 2][:], True, True).then_inc(qk_mm, 1)

            def project_values(b):
                ps = stack_bank(b, 0, v_ready, 2 * CC * (b + 1))
                for c in range(CC):
                    mm(ps[:, c * P:(c + 1) * P], ctx_b[b % 2][:, c * P:(c + 1) * P], wvT_sb[:], True, False)
                    last = mm(ps[:, c * P:(c + 1) * P], ones[0:1, :], bv_sb[:], False, True)
                last.then_inc(v_mm, 1)

            def stack(b, which):
                if b == 0:
                    pe.wait_ge(setup_done, 1)
                pe.wait_ge(qk_split, b + 1)
                hi, lo, s_hi, s_lo, aux, s_aux, done, stacked = (
                    (q_hi, q_lo, sel_q_hi, sel_q_lo, aux_q, sel_aux_q, q_mm, q_stacked) if which == 0 else
                    (k_hi, k_lo, sel_k_hi, sel_k_lo, aux_k, sel_aux_k, k_mm, k_stacked))
                for half in range(2):
                    ps = stack_bank(b, 1 + 2 * which + half, stacked, 2 * b + half + 1)
                    for n in range(2):
                        quad, cols = 2 * half + n, slice(n * T, (n + 1) * T)
                        mm(ps[:, cols], s_hi[:, quad, :], hi[:], True, False)
                        mm(ps[:, cols], s_lo[:, quad, :], lo[:], False, False)
                        last = mm(ps[:, cols], s_aux[:, b, :], aux[:], False, True)
                    last.then_inc(done, 1)

            def scores_for_maxima(b, quad):
                if quad == 0:
                    pe.wait_ge(q_stacked, 2 * (b + 1))
                    pe.wait_ge(kpad_in, 64 * (b + 1))
                for j in range(4):
                    n = NH * b + 4 * quad + j
                    ps = banks[n % 2].take(pe, p1_read, n + 1)
                    for c in range(CC):
                        last = mm(ps[:, c * T:(c + 1) * T], q_stack[b % 2][:, quad, c * P:(c + 1) * P],
                                  k_pad[b % 2][:, j, quad, :], True, True)
                    last.then_inc(p1_done, 1)

            def scores_transposed(b, quad):
                if quad == 0:
                    pe.wait_ge(q_max_ready, 2 * (b + 1))
                for j in range(4):
                    n = NH * b + 4 * quad + j
                    ps = banks[2 + n % 2].take(pe, exp_done, n + 1)
                    for c in range(CC):
                        last = mm(ps[:, c * T:(c + 1) * T], k_pad[b % 2][:, j, quad, c * P:(c + 1) * P],
                                  q_stack_max[:, quad, :], True, True)
                    last.then_inc(p2_done, 1)

            def values(b, quad):
                half, first = quad // 2, quad % 2 == 0
                if quad == 0:
                    pe.wait_ge(v_ready, 2 * CC * (b + 1))
                    banks[4].take(pe, o_read, b + 1)
                pe.wait_ge(exp_done, NH * b + 4 * quad + 4)
                for c in range(CC):
                    for j in range(4):
                        last = mm(bank[4][32 * j:32 * j + 32, half * T:(half + 1) * T],
                                  v_pad[b % 2][:, c, head_of(quad, j), :],
                                  probs[:, (4 * quad + j) % 8, c, :], first and c == 0, not first and c == CC - 1)
                last.then_inc(av_done, 1)

            def transpose_maxima(b):
                pe.wait_ge(negmax_ready, b + 1)
                ps = banks[5].take(pe, max_copied, b + 1)
                for c in range(CC):
                    last = nc.tensor.transpose(
                        ps[0:2 * NH, c * P:(c + 1) * P],
                        neg_max[:, c, :, :].rearrange("p k h -> p (k h)").bitcast(F32), ident[:])
                last.then_inc(max_T, 1)

            def maxima_rows(b):
                pe.wait_ge(max_copied, b + 1)
                for half in range(2):
                    ps = stack_bank(b + 1, 5 + half, q_max_ready, 2 * b + half + 1)
                    for n in range(2):
                        last = mm(ps[:, n * T:(n + 1) * T], sel_max[:, 2 * half + n, :], max_rows[:], True, True)
                    last.then_inc(max_mm, 1)

            def transpose_heads(b):
                pe.wait_ge(o_read, b + 1)
                ps = banks[5].take(pe, otok_ready, b + 1)
                for c in range(CC):
                    for f in range(2):
                        last = nc.tensor.transpose(ps[:, (2 * c + f) * P:(2 * c + f + 1) * P],
                                                   o_raw[:, f, c * P:(c + 1) * P], ident[:])
                last.then_inc(o_T, 1)

            def transpose_back(b):
                pe.wait_ge(otok_ready, b + 1)
                ps = banks[5].take(pe, x1_ready, b + 1)
                for c in range(CC):
                    last = nc.tensor.transpose(ps[:, c * P:(c + 1) * P], o_tok[:, c, :], ident[:])
                last.then_inc(o_back, 1)

            def transpose_second(b):
                pe.wait_ge(xn2_ready, b + 1)
                ps = banks[5].take(pe, xT_ready, b + 1)
                for c in range(CC):
                    last = nc.tensor.transpose(ps[:, c * P:(c + 1) * P], xn_f[:, c * P:(c + 1) * P], ident[:])
                last.then_inc(xn2_T, 1)

            for prep, peak, main, fin in ATTENTION:
                for quad in range(QUADS):
                    if peak is not None:
                        scores_for_maxima(peak, quad)
                    if main is not None:
                        scores_transposed(main, quad)
                        if quad:
                            values(main, quad - 1)
                    if prep is not None:
                        if quad == 0:
                            project(prep)
                        elif quad < 3:
                            stack(prep, quad - 1)
                    if fin is not None:
                        if quad == 0:
                            transpose_heads(fin)
                        elif quad == 1:
                            transpose_back(fin)
                        elif quad == 3:
                            transpose_second(fin)
                if peak is not None:
                    transpose_maxima(peak)
                if main is not None:
                    values(main, 3)
                if peak is not None:
                    maxima_rows(peak)
                if prep is not None:
                    project_values(prep)
                if main == 0:
                    pe.wait_ge(simsq_ready, 1)
                    ps = banks[5].take(pe, simsum_ready, 1)
                    for c in range(CC):
                        last = mm(ps[:, 0:NE], ones[:], sim_sq[:, c, :], c == 0, c == CC - 1)
                    last.then_inc(simsum_mm, 1)

            pe.wait_ge(xT_ready, NB)
            pe.wait_ge(simsum_ready, 2)
            ps = banks[5].take(pe, lg_read, 1)
            for b in range(NB):
                last = split_product(ps[:, b * NE:(b + 1) * NE],
                                     [(xT_hi[:, b, c, :], xT_lo[:, b, c, :], sim_hi[:, c, :], sim_lo[:, c, :])
                                      for c in range(CC)])
            last.then_inc(routed, 1)

            for e in range(NE):
                pe.wait_ge(whi_ready, e + 1)
                pe.wait_ge(wlo_ready, e + 1)
                for b in range(NB):
                    n = NB * e + b
                    ps = banks[n % 8].take(pe, moe_read, n + 1)
                    split_product(ps[:, 0:QKV],
                                  [(xT_hi[:, b, c, :], xT_lo[:, b, c, :], w_hi[e % 2][:, c, :], w_lo[e % 2][:, c, :])
                                   for c in range(CC)]).then_inc(moe_mm, 1)

            def output_experts(b, ks):
                if ks[0] == 0:
                    pe.wait_ge(ao_ready, b + 1)
                    pe.wait_ge(slo_ready, NE)
                for k in ks:
                    n = NE // 2 * b + k
                    ps = banks[n % 2].take(pe, oproj_read, n + 1)
                    two = slice(2 * k, 2 * k + 2)
                    split_product(ps[:].rearrange("p (e c) -> p e c", e=2),
                                  [(ao_hi[:], ao_lo[:], o_hi[:, two, :], o_lo[:, two, :])]).then_inc(oproj_mm, 1)

            def transposes(ps, parts, done):
                for n, part in enumerate(parts):
                    last = nc.tensor.transpose(ps[:, n * P:(n + 1) * P], part, ident[:])
                last.then_inc(done, 1)

            def last_experts(b):
                pe.wait_ge(combT_ready, b + 1)
                ps = banks[7].take(pe, acc4_ready, b + 1)
                mm(ps[:, 0:T], combT[:], b1_sb[:], True, True).then_inc(bias_mm, 1)
                for k in range(NE1 // 2):
                    n = NE1 // 2 * b + k
                    ps = banks[2 + n % 2].take(pe, l1_read, n + 1)
                    two = slice(2 * k, 2 * k + 2)
                    split_product(ps[:].rearrange("p (e c) -> p e c", e=2),
                                  [(x1_hi[:, c, :], x1_lo[:, c, :], w1_hi[:, c, two, :], w1_lo[:, c, two, :])
                                   for c in range(CC)]).then_inc(l1_mm, 1)

            for att, proj, wkv, last in TAIL:
                if last is not None:
                    pe.wait_ge(xn4_ready, last + 1)
                    transposes(banks[7].take(pe, x4_split, last + 1), [xn_1[:, c * P:(c + 1) * P] for c in range(CC)],
                               xn4_T)
                if wkv is not None:
                    pe.wait_ge(kn_ready, wkv + 1)
                    transposes(banks[6].take(pe, kT_ready, wkv + 1), [kn[:, c * P:(c + 1) * P] for c in range(CC)],
                               kn_T)
                if att is not None:
                    pe.wait_ge(moe_read, NB * (NE - 1) + att + 1)
                    transposes(banks[4].take(pe, qkT_ready, att + 1), [qkv[:, att, n * P:(n + 1) * P] for n in range(2)],
                               qk_T)
                if proj is not None:
                    output_experts(proj, (0, 1))
                if last is not None:
                    pe.wait_ge(x4_split, last + 1)
                    ps = banks[7].take(pe, nm4_ready, last + 1)
                    split_product(ps[:, 0:NE1], [(x1_hi[:, c, :], x1_lo[:, c, :], wg_hi[:, c, :], wg_lo[:, c, :])
                                                 for c in range(CC)]).then_inc(lg4_mm, 1)
                if att is not None:
                    pe.wait_ge(qkT_ready, att + 1)
                    ps = banks[5].take(pe, scr_ready, att + 1)
                    mm(ps[:, 0:P], qkT[:, 0, :], qkT[:, 1, :], True, True).then_inc(scored, 1)
                if proj is not None:
                    output_experts(proj, (2, 3, 4))
                if att is not None:
                    pe.wait_ge(pat_ready, att + 1)
                    transposes(banks[5].take(pe, patT_ready, att + 1), [pat[:]], pat_T)
                if last is not None:
                    pe.wait_ge(comb_ready, last + 1)
                    ps = banks[7].take(pe, combT_ready, last + 1)
                    nc.tensor.transpose(ps[0:NE1, 0:P], comb[:], ident[:]).then_inc(comb_T, 1)
                if proj is not None:
                    output_experts(proj, (5, 6, 7))
                if att is not None:
                    pe.wait_ge(patT_ready, att + 1)
                    ps = banks[4].take(pe, ao_ready, att + 1)
                    mm(ps[:, 0:P], qkv[:, att, 2 * HID:3 * HID], patT[:], True, True).then_inc(ao_mm, 1)
                if last is not None:
                    last_experts(last)
                if wkv is not None:
                    pe.wait_ge(y_ready, wkv + 1)
                    transposes(banks[6].take(pe, x3_ready, wkv + 1), [yT[:, c, :] for c in range(CC)], y_T)


_OUT = ((8, 128, 256), "float32")


def kernel(**inputs):
    import numpy as _np
    import concourse.bacc as _bacc
    from concourse import mybir as _mybir
    from concourse.bass_utils import run_bass_kernel_spmd as _run

    a = {k: _np.asarray(v) for k, v in inputs.items()}
    nb = a["x"].shape[0]
    laid = {
        "x": a["x"],
        "ctx": a["ctx_2048"],
        "ctxT": a["ctx_2048"].transpose(2, 0, 1),
        "mask": a["mask_Bx1x2048_fk1"].reshape(nb, -1),
        "maskT": a["mask_Bx1x2048_fk1"].reshape(nb, -1).T,
        "g_xattn": a["g_xattn"],
        "g_ffn": a["g_ffn"],
        "wqT": a["L0_xattn_Wq"].T,
        "wkT": a["L0_xattn_Wk"].T,
        "wvT": a["L0_xattn_Wv"].T,
        "bq": a["L0_xattn_bq"].reshape(-1, 1),
        "bk": a["L0_xattn_bk"].reshape(-1, 1),
        "bv": a["L0_xattn_bv"].reshape(1, -1),
        "sim": a["L0_ffn_sim_matrix"],
        "gates": a["L0_ffn_gates"],
        "wqkv": _np.concatenate([a["L0_ffn_q_proj"], a["L0_ffn_k_proj"], a["L0_ffn_v_proj"]], axis=2),
        "wo": a["L0_ffn_o_proj"],
        "wkv_w": a["L1_xattn_w"].reshape(-1, 128).T,
        "wkv_u": a["L1_xattn_u"].reshape(-1, 128).T,
        "wg": a["L1_ffn_wg"],
        "w1T": a["L1_ffn_W"].transpose(0, 2, 1),
        "b1": a["L1_ffn_b"],
    }
    nc = _bacc.Bacc("TRN2", target_bir_lowering=False, num_devices=1)
    arrays, args = {}, []
    for name, value in laid.items():
        value = _np.ascontiguousarray(value)
        arrays[f"in_{name}_dram"] = value
        args.append(nc.dram_tensor(f"in_{name}_dram", value.shape, _mybir.dt.from_np(value.dtype),
                                   kind="ExternalInput").ap())
    args.append(nc.dram_tensor("out_dram", _OUT[0], _mybir.dt.from_np(_np.dtype(_OUT[1])),
                               kind="ExternalOutput").ap())
    flamingo_two_layers(nc, *args)
    r = _run(nc, [arrays], core_ids=[0])
    return r.results[0]["out_dram"]
```

```python
from contextlib import ExitStack

import concourse.bass as bass
from concourse import mybir

ALU = mybir.AluOpType
ACT = mybir.ActivationFunctionType
AX = mybir.AxisListType
F32 = mybir.dt.float32
F32R = mybir.dt.float32r
U32 = mybir.dt.uint32

P = 128
NH = 16
HD = P // NH
QUADS = NH // 4
NEG_MASK = 1.0e6
NEG_CAUSAL = 1.0e9
NEG_START = -1.0e38
EPS = 1.0e-5


def head_of(quad, j):
    return 8 * (quad // 2) + 2 * j + quad % 2


class Tally:

    def __init__(self, sem):
        self.sem, self.n = sem, 0

    def step(self, instruction):
        instruction.then_inc(self.sem, 1)
        self.n += 1
        return self.n


class Bank:

    def __init__(self, psum):
        self.psum, self.reader = psum, None

    def take(self, engine, sem, value):
        if self.reader is not None:
            engine.wait_ge(*self.reader)
        self.reader = (sem, value)
        return self.psum


def flamingo_two_layers(nc, x, ctx, ctxT, mask, maskT, g_xattn, g_ffn, wqT, wkT, wvT, bq, bk, bv, sim, gates,
                        wqkv, wo, wkv_w, wkv_u, wg, w1T, b1, out):
    NB, _, T = x.shape
    CC = T // P
    NE = wqkv.shape[0]
    QKV = wqkv.shape[2]
    HID = QKV // 3
    NE1 = w1T.shape[0]
    XATTN_SCALE = float(HD) ** -0.5
    FFN_SCALE = float(HID) ** -0.5

    es = ExitStack()
    with es:
        def sb(name, shape, dt=F32):
            return es.enter_context(nc.sbuf_tensor(name, shape, dt))

        def sem(name):
            return es.enter_context(nc.semaphore(name))

        x_sb = sb("x_sb", [P, NB, T])
        mask_bc = sb("mask_bc", [P, NB, T])
        mask_col = sb("mask_col", [P, CC, NB])
        ctx_b = [sb(f"ctx_b{i}", [P, T]) for i in range(2)]
        ctxT_sb = sb("ctxT_sb", [P, CC, NB, P])
        wqT_sb, wkT_sb, wvT_sb = (sb(n, [P, P]) for n in ("wqT_sb", "wkT_sb", "wvT_sb"))
        bq_sb, bk_sb = sb("bq_sb", [P, 1]), sb("bk_sb", [P, 1])
        bv_sb = sb("bv_sb", [1, P])
        gx_sb, gf_sb = sb("gx_sb", [P, 2]), sb("gf_sb", [P, 2])
        tgx, tgf = sb("tgx", [P, 2]), sb("tgf", [P, 2])
        sim_sb = sb("sim_sb", [P, CC, NE])
        gates_sb = sb("gates_sb", [P, NE])
        wg_sb = sb("wg_sb", [P, CC, NE1])
        b1_sb = sb("b1_sb", [NE1, T])
        w_sb, u_sb = sb("w_sb", [P, CC]), sb("u_sb", [P, CC])
        ident = sb("ident", [P, P])
        ones = sb("ones", [P, P])
        zeros = sb("zeros", [P, P])
        minus_half = sb("minus_half", [P, NE])
        iota_e = sb("iota_e", [P, NE])
        causal = sb("causal", [P, P])
        causal_neg = sb("causal_neg", [P, P])
        arena = sb("arena", [P, 8 * QUADS * T], F32R)
        sel_q_hi, sel_q_lo, sel_k_hi, sel_k_lo = (
            arena[:, n * QUADS * P:(n + 1) * QUADS * P].rearrange("p (q n) -> p q n", q=QUADS) for n in range(4))
        sel_aux_q, sel_aux_k = (
            arena[:, (2 + n) * NB * P:(3 + n) * NB * P].rearrange("p (b n) -> p b n", b=NB) for n in range(2))
        q_stack0, q_stack1, q_stack_max, k_stack = (
            arena[:, (4 + n) * QUADS * T:(5 + n) * QUADS * T].rearrange("p (q t) -> p q t", q=QUADS)
            for n in range(4))
        q_stack = [q_stack0, q_stack1]
        sel_max = sb("sel_max", [2 * NH, QUADS, P], F32R)
        row_q, row_k = sb("row_q", [P, P]), sb("row_k", [P, P])
        batch_row = sb("batch_row", [P, NB])
        mask8 = sb("mask8", [P, T])
        aux_f = sb("aux_f", [P, 2, T])
        aux_q, aux_k = sb("aux_q", [P, T], F32R), sb("aux_k", [P, T], F32R)
        bn6 = sb("bn6", [P, NB, 6])
        mv = sb("mv", [P, NB, 2])
        var_eps, rstd = sb("var_eps", [P, NB]), sb("rstd", [P, NB])
        xn = sb("xn", [P, T])
        q_f, k_f = sb("q_f", [P, T]), sb("k_f", [P, T])
        q_hi, q_lo, k_hi, k_lo = (sb(n, [P, T], F32R) for n in ("q_hi", "q_lo", "k_hi", "k_lo"))
        k_pad = sb("k_pad", [P, 2 * QUADS, 4, T], F32R)
        v_pad = [sb(f"v_pad{i}", [P, CC, NH, 32]) for i in range(2)]
        mx = sb("mx", [P, CC, NH])
        neg_max = sb("neg_max", [P, CC, 2, NH], F32R)
        max_rows = sb("max_rows", [2 * NH, T], F32R)
        probs = sb("probs", [P, 8, CC, T])
        o_raw = sb("o_raw", [P, 2, T])
        o_den = sb("o_den", [P, CC, 2 * NH // 2])
        o_tok = sb("o_tok", [P, CC, P])
        bn6f, mvf = sb("bn6f", [P, 6]), sb("mvf", [P, 2])
        vef, rstdf = sb("vef", [P, 1]), sb("rstdf", [P, 1])
        xn_f = sb("xn_f", [P, T])
        sq_junk = sb("sq_junk", [P, T])
        nsq, rnorm = sb("nsq", [P, NB]), sb("rnorm", [P, NB])
        xT_hi, xT_lo = (sb(n, [P, NB, CC, P], F32R) for n in ("xT_hi", "xT_lo"))
        simn = sb("simn", [P, CC, NE])
        sim_sq = sb("sim_sq", [P, CC, NE])
        sim_r = sb("sim_r", [P, NE])
        sim_hi, sim_lo = sb("sim_hi", [P, CC, NE], F32R), sb("sim_lo", [P, CC, NE], F32R)
        sgate = sb("sgate", [P, NE])
        lg, gated, pos, fb = (sb(n, [P, NB, NE]) for n in ("lg", "gated", "pos", "fb"))
        top8, topi_f = sb("top8", [P, NB, 8]), sb("topi_f", [P, NB, 8])
        topi = sb("topi", [P, NB, 8], U32)
        inact, gmax, esum, ersum = (sb(n, [P, NB]) for n in ("inact", "gmax", "esum", "ersum"))
        w_e, w_et = sb("w_e", [P, NB, NE]), sb("w_et", [P, NB, NE])
        w_raw, w_hi, w_lo = ([sb(f"{n}{i}", [P, CC, QKV], d) for i in range(2)]
                             for n, d in (("w_raw", F32), ("w_hi", F32R), ("w_lo", F32R)))
        s_raw = [sb(f"s_raw{i}", [P, 2 * T]) for i in range(2)]
        qkv = probs[:].rearrange("p s c t -> p (s c t)")[:, 0:NB * QKV].rearrange("p (b n) -> p b n", b=NB)
        o_hi, o_lo = (k_pad[:, n * QUADS:(n + 1) * QUADS].rearrange("p q j t -> p (q j) t")
                      for n in range(2))
        w1_hi, w1_lo = (arena[:, n * CC * NE1 * T:(n + 1) * CC * NE1 * T].rearrange("p (c e t) -> p c e t", c=CC, e=NE1)
                        for n in range(2))
        qkT = sb("qkT", [P, 2, P])
        scr, pat, patT = sb("scr", [P, P]), sb("pat", [P, P]), sb("patT", [P, P])
        row_m, row_nm, row_s, row_r = (sb(n, [P, 1]) for n in ("row_m", "row_nm", "row_s", "row_r"))
        ao_hi, ao_lo = sb("ao_hi", [P, P], F32R), sb("ao_lo", [P, P], F32R)
        acc_odd = q_f
        w_full, u_full = sb("w_full", [P, CC, P]), sb("u_full", [P, CC, P])
        kn = ctx_b[0]
        kT = sb("kT", [P, CC, P])
        o_ext = sb("o_ext", [P, CC, P + 1])
        uk, no, ow = sb("uk", [P, CC, P]), sb("no", [P, CC, P]), sb("ow", [P, CC, P])
        arg1, arg2, e1, e2 = (mask_bc[:, 2 * n:2 * n + 2, :] for n in range(4))
        ev, e2v = sb("ev", [P, T]), sb("e2v", [P, T])
        pq = sb("pq", [P, 2, T + 1])
        num, den, yT = ctx_b[1], xn, sb("yT", [P, CC, P])
        xn_1 = sb("xn_1", [P, T])
        x1_hi, x1_lo = sb("x1_hi", [P, CC, P], F32R), sb("x1_lo", [P, CC, P], F32R)
        wg_hi, wg_lo = sb("wg_hi", [P, CC, NE1], F32R), sb("wg_lo", [P, CC, NE1], F32R)
        lg1, ex1, comb = sb("lg1", [P, NE1]), sb("ex1", [P, NE1]), sb("comb", [P, NE1])
        m8, i8f = sb("m8", [P, 8]), sb("i8f", [P, 8])
        i8 = sb("i8", [P, 8], U32)
        nm1, s1, r1 = sb("nm1", [P, 1]), sb("s1", [P, 1]), sb("r1", [P, 1])
        combT = sb("combT", [NE1, P])
        acc1 = k_f

        bank = [es.enter_context(nc.psum_tensor(f"bank{i}", [P, 512], F32)) for i in range(8)]

        ld_x, ld_mask, ld_mask8, ld_wts, ld_small, ld_late = (
            sem(n) for n in ("ld_x", "ld_mask", "ld_mask8", "ld_wts", "ld_small", "ld_late"))
        ctx_in = [sem("ctx_in0"), sem("ctx_in1")]
        kpad_in = [sem(f"kpad_in{i}") for i in range(2 * QUADS)]
        w_in, s_in = [sem("w_in0"), sem("w_in1")], [sem("s_in0"), sem("s_in1")]
        out_done = sem("out_done")
        consts, dve, setup_done, tanh_done = sem("consts"), sem("dve"), sem("setup_done"), sem("tanh_done")
        vef_ready, rstd_ready, xn_ready, qk_mm, v_mm = (
            sem(n) for n in ("vef_ready", "rstd_ready", "xn_ready", "qk_mm", "v_mm"))
        kf_ready, qk_split, v_ready, q_mm, k_mm, q_stacked, k_stacked = (
            sem(n) for n in ("kf_ready", "qk_split", "v_ready", "q_mm", "k_mm", "q_stacked", "k_stacked"))
        p1_done, p1_read, negmax_ready, max_T, max_copied, max_mm, q_max_ready = (
            sem(n) for n in ("p1_done", "p1_read", "negmax_ready", "max_T", "max_copied", "max_mm", "q_max_ready"))
        p2_done, exp_done, av_done, o_read, o_T, otok_ready, o_back, x1_ready = (
            sem(n) for n in ("p2_done", "exp_done", "av_done", "o_read", "o_T", "otok_ready", "o_back", "x1_ready"))
        ve2_ready, rstd2_ready, xn2_ready, xn2_T, xT_ready, sq_done = (
            sem(n) for n in ("ve2_ready", "rstd2_ready", "xn2_ready", "xn2_T", "xT_ready", "sq_done"))
        simsq_ready, simsum_mm, simsum_ready, simr_ready, sg_exp = (
            sem(n) for n in ("simsq_ready", "simsum_mm", "simsum_ready", "simr_ready", "sg_exp"))
        routed, nsq_ready, rnorm_ready, gated_ready, exp_w, lg_read = (
            sem(n) for n in ("routed", "nsq_ready", "rnorm_ready", "gated_ready", "exp_w", "lg_read"))
        whi_ready, wlo_ready, shi_ready, slo_ready, moe_mm, moe_read = (
            sem(n) for n in ("whi_ready", "wlo_ready", "shi_ready", "slo_ready", "moe_mm", "moe_read"))
        qk_T, qkT_ready, scored, scr_ready, pat_exp, pat_ready, pat_T, patT_ready, ao_mm, ao_ready = (
            sem(n) for n in ("qk_T", "qkT_ready", "scored", "scr_ready", "pat_exp", "pat_ready", "pat_T",
                             "patT_ready", "ao_mm", "ao_ready"))
        oproj_mm, oproj_read, ve3_ready, rstd3_ready, kn_ready, kn_T, kT_ready = (
            sem(n) for n in ("oproj_mm", "oproj_read", "ve3_ready", "rstd3_ready", "kn_ready", "kn_T", "kT_ready"))
        arg1_ready, e1_ready, arg2_ready, e2_ready, ev_ready, e2v_ready, y_ready, y_T, x3_ready = (
            sem(n) for n in ("arg1_ready", "e1_ready", "arg2_ready", "e2_ready", "ev_ready", "e2v_ready", "y_ready",
                             "y_T", "x3_ready"))
        ve4_ready, rstd4_ready, xn4_ready, xn4_T, x4_split, lg4_mm, nm4_ready, ex4_ready, comb_ready = (
            sem(n) for n in ("ve4_ready", "rstd4_ready", "xn4_ready", "xn4_T", "x4_split", "lg4_mm", "nm4_ready",
                             "ex4_ready", "comb_ready"))
        comb_T, combT_ready, bias_mm, acc4_ready, l1_mm, l1_read, xout_ready, wkv_used = (
            sem(n) for n in ("comb_T", "combT_ready", "bias_mm", "acc4_ready", "l1_mm", "l1_read", "xout_ready",
                             "wkv_used"))

        block = es.enter_context(nc.Block())

        def valid(*batches):
            return tuple(b if 0 <= b < NB else None for b in batches)

        PEAK_LEAD = 21
        NORMALISE, PROJECT, SPLIT = -36, -35, -34
        STACK = (-29, -28, -31, -30)
        NEGATE, MAX_T, MAX_ROWS = -5, -4, (-2, 0)
        VALUES_MM, VALUES_SPREAD = -14, -13
        VALUE_PRODUCTS = (5, 9, 13, 17)
        HEADS_OUT, HEADS_T, HEADS_NORM, HEADS_BACK, ADD = 18, 19, 20, 22, 23
        NORMALISE2, SECOND_T, SPLIT2 = 28, 30, 31
        TICKS = range(NORMALISE, NH * (NB - 1) + SPLIT2 + 1)

        def at(t, offset, work, *args):
            b, rest = divmod(t - offset, NH)
            if rest == 0 and 0 <= b < NB:
                work(b, *args)

        TAIL = [valid(i, i - 1, i - 2, i - 3) for i in range(NB + 3)]

        ST_PARITY = {}
        for t in TICKS:
            for use, offset in [*enumerate(STACK + MAX_ROWS), (6, VALUES_MM)]:
                at(t, offset, lambda b, u: ST_PARITY.setdefault((b, u), len(ST_PARITY) % 2), use)

        def st_bank(b, use):
            return bank[6 + ST_PARITY[(b, use)]][:]

        def side_part(n):
            if n % 2 == 0:
                k = n // 2
                return (o_hi[:, 2 * k:2 * k + 2, :], o_lo[:, 2 * k:2 * k + 2, :],
                        wo[2 * k:2 * k + 2].rearrange("e h c -> h e c"))
            c, k = divmod(n // 2, NE1 // 2)
            return (w1_hi[:, c, 2 * k:2 * k + 2, :], w1_lo[:, c, 2 * k:2 * k + 2, :],
                    w1T[2 * k:2 * k + 2, c * P:(c + 1) * P, :].rearrange("e h o -> h e o"))

        def pairs(tile):
            return tile.rearrange("p (e c) -> p e c", e=2)

        @block.sync
        def _(sp):
            def load_side(n):
                sp.dma_start(pairs(s_raw[n % 2][:]), side_part(n)[2]).then_inc(s_in[n % 2], 16)

            def load_expert(e):
                sp.dma_start(w_raw[e % 2][:], wqkv[e].rearrange("(c p) n -> p c n", p=P)).then_inc(w_in[e % 2], 16)

            sp.dma_start(x_sb[:], x.rearrange("b p t -> p b t")).then_inc(ld_x, 16)
            sp.dma_start(ctx_b[0][:], ctx[0]).then_inc(ctx_in[0], 16)
            for dst, src in ((wqT_sb, wqT), (wkT_sb, wkT), (wvT_sb, wvT)):
                sp.dma_start(dst[:], src).then_inc(ld_wts, 16)
            for dst, src in ((bq_sb, bq), (bk_sb, bk), (bv_sb, bv)):
                sp.dma_start(dst[:], src).then_inc(ld_wts, 16)
            sp.wait_ge(consts, 1)
            for s in range(4):
                sp.dma_start(mask8[32 * s:32 * s + NB, :], mask).then_inc(ld_mask8, 16)
            sp.dma_start(mask_bc[:], mask.partition_broadcast(P)).then_inc(ld_mask, 16)
            sp.dma_start(mask_col[:], maskT.rearrange("(c p) b -> p c b", p=P)).then_inc(ld_mask, 16)
            for dst, src in ((gx_sb[:], g_xattn.partition_broadcast(P)), (gf_sb[:], g_ffn.partition_broadcast(P)),
                             (gates_sb[:], gates.partition_broadcast(P)),
                             (sim_sb[:], sim.rearrange("(c p) e -> p c e", p=P))):
                sp.dma_start(dst, src).then_inc(ld_small, 16)
            sp.dma_start(ctx_b[1][:], ctx[1]).then_inc(ctx_in[1], 16)
            for dst, src in ((wg_sb[:], wg.rearrange("(c p) e -> p c e", p=P)), (b1_sb[:], b1),
                             (w_sb[:], wkv_w),
                             (u_sb[:], wkv_u),
                             (ctxT_sb[:], ctxT.rearrange("(c p) b t -> p c b t", p=P))):
                sp.dma_start(dst, src).then_inc(ld_late, 16)
            for n in range(2):
                load_expert(n)
                load_side(n)
            for b in range(NB):
                for quad in range(QUADS):
                    n = QUADS * b + quad
                    sp.wait_ge(k_stacked, 2 * b + quad // 2 + 1)
                    if n >= 8:
                        sp.wait_ge(p2_done, 4 * (n - 7))
                    else:
                        sp.wait_ge(setup_done, 1)
                    for j in range(4):
                        sp.dma_start(k_pad[32 * j:32 * j + 32, n % 8, j, :].bitcast(F32),
                                     k_stack[32 * j:32 * j + 32, quad, :].bitcast(F32)).then_inc(kpad_in[n % 8], 16)
                if b + 2 < NB:
                    sp.wait_ge(v_mm, b + 1)
                    sp.dma_start(ctx_b[b % 2][:], ctx[b + 2]).then_inc(ctx_in[b % 2], 16)
            for e in range(2, NE):
                sp.wait_ge(whi_ready, e - 1)
                sp.wait_ge(wlo_ready, e - 1)
                load_expert(e)
                sp.wait_ge(shi_ready, e - 1)
                sp.wait_ge(slo_ready, e - 1)
                load_side(e)
            for b in range(NB):
                sp.wait_ge(xout_ready, b + 1)
                sp.dma_start(out[b], x_sb[:, b, :]).then_inc(out_done, 16)
            sp.wait_ge(out_done, 16 * NB)

        @block.gpsimd
        def _(eng):
            g = nc.gpsimd
            made = Tally(consts)
            made.step(g.memset(mask8[:], 0.0))
            made.step(g.memset(ones[:], 1.0))
            made.step(g.memset(zeros[:], 0.0))
            made.step(g.memset(minus_half[:], -0.5))
            eng.wait_ge(consts, made.n)
            made.step(g.affine_select(out=ident[:], in_=ones[:], compare_op=ALU.is_equal, fill=0.0, base=0,
                                      pattern=[[-1, P]], channel_multiplier=1))
            made.step(g.affine_select(out=causal[:], in_=ones[:], compare_op=ALU.is_ge, fill=0.0, base=0,
                                      pattern=[[-1, P]], channel_multiplier=1))
            made.step(g.affine_select(out=causal_neg[:], in_=zeros[:], compare_op=ALU.is_ge, fill=-NEG_CAUSAL,
                                      base=0, pattern=[[-1, P]], channel_multiplier=1))
            made.step(g.iota(iota_e[:], pattern=[[1, NE]], base=0, channel_multiplier=0,
                             allow_small_or_imprecise_dtypes=True))
            for i in range(2):
                made.step(g.memset(v_pad[i][:], 0.0))
            eng.wait_ge(consts, made.n)
            for i in range(2):
                by_pair = v_pad[i][:].rearrange("p c (g i) n -> p (c g) i n", i=2)
                for k in range(2):
                    made.step(g.memset(by_pair[:, :, k, 16 + k:17 + k], 1.0))
            for i in range(2):
                made.step(g.memset(k_pad[:, QUADS * i:QUADS * (i + 1)].bitcast(F32), 0.0))
            eng.wait_ge(vef_ready, 1)
            g.tensor_tensor(rstd[:], var_eps[:], minus_half[:, 0:NB], ALU.pow).then_inc(rstd_ready, 1)
            eng.wait_ge(simsum_ready, 1)
            g.tensor_tensor(sim_r[:], sim_sq[:, 0, :], minus_half[:], ALU.pow).then_inc(simr_ready, 1)

            def expert_lo(e):
                eng.wait_ge(w_in[e % 2], 16 * (e // 2 + 1))
                eng.wait_ge(whi_ready, e + 1)
                if e >= 2:
                    eng.wait_ge(moe_mm, NB * (e - 1))
                g.tensor_tensor(w_lo[e % 2][:], w_raw[e % 2][:], w_hi[e % 2][:].bitcast(F32),
                                ALU.subtract).then_inc(wlo_ready, 1)

            def side_lo(n):
                eng.wait_ge(s_in[n % 2], 16 * (n // 2 + 1))
                eng.wait_ge(shi_ready, n + 1)
                hi, lo, _ = side_part(n)
                g.tensor_tensor(lo, pairs(s_raw[n % 2][:]), hi.bitcast(F32), ALU.subtract).then_inc(slo_ready, 1)

            for e in range(2):
                expert_lo(e)
            for b in range(NB):
                eng.wait_ge(ve2_ready, b + 1)
                g.tensor_tensor(rstdf[:], vef[:], minus_half[:, 0:1], ALU.pow).then_inc(rstd2_ready, 1)
            eng.wait_ge(nsq_ready, 1)
            g.tensor_tensor(rnorm[:], nsq[:], minus_half[:, 0:NB], ALU.pow).then_inc(rnorm_ready, 1)
            for e in range(NE):
                if e >= 2:
                    expert_lo(e)
                side_lo(e)
            for _, proj, wkv, last in TAIL:
                if wkv is not None:
                    eng.wait_ge(e2_ready, wkv + 1)
                    g.tensor_tensor(e2v[:].rearrange("p (c t) -> p c t", c=CC),
                                    e2[:, 1, :].rearrange("p (c t) -> p c t", c=CC), ctxT_sb[:, :, wkv, :],
                                    ALU.mult).then_inc(e2v_ready, 1)
                    eng.wait_ge(e1_ready, wkv + 1)
                    g.tensor_tensor(ev[:].rearrange("p (c t) -> p c t", c=CC),
                                    e1[:, 1, :].rearrange("p (c t) -> p c t", c=CC), ctxT_sb[:, :, wkv, :],
                                    ALU.mult).then_inc(ev_ready, 1)
                if proj is not None:
                    eng.wait_ge(ve3_ready, proj + 1)
                    g.tensor_tensor(rstd[:, 0:1], var_eps[:, 0:1], minus_half[:, 0:1], ALU.pow).then_inc(rstd3_ready, 1)
                if wkv is not None:
                    eng.wait_ge(ve4_ready, wkv + 1)
                    g.tensor_tensor(rstd[:, 1:2], var_eps[:, 1:2], minus_half[:, 0:1], ALU.pow).then_inc(rstd4_ready, 1)

        @block.scalar
        def _(act):
            a = nc.scalar
            act.wait_ge(ld_small, 64)
            a.activation(tgx[:], gx_sb[:], ACT.Tanh).then_inc(tanh_done, 1)
            a.activation(tgf[:], gf_sb[:], ACT.Tanh).then_inc(tanh_done, 1)
            a.activation(sgate[:], gates_sb[:], ACT.Exp, scale=-1.0).then_inc(sg_exp, 1)

            def expert_hi(e):
                act.wait_ge(w_in[e % 2], 16 * (e // 2 + 1))
                if e >= 2:
                    act.wait_ge(moe_mm, NB * (e - 1))
                a.activation(w_hi[e % 2][:], w_raw[e % 2][:], ACT.Copy).then_inc(whi_ready, 1)

            def side_hi(n):
                act.wait_ge(s_in[n % 2], 16 * (n // 2 + 1))
                a.activation(side_part(n)[0], pairs(s_raw[n % 2][:]), ACT.Copy).then_inc(shi_ready, 1)

            def exponential(n):
                if n % 4 == 0 and n >= 8:
                    act.wait_ge(av_done, n // 4 - 1)
                act.wait_ge(p2_done, n + 1)
                a.activation(probs[:, n % 8, :, :], bank[2 + n % 2][:].rearrange("p (c t) -> p c t", c=CC),
                             ACT.Exp).then_inc(exp_done, 1)

            def stack_copy(b, use):
                half = use % 2
                done, stacked, dst = ((q_mm, q_stacked, q_stack[b % 2]) if use < 2 else (k_mm, k_stacked, k_stack))
                if use == 0 and b >= 2:
                    act.wait_ge(q_max_ready, 2 * (b - 1))
                if use >= 2 and b >= 1:
                    for n in range(QUADS * (b - 1) + 2 * half, QUADS * (b - 1) + 2 * half + 2):
                        act.wait_ge(kpad_in[n % 8], 64 * (n // 8 + 1))
                act.wait_ge(done, 2 * b + half + 1)
                a.activation(dst[:, 2 * half:2 * half + 2, :],
                             st_bank(b, use).rearrange("p (q t) -> p q t", q=2), ACT.Copy).then_inc(stacked, 1)

            def heads_out(b):
                act.wait_ge(av_done, 4 * (b + 1))
                if b >= 1:
                    act.wait_ge(o_T, b)
                a.activation(o_raw[:], bank[4][:].rearrange("p (f t) -> p f t", f=2), ACT.Copy).then_inc(o_read, 1)

            def copy_maxima(b):
                act.wait_ge(max_T, b + 1)
                if b >= 1:
                    act.wait_ge(max_mm, 2 * b)
                a.activation(max_rows[:], bank[5][0:2 * NH, 0:T], ACT.Copy).then_inc(max_copied, 1)

            def square_second(b):
                act.wait_ge(xn2_ready, b + 1)
                a.activation(sq_junk[:], xn_f[:], ACT.Square, accum_out=nsq[:, b:b + 1]).then_inc(sq_done, 1)

            for t in TICKS:
                if 0 <= t < NH * NB:
                    exponential(t)
                for use, offset in enumerate(STACK):
                    at(t, offset, stack_copy, use)
                at(t, MAX_T, copy_maxima)
                at(t, HEADS_OUT, heads_out)
                at(t, NORMALISE2 + 1, square_second)
                if t in (6, 8):
                    expert_hi(t // 2 - 3)
            act.wait_ge(gated_ready, 1)
            a.activation(w_e[:], gated[:], ACT.Exp).then_inc(exp_w, 1)
            for e in range(NE):
                if e >= 2:
                    expert_hi(e)
                side_hi(e)

            for att, proj, wkv, last in TAIL:
                if wkv is not None:
                    act.wait_ge(kn_T, wkv + 1)
                    if wkv >= 1:
                        act.wait_ge(wkv_used, wkv)
                    a.activation(kT[:], bank[6][:, 0:T].rearrange("p (c t) -> p c t", c=CC), ACT.Copy).then_inc(kT_ready, 1)
                if att is not None:
                    act.wait_ge(qk_T, att + 1)
                    if att >= 1:
                        act.wait_ge(scored, att)
                    a.activation(qkT[:], bank[4][:, 0:2 * P].rearrange("p (c t) -> p c t", c=2),
                                 ACT.Copy).then_inc(qkT_ready, 1)
                if wkv is not None:
                    act.wait_ge(arg2_ready, wkv + 1)
                    a.activation(e2[:], arg2[:], ACT.Exp).then_inc(e2_ready, 1)
                    act.wait_ge(arg1_ready, wkv + 1)
                    a.activation(e1[:], arg1[:], ACT.Exp).then_inc(e1_ready, 1)
                if last is not None:
                    act.wait_ge(nm4_ready, last + 1)
                    a.activation(ex1[:], lg1[:], ACT.Exp, bias=nm1[:], accum_out=s1[:]).then_inc(ex4_ready, 1)
                if att is not None:
                    act.wait_ge(scr_ready, att + 1)
                    a.activation(pat[:], scr[:], ACT.Exp, bias=row_nm[:], accum_out=row_s[:]).then_inc(pat_exp, 1)
                    act.wait_ge(pat_T, att + 1)
                    if att >= 1:
                        act.wait_ge(ao_mm, att)
                    a.activation(patT[:], bank[5][:, 0:P], ACT.Copy).then_inc(patT_ready, 1)
                if last is not None:
                    act.wait_ge(comb_T, last + 1)
                    if last >= 1:
                        act.wait_ge(bias_mm, last)
                    a.activation(combT[:], bank[7][0:NE1, 0:P], ACT.Copy).then_inc(combT_ready, 1)

        @block.vector
        def _(eng):
            v = nc.vector
            d = Tally(dve)

            def then(instruction):
                eng.wait_ge(dve, d.step(instruction))

            eng.wait_ge(ld_x, 16)
            for b in range(NB):
                n = d.step(v.bn_stats(bn6[:, b, :], x_sb[:, b, :]))
            eng.wait_ge(dve, n)
            for b in range(NB):
                n = d.step(v.bn_aggr(mv[:, b, :], bn6[:, b, :]))
            eng.wait_ge(dve, n)
            v.tensor_scalar(var_eps[:], mv[:, :, 1], EPS, None, ALU.add).then_inc(vef_ready, 1)

            for t in (sel_q_hi, sel_q_lo, sel_k_hi, sel_k_lo, sel_max):
                n = d.step(v.memset(t[:].bitcast(F32), 0.0))
            for t in (row_q, row_k):
                n = d.step(v.memset(t[:], 0.0))
            eng.wait_ge(dve, n)
            eng.wait_ge(consts, 8)
            for t, parts in ((sel_q_hi, (0, 1)), (sel_q_lo, (2,)), (sel_k_hi, (0, 2)), (sel_k_lo, (1,))):
                for quad in range(QUADS):
                    half, odd = divmod(quad, 2)
                    src = ident[:, 64 * half:64 * half + 64].rearrange("p (j n) -> p j n", n=16)[
                        :, :, HD * odd:HD * (odd + 1)]
                    dst = t[:, quad, :].rearrange("p (j n) -> p j n", j=4)
                    for part in parts:
                        n = d.step(v.tensor_copy(dst[:, :, HD * part:HD * (part + 1)], src))
            for quad in range(QUADS):
                for part in range(2):
                    h0 = NH * part + head_of(quad, 0)
                    n = d.step(v.tensor_copy(sel_max[:, quad, 29 + part::32], ident[0:2 * NH, h0:h0 + 7:2]))
            by_head_q = row_q[:].rearrange("p (j n) -> p j n", j=4)
            by_head_k = row_k[:].rearrange("p (j n) -> p j n", j=4)
            for s, row, end in ((0, 24, 26), (1, 26, 27), (2, 27, 28), (3, 28, 29)):
                n = d.step(v.memset(by_head_q[32 * s:32 * s + 32, :, row:end], 1.0))
            for s, row, end in ((0, 24, 25), (0, 26, 27), (1, 25, 26), (2, 27, 31)):
                n = d.step(v.memset(by_head_k[32 * s:32 * s + 32, :, row:end], 1.0))
            for s in range(4):
                n = d.step(v.tensor_copy(batch_row[32 * s:32 * s + 32, :], ident[32 * s:32 * s + 32, 32 * s:32 * s + NB]))
            eng.wait_ge(ld_mask8, 64)
            n = d.step(v.tensor_scalar(aux_f[0:64, 0, :], mask8[0:64, :], -NEG_MASK, None, ALU.mult))
            n = d.step(v.tensor_scalar(aux_f[64:128, 0, :], mask8[64:128, :], 1.0, NEG_MASK, ALU.subtract, ALU.mult))
            n = d.step(v.tensor_scalar(aux_f[:, 1, :], mask8[:], -1.0, 1.0, ALU.mult, ALU.add))
            eng.wait_ge(dve, n)
            for dst, k in ((aux_q, 0), (aux_k, 1)):
                n = d.step(v.tensor_copy(dst[:], aux_f[:, k, :]))
            eng.wait_ge(dve, n)
            for p0, dst, k in ((32, aux_q, 0), (96, aux_q, 0), (32, aux_k, 1)):
                n = d.step(v.tensor_tensor(dst[p0:p0 + 32, :], aux_f[p0:p0 + 32, k, :],
                                           dst[p0:p0 + 32, :].bitcast(F32), ALU.subtract))
            n = d.step(v.tensor_scalar(aux_k[64:96, :], aux_f[64:96, 1, :], 0.0, 1.0, ALU.mult, ALU.add))
            n = d.step(v.tensor_scalar(aux_k[96:128, :], aux_f[96:128, 1, :], 0.0, None, ALU.mult))
            for dst, rows in ((sel_aux_q, row_q), (sel_aux_k, row_k)):
                n = d.step(v.tensor_tensor(dst[:], batch_row[:].unsqueeze(2).to_broadcast([P, NB, P]),
                                           rows[:].unsqueeze(1).to_broadcast([P, NB, P]), ALU.mult))
            eng.wait_ge(ld_mask, 32)
            eng.wait_ge(ld_wts, 96)
            n = d.step(v.tensor_scalar(wqT_sb[:], wqT_sb[:], XATTN_SCALE, None, ALU.mult))
            n = d.step(v.tensor_scalar(bq_sb[:], bq_sb[:], XATTN_SCALE, None, ALU.mult))
            eng.wait_ge(dve, n)
            eng.wait_ge(consts, 16)
            v.memset(pq[:, :, 0:1], 0.0).then_inc(setup_done, 1)

            def prepare(b):
                if b == 0:
                    eng.wait_ge(rstd_ready, 1)
                else:
                    eng.wait_ge(qk_mm, b)
                v.tensor_scalar(xn[:], x_sb[:, b, :], mv[:, b, 0:1], rstd[:, b:b + 1], ALU.subtract,
                                ALU.mult).then_inc(xn_ready, 1)

            def project(b):
                eng.wait_ge(ld_wts, 96)
                eng.wait_ge(qk_mm, b + 1)
                v.scalar_tensor_tensor(q_f[:], bank[5][:, 0:T], bq_sb[:], mask_bc[:, b, :], ALU.add,
                                       ALU.mult).then_inc(dve, 1)
                d.n += 1
                nq = d.n
                v.scalar_tensor_tensor(k_f[:], bank[5][:, T:2 * T], bk_sb[:], mask_bc[:, b, :], ALU.add,
                                       ALU.mult).then_inc(kf_ready, 1)
                if b >= 1:
                    eng.wait_ge(q_mm, 2 * b)
                eng.wait_ge(dve, nq)
                nq = d.step(v.tensor_copy(q_hi[:], q_f[:]))
                eng.wait_ge(kf_ready, b + 1)
                nk = d.step(v.tensor_copy(k_hi[:], k_f[:]))
                eng.wait_ge(dve, nq)
                d.step(v.tensor_tensor(q_lo[:], q_f[:], q_hi[:].bitcast(F32), ALU.subtract))
                eng.wait_ge(dve, nk)
                v.tensor_tensor(k_lo[:], k_f[:], k_hi[:].bitcast(F32), ALU.subtract).then_inc(qk_split, 1)

            def spread_values(b):
                eng.wait_ge(v_mm, b + 1)
                if b >= 2:
                    eng.wait_ge(av_done, 4 * (b - 1))
                vp = v_pad[b % 2][:].rearrange("p c (g i) n -> p c g i n", i=2)
                src = st_bank(b, 6)[:, 0:CC * P].rearrange("p (c g i n) -> p c g i n", c=CC, i=2, n=HD)
                for c in range(CC):
                    for i in range(2):
                        v.tensor_scalar(vp[:, c, :, i, HD * i:HD * (i + 1)], src[:, c, :, i, :],
                                        mask_col[:, c, b:b + 1], None, ALU.mult).then_inc(v_ready, 1)

            def maxima(n):
                h = head_of(n % NH // 4, n % 4)
                eng.wait_ge(p1_done, n + 1)
                if n % NH == 0 and n:
                    eng.wait_ge(negmax_ready, n // NH)
                v.tensor_reduce(mx[:, :, h], bank[n % 2][:].rearrange("p (c s) -> p c s", c=CC), axis=AX.X,
                                op=ALU.max).then_inc(p1_read, 1)

            def negate_maxima(b):
                eng.wait_ge(p1_read, NH * (b + 1))
                if b >= 1:
                    eng.wait_ge(max_T, b)
                then(v.tensor_scalar(neg_max[:, :, 0, :], mx[:], -1.0, None, ALU.mult))
                v.scalar_tensor_tensor(neg_max[:, :, 1, :], mx[:], -1.0, neg_max[:, :, 0, :].bitcast(F32), ALU.mult,
                                       ALU.subtract).then_inc(negmax_ready, 1)

            def add_maxima(b, half):
                if b >= 1:
                    eng.wait_ge(p2_done, NH * (b - 1) + 8 * (half + 1))
                eng.wait_ge(q_stacked, 2 * (b + 1))
                eng.wait_ge(max_mm, 2 * b + half + 1)
                s = slice(2 * half, 2 * half + 2)
                v.tensor_tensor(q_stack_max[:, s, :], st_bank(b, 4 + half).rearrange("p (q t) -> p q t", q=2),
                                q_stack[b % 2][:, s, :].bitcast(F32), ALU.add).then_inc(q_max_ready, 1)

            def normalise_heads(b):
                eng.wait_ge(o_T, b + 1)
                cols = bank[5][:].rearrange("p (g n) -> p g n", n=32)
                then(v.reciprocal(o_den[:].rearrange("p c (g i) -> p (c g) i", i=2), cols[:, :, 16:18]))
                then(v.tensor_tensor(o_den[:], o_den[:], mask_col[:, :, b:b + 1].to_broadcast([P, CC, NH]), ALU.mult))
                if b >= 1:
                    eng.wait_ge(o_back, b)
                v.tensor_tensor(o_tok[:].rearrange("p c (g i n) -> p (c g) i n", i=2, n=HD),
                                cols[:, :, 0:16].rearrange("p g (i n) -> p g i n", i=2),
                                o_den[:].rearrange("p c (g i) -> p (c g) i", i=2).unsqueeze(3).to_broadcast(
                                    [P, CC * NH // 2, 2, HD]), ALU.mult).then_inc(otok_ready, 1)

            def add_attention(b):
                eng.wait_ge(tanh_done, 2)
                eng.wait_ge(o_back, b + 1)
                v.scalar_tensor_tensor(x_sb[:, b, :], bank[5][:, 0:T], tgx[:, 0:1], x_sb[:, b, :], ALU.mult,
                                       ALU.add).then_inc(x1_ready, 1)
                eng.wait_ge(x1_ready, b + 1)
                then(v.bn_stats(bn6f[:], x_sb[:, b, :]))
                then(v.bn_aggr(mvf[:], bn6f[:]))
                if b >= 1:
                    eng.wait_ge(rstd2_ready, b)
                v.tensor_scalar(vef[:], mvf[:, 1:2], EPS, None, ALU.add).then_inc(ve2_ready, 1)

            def normalise_second(b):
                eng.wait_ge(rstd2_ready, b + 1)
                if b >= 1:
                    eng.wait_ge(xn2_T, b)
                    eng.wait_ge(sq_done, b)
                v.tensor_scalar(xn_f[:], x_sb[:, b, :], mvf[:, 0:1], rstdf[:], ALU.subtract,
                                ALU.mult).then_inc(xn2_ready, 1)

            def split_second(b):
                eng.wait_ge(xn2_T, b + 1)
                src = bank[5][:, 0:T].rearrange("p (c n) -> p c n", c=CC)
                then(v.tensor_copy(xT_hi[:, b, :, :], src))
                v.tensor_tensor(xT_lo[:, b, :, :], src, xT_hi[:, b, :, :].bitcast(F32),
                                ALU.subtract).then_inc(xT_ready, 1)

            def other_constants():
                eng.wait_ge(ld_small, 64)
                v.tensor_tensor(sim_sq[:], sim_sb[:], sim_sb[:], ALU.mult).then_inc(simsq_ready, 1)
                eng.wait_ge(sg_exp, 1)
                then(v.tensor_scalar(sgate[:], sgate[:], 1.0, None, ALU.add))
                then(v.reciprocal(sgate[:], sgate[:]))
                eng.wait_ge(ld_late, 80)
                for c in range(CC):
                    d.step(v.tensor_scalar(w_full[:, c, :], ones[:], w_sb[:, c:c + 1], None, ALU.mult))
                    d.step(v.tensor_scalar(u_full[:, c, :], ones[:], u_sb[:, c:c + 1], None, ALU.mult))
                d.step(v.memset(o_ext[:, :, 0:1], NEG_START))
                then(v.tensor_copy(wg_hi[:], wg_sb[:]))
                then(v.tensor_tensor(wg_lo[:], wg_sb[:], wg_hi[:].bitcast(F32), ALU.subtract))

            def router_sums():
                eng.wait_ge(simsum_mm, 1)
                v.tensor_scalar(sim_sq[:, 0, :], bank[5][:, 0:NE], 1e-24, None, ALU.max).then_inc(simsum_ready, 1)

            def router_columns():
                eng.wait_ge(simr_ready, 1)
                then(v.tensor_tensor(simn[:], sim_sb[:], sim_r[:].unsqueeze(1).to_broadcast([P, CC, NE]), ALU.mult))
                then(v.tensor_copy(sim_hi[:], simn[:]))
                v.tensor_tensor(sim_lo[:], simn[:], sim_hi[:].bitcast(F32), ALU.subtract).then_inc(simsum_ready, 1)

            for t in TICKS:
                at(t, NEGATE, negate_maxima)
                if 0 <= t + PEAK_LEAD < NH * NB:
                    maxima(t + PEAK_LEAD)
                at(t, NORMALISE, prepare)
                at(t, SPLIT, project)
                for half, offset in enumerate(MAX_ROWS):
                    at(t, offset + 1, add_maxima, half)
                at(t, VALUES_SPREAD, spread_values)
                at(t, HEADS_NORM, normalise_heads)
                at(t, ADD, add_attention)
                at(t, NORMALISE2, normalise_second)
                at(t, SPLIT2, split_second)
                if t == 2:
                    other_constants()
                if t == 5:
                    router_sums()
                if t == 10:
                    router_columns()

            eng.wait_ge(sq_done, NB)
            v.tensor_scalar(nsq[:], nsq[:], 1e-24, None, ALU.max).then_inc(nsq_ready, 1)
            eng.wait_ge(rnorm_ready, 1)
            eng.wait_ge(routed, 1)
            v.tensor_tensor(lg[:], bank[5][:, 0:NB * NE].rearrange("p (b e) -> p b e", b=NB),
                            rnorm[:].unsqueeze(2).to_broadcast([P, NB, NE]), ALU.mult).then_inc(lg_read, 1)
            eng.wait_ge(lg_read, 1)
            then(v.tensor_tensor(lg[:], lg[:], sgate[:].unsqueeze(1).to_broadcast([P, NB, NE]), ALU.subtract))
            for b in range(NB):
                n = d.step(v.max(top8[:, b, :], lg[:, b, :]))
            eng.wait_ge(dve, n)
            for b in range(NB):
                n = d.step(v.max_index(topi[:, b, :], top8[:, b, :], lg[:, b, :]))
            then(v.tensor_scalar(gmax[:], top8[:, :, 0], 0.0, None, ALU.max))
            then(v.tensor_scalar(gated[:], lg[:], 0.0, None, ALU.max))
            v.tensor_tensor(gated[:], gated[:], gmax[:].unsqueeze(2).to_broadcast([P, NB, NE]),
                            ALU.subtract).then_inc(gated_ready, 1)
            then(v.tensor_copy(topi_f[:], topi[:]))
            iota_b = iota_e[:].unsqueeze(1).to_broadcast([P, NB, NE])
            then(v.tensor_tensor(fb[:], iota_b, topi_f[:, :, 0:1].to_broadcast([P, NB, NE]), ALU.is_equal))
            then(v.tensor_tensor(pos[:], iota_b, topi_f[:, :, 1:2].to_broadcast([P, NB, NE]), ALU.is_equal))
            then(v.tensor_tensor(fb[:], fb[:], pos[:], ALU.add))
            then(v.tensor_scalar(inact[:], top8[:, :, 0], 0.0, None, ALU.is_le))
            then(v.tensor_tensor(fb[:], fb[:], inact[:].unsqueeze(2).to_broadcast([P, NB, NE]), ALU.mult))
            then(v.tensor_scalar(pos[:], lg[:], 0.0, None, ALU.is_gt))
            then(v.tensor_tensor(pos[:], pos[:], fb[:], ALU.add))
            eng.wait_ge(exp_w, 1)
            then(v.tensor_tensor(w_e[:], w_e[:], pos[:], ALU.mult))
            then(v.tensor_reduce(esum[:], w_e[:], axis=AX.X, op=ALU.add))
            then(v.reciprocal(ersum[:], esum[:]))
            then(v.tensor_tensor(w_e[:], w_e[:], ersum[:].unsqueeze(2).to_broadcast([P, NB, NE]), ALU.mult))
            then(v.tensor_scalar(w_et[:], w_e[:], tgf[:, 0:1], None, ALU.mult))

            for e in range(NE):
                for b in range(NB):
                    n = NB * e + b
                    eng.wait_ge(moe_mm, n + 1)
                    src = bank[n % 8][:, 0:QKV]
                    if e == 0:
                        v.tensor_scalar(qkv[:, b, :], src, w_e[:, b, e:e + 1], None, ALU.mult).then_inc(moe_read, 1)
                    else:
                        eng.wait_ge(moe_read, n - NB + 1)
                        v.scalar_tensor_tensor(qkv[:, b, :], src, w_e[:, b, e:e + 1], qkv[:, b, :], ALU.mult,
                                               ALU.add).then_inc(moe_read, 1)

            def flat(tile):
                return tile.rearrange("p (c t) -> p c t", c=CC)

            def output_experts(b, ks):
                for k in ks:
                    n = NE // 2 * b + k
                    eng.wait_ge(oproj_mm, n + 1)
                    src = bank[n % 2]
                    even, odd = w_et[:, b, 2 * k:2 * k + 1], w_et[:, b, 2 * k + 1:2 * k + 2]
                    if k:
                        eng.wait_ge(oproj_read, n)
                        eng.wait_ge(dve, d.n)
                    d.step(v.scalar_tensor_tensor(x_sb[:, b, :], src[:, 0:T], even, x_sb[:, b, :], ALU.mult, ALU.add))
                    if k == 0:
                        v.tensor_scalar(acc_odd[:], src[:, T:2 * T], odd, None, ALU.mult).then_inc(oproj_read, 1)
                    else:
                        v.scalar_tensor_tensor(acc_odd[:], src[:, T:2 * T], odd, acc_odd[:], ALU.mult,
                                               ALU.add).then_inc(oproj_read, 1)

            def statistics(b, col, ready):
                then(v.bn_stats(bn6f[:], x_sb[:, b, :]))
                then(v.bn_aggr(mv[:, col, :], bn6f[:]))
                v.tensor_scalar(var_eps[:, col:col + 1], mv[:, col, 1:2], EPS, None, ALU.add).then_inc(ready, 1)

            def experts_done(b):
                eng.wait_ge(oproj_read, NE // 2 * (b + 1))
                eng.wait_ge(dve, d.n)
                then(v.tensor_tensor(x_sb[:, b, :], x_sb[:, b, :], acc_odd[:], ALU.add))
                statistics(b, 0, ve3_ready)

            def keys(b):
                eng.wait_ge(rstd3_ready, b + 1)
                if b >= 1:
                    eng.wait_ge(kn_T, b)
                v.tensor_scalar(kn[:], x_sb[:, b, :], mv[:, 0, 0:1], rstd[:, 0:1], ALU.subtract,
                                ALU.mult).then_inc(kn_ready, 1)

            def wkv_exponents(b):
                o_prev, o_next = o_ext[:, :, 0:P], o_ext[:, :, 1:P + 1]
                eng.wait_ge(kT_ready, b + 1)
                for c in range(CC):
                    d.step(v.tensor_tensor_scan(o_ext[:, c, 1:P + 1], w_full[:, c, :], kT[:, c, :], NEG_START,
                                                op0=ALU.add, op1=ALU.max))
                d.step(v.tensor_tensor(uk[:], kT[:], u_full[:], ALU.add))
                eng.wait_ge(dve, d.n)
                n_ow = d.step(v.tensor_tensor(ow[:], o_prev, w_full[:], ALU.add))
                n_no = d.step(v.tensor_tensor(no[:], o_prev, uk[:], ALU.max))
                eng.wait_ge(dve, n_ow)
                d.step(v.tensor_tensor(flat(arg2[:, 0, :]), ow[:], o_next, ALU.subtract))
                if b >= 1:
                    eng.wait_ge(e2_ready, b)
                v.tensor_tensor(flat(arg2[:, 1, :]), kT[:], o_next, ALU.subtract).then_inc(arg2_ready, 1)
                eng.wait_ge(dve, d.n)
                d.step(v.tensor_tensor(flat(arg1[:, 0, :]), o_prev, no[:], ALU.subtract))
                v.tensor_tensor(flat(arg1[:, 1, :]), uk[:], no[:], ALU.subtract).then_inc(arg1_ready, 1)
                eng.wait_ge(arg2_ready, b + 1)

            def wkv_sums(b):
                eng.wait_ge(e2v_ready, b + 1)
                eng.wait_ge(e2_ready, b + 1)
                d.step(v.tensor_tensor_scan(pq[:, 0, 1:T + 1], e2[:, 0, :], e2v[:], 0.0, op0=ALU.mult, op1=ALU.add))
                then(v.tensor_tensor_scan(pq[:, 1, 1:T + 1], e2[:, 0, :], e2[:, 1, :], 0.0, op0=ALU.mult,
                                          op1=ALU.add))
                eng.wait_ge(e1_ready, b + 1)
                n_num = d.step(v.tensor_tensor(num[:], e1[:, 0, :], pq[:, 0, 0:T], ALU.mult))
                n_den = d.step(v.tensor_tensor(den[:], e1[:, 0, :], pq[:, 1, 0:T], ALU.mult))
                eng.wait_ge(dve, n_den)
                then(v.tensor_tensor(den[:], den[:], e1[:, 1, :], ALU.add))
                n_den = d.step(v.reciprocal(den[:], den[:]))
                eng.wait_ge(ev_ready, b + 1)
                n_num = d.step(v.tensor_tensor(num[:], num[:], ev[:], ALU.add))
                eng.wait_ge(dve, n_num)
                if b >= 1:
                    eng.wait_ge(y_T, b)
                v.tensor_tensor(yT[:], flat(num[:]), flat(den[:]), ALU.mult).then_inc(y_ready, 1)
                eng.wait_ge(y_ready, b + 1)
                v.memset(row_m[:, 0:1], 0.0).then_inc(wkv_used, 1)

            def add_wkv(b):
                eng.wait_ge(y_T, b + 1)
                v.scalar_tensor_tensor(x_sb[:, b, :], bank[6][:, 0:T], tgx[:, 1:2], x_sb[:, b, :], ALU.mult,
                                       ALU.add).then_inc(x3_ready, 1)
                eng.wait_ge(x3_ready, b + 1)
                statistics(b, 1, ve4_ready)

            def normalise_last(b):
                eng.wait_ge(rstd4_ready, b + 1)
                v.tensor_scalar(xn_1[:], x_sb[:, b, :], mv[:, 1, 0:1], rstd[:, 1:2], ALU.subtract,
                                ALU.mult).then_inc(xn4_ready, 1)

            def split_last(b):
                eng.wait_ge(xn4_T, b + 1)
                src = flat(bank[7][:, 0:T])
                if b >= 1:
                    eng.wait_ge(l1_mm, NE1 // 2 * b)
                then(v.tensor_copy(x1_hi[:], src))
                v.tensor_tensor(x1_lo[:], src, x1_hi[:].bitcast(F32), ALU.subtract).then_inc(x4_split, 1)

            def gate_last(b):
                eng.wait_ge(lg4_mm, b + 1)
                then(v.tensor_copy(lg1[:], bank[7][:, 0:NE1]))
                then(v.max(m8[:], lg1[:]))
                d.step(v.max_index(i8[:], m8[:], lg1[:]))
                v.tensor_scalar(nm1[:], m8[:, 0:1], -1.0, None, ALU.mult).then_inc(nm4_ready, 1)

            def combine_last(b):
                eng.wait_ge(dve, d.n)
                then(v.tensor_copy(i8f[:], i8[:]))
                then(v.tensor_scalar(comb[:], iota_e[:, 0:NE1], i8f[:, 0:1], None, ALU.is_equal))
                eng.wait_ge(ex4_ready, b + 1)
                then(v.reciprocal(r1[:], s1[:]))
                then(v.tensor_tensor(r1[:], r1[:], tgf[:, 1:2], ALU.mult))
                v.tensor_scalar(comb[:], comb[:], r1[:], None, ALU.mult).then_inc(comb_ready, 1)

            def last_experts(b):
                eng.wait_ge(comb_ready, b + 1)
                eng.wait_ge(bias_mm, b + 1)
                v.tensor_tensor(x_sb[:, b, :], bank[7][:, 0:T], x_sb[:, b, :], ALU.add).then_inc(acc4_ready, 1)
                eng.wait_ge(acc4_ready, b + 1)
                for k in range(NE1 // 2):
                    n = NE1 // 2 * b + k
                    eng.wait_ge(l1_mm, n + 1)
                    src = bank[2 + n % 2]
                    even, odd = comb[:, 2 * k:2 * k + 1], comb[:, 2 * k + 1:2 * k + 2]
                    if k:
                        eng.wait_ge(l1_read, n)
                        eng.wait_ge(dve, d.n)
                    d.step(v.scalar_tensor_tensor(x_sb[:, b, :], src[:, 0:T], even, x_sb[:, b, :], ALU.mult, ALU.add))
                    if k == 0:
                        v.tensor_scalar(acc1[:], src[:, T:2 * T], odd, None, ALU.mult).then_inc(l1_read, 1)
                    else:
                        v.scalar_tensor_tensor(acc1[:], src[:, T:2 * T], odd, acc1[:], ALU.mult,
                                               ALU.add).then_inc(l1_read, 1)
                eng.wait_ge(l1_read, NE1 // 2 * (b + 1))
                eng.wait_ge(dve, d.n)
                v.tensor_tensor(x_sb[:, b, :], x_sb[:, b, :], acc1[:], ALU.add).then_inc(xout_ready, 1)

            def mask_scores(b):
                eng.wait_ge(scored, b + 1)
                then(v.scalar_tensor_tensor(scr[:], bank[5][:, 0:P], FFN_SCALE, causal[:], ALU.mult, ALU.mult))
                then(v.tensor_tensor_reduce(out=scr[:], in0=scr[:], in1=causal_neg[:], scale=1.0, scalar=-3.0e38,
                                            op0=ALU.add, op1=ALU.max, accum_out=row_m[:]))
                v.tensor_scalar(row_nm[:], row_m[:], -1.0, None, ALU.mult).then_inc(scr_ready, 1)

            def normalise_rows(b):
                eng.wait_ge(pat_exp, b + 1)
                then(v.reciprocal(row_r[:], row_s[:]))
                v.tensor_scalar(pat[:], pat[:], row_r[:], None, ALU.mult).then_inc(pat_ready, 1)

            def split_attention(b):
                eng.wait_ge(ao_mm, b + 1)
                if b >= 1:
                    eng.wait_ge(oproj_mm, NE // 2 * b)
                then(v.tensor_copy(ao_hi[:], bank[4][:, 0:P]))
                v.tensor_tensor(ao_lo[:], bank[4][:, 0:P], ao_hi[:].bitcast(F32), ALU.subtract).then_inc(ao_ready, 1)

            for att, proj, wkv, last in TAIL:
                if last is not None:
                    split_last(last)
                if wkv is not None:
                    wkv_exponents(wkv)
                if proj is not None:
                    output_experts(proj, (0, 1))
                if last is not None:
                    gate_last(last)
                if att is not None:
                    mask_scores(att)
                if proj is not None:
                    output_experts(proj, (2, 3, 4))
                if att is not None:
                    normalise_rows(att)
                if last is not None:
                    combine_last(last)
                if wkv is not None:
                    wkv_sums(wkv)
                if proj is not None:
                    output_experts(proj, (5, 6, 7))
                    experts_done(proj)
                if att is not None:
                    split_attention(att)
                if last is not None:
                    last_experts(last)
                if proj is not None:
                    keys(proj)
                if wkv is not None:
                    add_wkv(wkv)
                    normalise_last(wkv)

        @block.tensor
        def _(pe):
            banks = [Bank(b) for b in bank]
            stack_uses = [0]

            def stack_bank(b, use, reader, value):
                assert ST_PARITY[(b, use)] == stack_uses[0] % 2
                stack_uses[0] += 1
                return banks[6 + ST_PARITY[(b, use)]].take(pe, reader, value)

            def mm(out_, lhsT, rhs, start, stop):
                return nc.tensor.matmul(out_, lhsT, rhs, start=start, stop=stop)

            def split_product(out_, terms):
                steps = [s for lh, ll, rh, rl in terms for s in ((lh, rh), (lh, rl), (ll, rh))]
                for n, (l, r) in enumerate(steps):
                    last = mm(out_, l, r, n == 0, n == len(steps) - 1)
                return last

            def project(b):
                pe.wait_ge(setup_done, 1)
                pe.wait_ge(xn_ready, b + 1)
                pe.wait_ge(ctx_in[b % 2], 16 * (b // 2 + 1))
                ps = banks[5].take(pe, kf_ready, b + 1)
                mm(ps[:, 0:T], wqT_sb[:], xn[:], True, True)
                mm(ps[:, T:2 * T], wkT_sb[:], ctx_b[b % 2][:], True, True).then_inc(qk_mm, 1)

            def project_values(b):
                ps = stack_bank(b, 6, v_ready, 2 * CC * (b + 1))
                for c in range(CC):
                    mm(ps[:, c * P:(c + 1) * P], ctx_b[b % 2][:, c * P:(c + 1) * P], wvT_sb[:], True, False)
                    last = mm(ps[:, c * P:(c + 1) * P], ones[0:1, :], bv_sb[:], False, True)
                last.then_inc(v_mm, 1)

            def stack(b, use):
                if use == 2:
                    pe.wait_ge(qk_split, b + 1)
                hi, lo, s_hi, s_lo, aux, s_aux, done, stacked = (
                    (q_hi, q_lo, sel_q_hi, sel_q_lo, aux_q, sel_aux_q, q_mm, q_stacked) if use < 2 else
                    (k_hi, k_lo, sel_k_hi, sel_k_lo, aux_k, sel_aux_k, k_mm, k_stacked))
                half = use % 2
                ps = stack_bank(b, use, stacked, 2 * b + half + 1)
                for n in range(2):
                    quad, cols = 2 * half + n, slice(n * T, (n + 1) * T)
                    mm(ps[:, cols], s_hi[:, quad, :], hi[:], True, False)
                    mm(ps[:, cols], s_lo[:, quad, :], lo[:], False, False)
                    last = mm(ps[:, cols], s_aux[:, b, :], aux[:], False, True)
                last.then_inc(done, 1)

            def scores_for_maxima(n):
                b, quad, j = n // NH, n % NH // 4, n % 4
                if n % NH == 0:
                    pe.wait_ge(q_stacked, 2 * (b + 1))
                if j == 0:
                    q = QUADS * b + quad
                    pe.wait_ge(kpad_in[q % 8], 64 * (q // 8 + 1))
                ps = banks[n % 2].take(pe, p1_read, n + 1)
                for c in range(CC):
                    last = mm(ps[:, c * T:(c + 1) * T], q_stack[b % 2][:, quad, c * P:(c + 1) * P],
                              k_pad[:, n // 4 % 8, j, :], True, True)
                last.then_inc(p1_done, 1)

            def scores_transposed(n):
                b, quad, j = n // NH, n % NH // 4, n % 4
                if n % 8 == 0:
                    pe.wait_ge(q_max_ready, n // 8 + 1)
                ps = banks[2 + n % 2].take(pe, exp_done, n + 1)
                for c in range(CC):
                    last = mm(ps[:, c * T:(c + 1) * T], k_pad[:, n // 4 % 8, j, c * P:(c + 1) * P],
                              q_stack_max[:, quad, :], True, True)
                last.then_inc(p2_done, 1)

            def values(b, quad):
                half, first = quad // 2, quad % 2 == 0
                if quad == 0:
                    pe.wait_ge(v_ready, 2 * CC * (b + 1))
                    banks[4].take(pe, o_read, b + 1)
                pe.wait_ge(exp_done, NH * b + 4 * quad + 4)
                for c in range(CC):
                    for j in range(4):
                        last = mm(bank[4][32 * j:32 * j + 32, half * T:(half + 1) * T],
                                  v_pad[b % 2][:, c, head_of(quad, j), :],
                                  probs[:, (4 * quad + j) % 8, c, :], first and c == 0, not first and c == CC - 1)
                last.then_inc(av_done, 1)

            def transpose_maxima(b):
                pe.wait_ge(negmax_ready, b + 1)
                ps = banks[5].take(pe, max_copied, b + 1)
                for c in range(CC):
                    last = nc.tensor.transpose(
                        ps[0:2 * NH, c * P:(c + 1) * P],
                        neg_max[:, c, :, :].rearrange("p k h -> p (k h)").bitcast(F32), ident[:])
                last.then_inc(max_T, 1)

            def maxima_rows(b, half):
                pe.wait_ge(max_copied, b + 1)
                ps = stack_bank(b, 4 + half, q_max_ready, 2 * b + half + 1)
                for n in range(2):
                    last = mm(ps[:, n * T:(n + 1) * T], sel_max[:, 2 * half + n, :], max_rows[:], True, True)
                last.then_inc(max_mm, 1)

            def transpose_heads(b):
                pe.wait_ge(o_read, b + 1)
                ps = banks[5].take(pe, otok_ready, b + 1)
                for c in range(CC):
                    for f in range(2):
                        last = nc.tensor.transpose(ps[:, (2 * c + f) * P:(2 * c + f + 1) * P],
                                                   o_raw[:, f, c * P:(c + 1) * P], ident[:])
                last.then_inc(o_T, 1)

            def transpose_back(b):
                pe.wait_ge(otok_ready, b + 1)
                ps = banks[5].take(pe, x1_ready, b + 1)
                for c in range(CC):
                    last = nc.tensor.transpose(ps[:, c * P:(c + 1) * P], o_tok[:, c, :], ident[:])
                last.then_inc(o_back, 1)

            def transpose_second(b):
                pe.wait_ge(xn2_ready, b + 1)
                ps = banks[5].take(pe, xT_ready, b + 1)
                for c in range(CC):
                    last = nc.tensor.transpose(ps[:, c * P:(c + 1) * P], xn_f[:, c * P:(c + 1) * P], ident[:])
                last.then_inc(xn2_T, 1)

            def router_columns():
                pe.wait_ge(simsq_ready, 1)
                ps = banks[5].take(pe, simsum_ready, 1)
                for c in range(CC):
                    last = mm(ps[:, 0:NE], ones[:], sim_sq[:, c, :], c == 0, c == CC - 1)
                last.then_inc(simsum_mm, 1)

            for t in TICKS:
                if 0 <= t + PEAK_LEAD < NH * NB:
                    scores_for_maxima(t + PEAK_LEAD)
                if 0 <= t < NH * NB:
                    scores_transposed(t)
                for quad, offset in enumerate(VALUE_PRODUCTS):
                    at(t, offset, values, quad)
                at(t, PROJECT, project)
                at(t, MAX_T, transpose_maxima)
                for use, offset in [*enumerate(STACK + MAX_ROWS), (6, VALUES_MM)]:
                    at(t, offset, project_values if use == 6 else maxima_rows if use > 3 else stack,
                       *(() if use == 6 else (use - 4,) if use > 3 else (use,)))
                at(t, HEADS_T, transpose_heads)
                at(t, HEADS_BACK, transpose_back)
                at(t, SECOND_T, transpose_second)
                if t == 4:
                    router_columns()

            pe.wait_ge(xT_ready, NB)
            pe.wait_ge(simsum_ready, 2)
            ps = banks[5].take(pe, lg_read, 1)
            for b in range(NB):
                last = split_product(ps[:, b * NE:(b + 1) * NE],
                                     [(xT_hi[:, b, c, :], xT_lo[:, b, c, :], sim_hi[:, c, :], sim_lo[:, c, :])
                                      for c in range(CC)])
            last.then_inc(routed, 1)

            for e in range(NE):
                pe.wait_ge(whi_ready, e + 1)
                pe.wait_ge(wlo_ready, e + 1)
                for b in range(NB):
                    n = NB * e + b
                    ps = banks[n % 8].take(pe, moe_read, n + 1)
                    split_product(ps[:, 0:QKV],
                                  [(xT_hi[:, b, c, :], xT_lo[:, b, c, :], w_hi[e % 2][:, c, :], w_lo[e % 2][:, c, :])
                                   for c in range(CC)]).then_inc(moe_mm, 1)

            def output_experts(b, ks):
                if ks[0] == 0:
                    pe.wait_ge(ao_ready, b + 1)
                    pe.wait_ge(slo_ready, NE)
                for k in ks:
                    n = NE // 2 * b + k
                    ps = banks[n % 2].take(pe, oproj_read, n + 1)
                    two = slice(2 * k, 2 * k + 2)
                    split_product(ps[:].rearrange("p (e c) -> p e c", e=2),
                                  [(ao_hi[:], ao_lo[:], o_hi[:, two, :], o_lo[:, two, :])]).then_inc(oproj_mm, 1)

            def transposes(ps, parts, done):
                for n, part in enumerate(parts):
                    last = nc.tensor.transpose(ps[:, n * P:(n + 1) * P], part, ident[:])
                last.then_inc(done, 1)

            def last_experts(b):
                pe.wait_ge(combT_ready, b + 1)
                ps = banks[7].take(pe, acc4_ready, b + 1)
                mm(ps[:, 0:T], combT[:], b1_sb[:], True, True).then_inc(bias_mm, 1)
                for k in range(NE1 // 2):
                    n = NE1 // 2 * b + k
                    ps = banks[2 + n % 2].take(pe, l1_read, n + 1)
                    two = slice(2 * k, 2 * k + 2)
                    split_product(ps[:].rearrange("p (e c) -> p e c", e=2),
                                  [(x1_hi[:, c, :], x1_lo[:, c, :], w1_hi[:, c, two, :], w1_lo[:, c, two, :])
                                   for c in range(CC)]).then_inc(l1_mm, 1)

            for att, proj, wkv, last in TAIL:
                if last is not None:
                    pe.wait_ge(xn4_ready, last + 1)
                    transposes(banks[7].take(pe, x4_split, last + 1), [xn_1[:, c * P:(c + 1) * P] for c in range(CC)],
                               xn4_T)
                if wkv is not None:
                    pe.wait_ge(kn_ready, wkv + 1)
                    transposes(banks[6].take(pe, kT_ready, wkv + 1), [kn[:, c * P:(c + 1) * P] for c in range(CC)],
                               kn_T)
                if att is not None:
                    pe.wait_ge(moe_read, NB * (NE - 1) + att + 1)
                    transposes(banks[4].take(pe, qkT_ready, att + 1), [qkv[:, att, n * P:(n + 1) * P] for n in range(2)],
                               qk_T)
                if proj is not None:
                    output_experts(proj, (0, 1))
                if last is not None:
                    pe.wait_ge(x4_split, last + 1)
                    ps = banks[7].take(pe, nm4_ready, last + 1)
                    split_product(ps[:, 0:NE1], [(x1_hi[:, c, :], x1_lo[:, c, :], wg_hi[:, c, :], wg_lo[:, c, :])
                                                 for c in range(CC)]).then_inc(lg4_mm, 1)
                if att is not None:
                    pe.wait_ge(qkT_ready, att + 1)
                    ps = banks[5].take(pe, scr_ready, att + 1)
                    mm(ps[:, 0:P], qkT[:, 0, :], qkT[:, 1, :], True, True).then_inc(scored, 1)
                if proj is not None:
                    output_experts(proj, (2, 3, 4))
                if att is not None:
                    pe.wait_ge(pat_ready, att + 1)
                    transposes(banks[5].take(pe, patT_ready, att + 1), [pat[:]], pat_T)
                if last is not None:
                    pe.wait_ge(comb_ready, last + 1)
                    ps = banks[7].take(pe, combT_ready, last + 1)
                    nc.tensor.transpose(ps[0:NE1, 0:P], comb[:], ident[:]).then_inc(comb_T, 1)
                if proj is not None:
                    output_experts(proj, (5, 6, 7))
                if att is not None:
                    pe.wait_ge(patT_ready, att + 1)
                    ps = banks[4].take(pe, ao_ready, att + 1)
                    mm(ps[:, 0:P], qkv[:, att, 2 * HID:3 * HID], patT[:], True, True).then_inc(ao_mm, 1)
                if last is not None:
                    last_experts(last)
                if wkv is not None:
                    pe.wait_ge(y_ready, wkv + 1)
                    transposes(banks[6].take(pe, x3_ready, wkv + 1), [yT[:, c, :] for c in range(CC)], y_T)


_OUT = ((8, 128, 256), "float32")


def kernel(**inputs):
    import numpy as _np
    import concourse.bacc as _bacc
    from concourse import mybir as _mybir
    from concourse.bass_utils import run_bass_kernel_spmd as _run

    a = {k: _np.asarray(v) for k, v in inputs.items()}
    nb = a["x"].shape[0]
    laid = {
        "x": a["x"],
        "ctx": a["ctx_2048"],
        "ctxT": a["ctx_2048"].transpose(2, 0, 1),
        "mask": a["mask_Bx1x2048_fk1"].reshape(nb, -1),
        "maskT": a["mask_Bx1x2048_fk1"].reshape(nb, -1).T,
        "g_xattn": a["g_xattn"],
        "g_ffn": a["g_ffn"],
        "wqT": a["L0_xattn_Wq"].T,
        "wkT": a["L0_xattn_Wk"].T,
        "wvT": a["L0_xattn_Wv"].T,
        "bq": a["L0_xattn_bq"].reshape(-1, 1),
        "bk": a["L0_xattn_bk"].reshape(-1, 1),
        "bv": a["L0_xattn_bv"].reshape(1, -1),
        "sim": a["L0_ffn_sim_matrix"],
        "gates": a["L0_ffn_gates"],
        "wqkv": _np.concatenate([a["L0_ffn_q_proj"], a["L0_ffn_k_proj"], a["L0_ffn_v_proj"]], axis=2),
        "wo": a["L0_ffn_o_proj"],
        "wkv_w": a["L1_xattn_w"].reshape(-1, 128).T,
        "wkv_u": a["L1_xattn_u"].reshape(-1, 128).T,
        "wg": a["L1_ffn_wg"],
        "w1T": a["L1_ffn_W"].transpose(0, 2, 1),
        "b1": a["L1_ffn_b"],
    }
    nc = _bacc.Bacc("TRN2", target_bir_lowering=False, num_devices=1)
    arrays, args = {}, []
    for name, value in laid.items():
        value = _np.ascontiguousarray(value)
        arrays[f"in_{name}_dram"] = value
        args.append(nc.dram_tensor(f"in_{name}_dram", value.shape, _mybir.dt.from_np(value.dtype),
                                   kind="ExternalInput").ap())
    args.append(nc.dram_tensor("out_dram", _OUT[0], _mybir.dt.from_np(_np.dtype(_OUT[1])),
                               kind="ExternalOutput").ap())
    flamingo_two_layers(nc, *args)
    r = _run(nc, [arrays], core_ids=[0])
    return r.results[0]["out_dram"]
```

```python
from contextlib import ExitStack

import concourse.bass as bass
from concourse import mybir

ALU = mybir.AluOpType
ACT = mybir.ActivationFunctionType
AX = mybir.AxisListType
F32 = mybir.dt.float32
F32R = mybir.dt.float32r
U32 = mybir.dt.uint32

P = 128
NH = 16
HD = P // NH
QUADS = NH // 4
NEG_MASK = 1.0e6
NEG_CAUSAL = 1.0e9
NEG_START = -1.0e38
EPS = 1.0e-5


def head_of(quad, j):
    return 8 * (quad // 2) + 2 * j + quad % 2


class Tally:

    def __init__(self, sem):
        self.sem, self.n = sem, 0

    def step(self, instruction):
        instruction.then_inc(self.sem, 1)
        self.n += 1
        return self.n


class Bank:

    def __init__(self, psum):
        self.psum, self.reader = psum, None

    def take(self, engine, sem, value):
        if self.reader is not None:
            engine.wait_ge(*self.reader)
        self.reader = (sem, value)
        return self.psum


def flamingo_two_layers(nc, x, ctx, ctxT, mask, maskT, g_xattn, g_ffn, wqT, wkT, wvT, bq, bk, bv, sim, gates,
                        wqkv, wo, wkv_w, wkv_u, wg, w1c, b1, out):
    NB, _, T = x.shape
    CC = T // P
    NE = wqkv.shape[0]
    QKV = wqkv.shape[2]
    HID = QKV // 3
    NE1 = w1c.shape[0] // CC
    XATTN_SCALE = float(HD) ** -0.5
    FFN_SCALE = float(HID) ** -0.5

    es = ExitStack()
    with es:
        def sb(name, shape, dt=F32):
            return es.enter_context(nc.sbuf_tensor(name, shape, dt))

        def sem(name):
            return es.enter_context(nc.semaphore(name))

        x_sb = sb("x_sb", [P, NB, T])
        mask_bc = sb("mask_bc", [P, NB, T])
        mask_col = sb("mask_col", [P, CC, NB])
        ctx_b = [sb(f"ctx_b{i}", [P, T]) for i in range(2)]
        ctxT_sb = sb("ctxT_sb", [P, CC, NB, P])
        wqT_sb, wkT_sb, wvT_sb = (sb(n, [P, P]) for n in ("wqT_sb", "wkT_sb", "wvT_sb"))
        bq_sb, bk_sb = sb("bq_sb", [P, 1]), sb("bk_sb", [P, 1])
        bv_sb = sb("bv_sb", [1, P])
        gx_sb, gf_sb = sb("gx_sb", [P, 2]), sb("gf_sb", [P, 2])
        tgx, tgf = sb("tgx", [P, 2]), sb("tgf", [P, 2])
        sim_sb = sb("sim_sb", [P, CC, NE])
        gates_sb = sb("gates_sb", [P, NE])
        wg_sb = sb("wg_sb", [P, CC, NE1])
        b1_sb = sb("b1_sb", [NE1, T])
        w_sb, u_sb = sb("w_sb", [P, CC]), sb("u_sb", [P, CC])
        ident = sb("ident", [P, P])
        ones = sb("ones", [P, P])
        zeros = sb("zeros", [P, P])
        minus_half = sb("minus_half", [P, NE])
        iota_e = sb("iota_e", [P, NE])
        causal = sb("causal", [P, P])
        causal_neg = sb("causal_neg", [P, P])
        arena = sb("arena", [P, 8 * QUADS * T], F32R)
        sel_q_hi, sel_q_lo, sel_k_hi, sel_k_lo = (
            arena[:, n * QUADS * P:(n + 1) * QUADS * P].rearrange("p (q n) -> p q n", q=QUADS) for n in range(4))
        sel_aux_q, sel_aux_k = (
            arena[:, (2 + n) * NB * P:(3 + n) * NB * P].rearrange("p (b n) -> p b n", b=NB) for n in range(2))
        q_stack0, q_stack1, q_stack_max, k_stack = (
            arena[:, (4 + n) * QUADS * T:(5 + n) * QUADS * T].rearrange("p (q t) -> p q t", q=QUADS)
            for n in range(4))
        q_stack = [q_stack0, q_stack1]
        sel_max = sb("sel_max", [2 * NH, QUADS, P], F32R)
        row_q, row_k = sb("row_q", [P, P]), sb("row_k", [P, P])
        batch_row = sb("batch_row", [P, NB])
        mask8 = sb("mask8", [P, T])
        aux_f = sb("aux_f", [P, 2, T])
        aux_q, aux_k = sb("aux_q", [P, T], F32R), sb("aux_k", [P, T], F32R)
        bn6 = sb("bn6", [P, NB, 6])
        mv = sb("mv", [P, NB, 2])
        var_eps, rstd = sb("var_eps", [P, NB]), sb("rstd", [P, NB])
        xn = sb("xn", [P, T])
        q_f, k_f = sb("q_f", [P, T]), sb("k_f", [P, T])
        q_hi, q_lo, k_hi, k_lo = (sb(n, [P, T], F32R) for n in ("q_hi", "q_lo", "k_hi", "k_lo"))
        k_pad = sb("k_pad", [P, 2 * QUADS, 4, T], F32R)
        v_pad = [sb(f"v_pad{i}", [P, CC, NH, 32]) for i in range(2)]
        mx = sb("mx", [P, CC, NH])
        neg_max = sb("neg_max", [P, CC, 2, NH], F32R)
        max_rows = sb("max_rows", [2 * NH, T], F32R)
        probs = sb("probs", [P, 8, CC, T])
        o_raw = sb("o_raw", [P, 2, T])
        o_den = sb("o_den", [P, CC, 2 * NH // 2])
        o_tok = sb("o_tok", [P, CC, P])
        bn6f, mvf = sb("bn6f", [P, 6]), sb("mvf", [P, 2])
        vef, rstdf = sb("vef", [P, 1]), sb("rstdf", [P, 1])
        xn_f = sb("xn_f", [P, T])
        sq_junk = sb("sq_junk", [P, T])
        nsq, rnorm = sb("nsq", [P, NB]), sb("rnorm", [P, NB])
        xT_hi, xT_lo = (sb(n, [P, NB, CC, P], F32R) for n in ("xT_hi", "xT_lo"))
        simn = sb("simn", [P, CC, NE])
        sim_sq = sb("sim_sq", [P, CC, NE])
        sim_r = sb("sim_r", [P, NE])
        sim_parts = sb("sim_parts", [P, CC, 2, NE], F32R)
        sgate = sb("sgate", [P, NE])
        lg, gated, pos, fb = (sb(n, [P, NB, NE]) for n in ("lg", "gated", "pos", "fb"))
        top8, topi_f = sb("top8", [P, NB, 8]), sb("topi_f", [P, NB, 8])
        topi = sb("topi", [P, NB, 8], U32)
        inact, gmax, esum, ersum = (sb(n, [P, NB]) for n in ("inact", "gmax", "esum", "ersum"))
        w_e, w_et = sb("w_e", [P, NB, NE]), sb("w_et", [P, NB, NE])
        w_raw, w_hi, w_lo = ([sb(f"{n}{i}", [P, CC, QKV], d) for i in range(2)]
                             for n, d in (("w_raw", F32), ("w_hi", F32R), ("w_lo", F32R)))
        s_raw = [sb(f"s_raw{i}", [P, 2 * T]) for i in range(2)]
        qkv = probs[:].rearrange("p s c t -> p (s c t)")[:, 0:NB * QKV].rearrange("p (b n) -> p b n", b=NB)
        o_hi, o_lo = (k_pad[:, n * QUADS:(n + 1) * QUADS].rearrange("p q j t -> p (q j) t")
                      for n in range(2))
        w1_hi, w1_lo = (arena[:, n * CC * NE1 * T:(n + 1) * CC * NE1 * T].rearrange("p (c e t) -> p c e t", c=CC, e=NE1)
                        for n in range(2))
        qkT = sb("qkT", [P, 2, P])
        scr, pat, patT = sb("scr", [P, P]), sb("pat", [P, P]), sb("patT", [P, P])
        row_m, row_nm, row_s, row_r = (sb(n, [P, 1]) for n in ("row_m", "row_nm", "row_s", "row_r"))
        ao_f = sb("ao_f", [P, P])
        w_parts = sb("w_parts", [P, NB, 2, NE], F32R)
        wT = sb("wT", [2 * NE, NB * P], F32R)
        wa_f = [v.rearrange("p c h n -> p (c h n)") for v in (v_pad[0][:], v_pad[1][:])]
        wa_hi, wa_lo = (t[:].rearrange("p b c t -> p (b c t)") for t in (xT_hi, xT_lo))
        GROUP = 4
        GROUPS = NE // GROUP

        def weight_rows(e):
            if e < 4:
                return (aux_q, aux_k)[e // 2][0:2 * NE, e % 2 * P:(e % 2 + 1) * P]
            if e < 8:
                return sel_max[:, e - 4, :]
            return (q_hi, q_lo, k_hi, k_lo)[e // 2 - 4][0:2 * NE, e % 2 * P:(e % 2 + 1) * P]

        w_full = sb("w_full", [P, CC, P])
        kn = ctx_b[0]
        kT = sb("kT", [P, CC, P])
        o_ext = sb("o_ext", [P, CC, P + 1])
        uk, no = sb("uk", [P, CC, P]), sb("no", [P, CC, P])
        arg1, arg2, e1, e2 = (mask_bc[:, 2 * n:2 * n + 2, :] for n in range(4))
        ev, e2v = sb("ev", [P, T]), sb("e2v", [P, T])
        pq = sb("pq", [P, 2, T + 1])
        num, den, yT = ctx_b[1], xn, sb("yT", [P, CC, P])
        xn_1 = sb("xn_1", [P, T])
        x1_hi, x1_lo = sb("x1_hi", [P, CC, P], F32R), sb("x1_lo", [P, CC, P], F32R)
        wg_parts = sb("wg_parts", [P, CC, 2, NE1], F32R)
        lg1, ex1, comb = sb("lg1", [P, NE1]), sb("ex1", [P, NE1]), sb("comb", [P, NE1])
        m8, i8f = sb("m8", [P, 8]), sb("i8f", [P, 8])
        i8 = sb("i8", [P, 8], U32)
        nm1, s1, r1 = sb("nm1", [P, 1]), sb("s1", [P, 1]), sb("r1", [P, 1])
        combT = sb("combT", [NE1, P])
        odd_out = [q_f, k_f, sq_junk, xn_f]
        bias_term = o_raw[:, 0, :]
        odd_sum = o_tok[:].rearrange("p c t -> p (c t)")

        bank = [es.enter_context(nc.psum_tensor(f"bank{i}", [P, 512], F32)) for i in range(8)]

        ld_x0, ld_x, ld_mask0, ld_mask, ld_mask8, ld_wts, ld_values, ld_small, ld_late = (
            sem(n) for n in ("ld_x0", "ld_x", "ld_mask0", "ld_mask", "ld_mask8", "ld_wts", "ld_values", "ld_small",
                             "ld_late"))
        xThi_ready = sem("xThi_ready")
        mask8_clear, sel_clear, ident_ready, kpad_clear, wq_scaled = (
            sem(n) for n in ("mask8_clear", "sel_clear", "ident_ready", "kpad_clear", "wq_scaled"))
        ctx_in = [sem("ctx_in0"), sem("ctx_in1")]
        kpad_in = [sem(f"kpad_in{i}") for i in range(2 * QUADS)]
        w_in, s_in = [sem("w_in0"), sem("w_in1")], [sem("s_in0"), sem("s_in1")]
        out_done = sem("out_done")
        consts, dve, pool, setup_done, tanh_done = (sem(n) for n in ("consts", "dve", "pool", "setup_done", "tanh_done"))
        vef_ready, rstd_ready, xn_ready, qk_mm, v_mm = (
            sem(n) for n in ("vef_ready", "rstd_ready", "xn_ready", "qk_mm", "v_mm"))
        kf_ready, qk_split, v_ready, q_mm, k_mm, q_stacked, k_stacked = (
            sem(n) for n in ("kf_ready", "qk_split", "v_ready", "q_mm", "k_mm", "q_stacked", "k_stacked"))
        p1_done, p1_read, negmax_ready, max_T, max_copied, max_mm, q_max_ready = (
            sem(n) for n in ("p1_done", "p1_read", "negmax_ready", "max_T", "max_copied", "max_mm", "q_max_ready"))
        p2_done, exp_done, av_done, o_read, o_T, otok_ready, o_back, x1_ready = (
            sem(n) for n in ("p2_done", "exp_done", "av_done", "o_read", "o_T", "otok_ready", "o_back", "x1_ready"))
        ve2_ready, rstd2_ready, xn2_ready, xn2_T, xT_ready, sq_done = (
            sem(n) for n in ("ve2_ready", "rstd2_ready", "xn2_ready", "xn2_T", "xT_ready", "sq_done"))
        simsq_ready, simsum_mm, simsum_ready, simr_ready, sg_exp = (
            sem(n) for n in ("simsq_ready", "simsum_mm", "simsum_ready", "simr_ready", "sg_exp"))
        routed, nsq_ready, rnorm_ready, gated_ready, exp_w, lg_read = (
            sem(n) for n in ("routed", "nsq_ready", "rnorm_ready", "gated_ready", "exp_w", "lg_read"))
        whi_ready, wlo_ready, shi_ready, slo_ready, moe_mm, moe_read = (
            sem(n) for n in ("whi_ready", "wlo_ready", "shi_ready", "slo_ready", "moe_mm", "moe_read"))
        qk_T, qkT_ready, scored, scr_ready, pat_exp, pat_ready, pat_T, patT_ready, ao_mm, ao_ready = (
            sem(n) for n in ("qk_T", "qkT_ready", "scored", "scr_ready", "pat_exp", "pat_ready", "pat_T",
                             "patT_ready", "ao_mm", "ao_ready"))
        wparts_ready, wparts_T, wT_ready, rows_ready, wb_mm, wa_ready, wahi_ready, walo_ready = (
            sem(n) for n in ("wparts_ready", "wparts_T", "wT_ready", "rows_ready", "wb_mm", "wa_ready", "wahi_ready",
                             "walo_ready"))
        oproj_mm, x2_ready, ve3_ready, rstd3_ready, kn_ready, kn_T, kT_ready, uk_ready = (
            sem(n) for n in ("oproj_mm", "x2_ready", "ve3_ready", "rstd3_ready", "kn_ready", "kn_T", "kT_ready",
                             "uk_ready"))
        den_ready = sem("den_ready")
        sums_ready, num_ready, x4hi_ready, odd_ready, odd_added = (
            sem(n) for n in ("sums_ready", "num_ready", "x4hi_ready", "odd_ready", "odd_added"))
        arg1_ready, e1_ready, arg2_ready, e2_ready, ev_ready, e2v_ready, y_ready, y_T, x3_ready = (
            sem(n) for n in ("arg1_ready", "e1_ready", "arg2_ready", "e2_ready", "ev_ready", "e2v_ready", "y_ready",
                             "y_T", "x3_ready"))
        ve4_ready, rstd4_ready, xn4_ready, xn4_T, x4_split, lg4_mm, nm4_ready, ex4_ready, comb_ready = (
            sem(n) for n in ("ve4_ready", "rstd4_ready", "xn4_ready", "xn4_T", "x4_split", "lg4_mm", "nm4_ready",
                             "ex4_ready", "comb_ready"))
        comb_T, combT_ready, bias_mm, bias_ready, l1_mm, l1_even, xout_ready = (
            sem(n) for n in ("comb_T", "combT_ready", "bias_mm", "bias_ready", "l1_mm", "l1_even", "xout_ready"))

        block = es.enter_context(nc.Block())

        PEAK_LEAD = 21
        NORMALISE, PROJECT, SPLIT = -36, -34, -34
        STACK = (-31, -27, -32, -30)
        NEGATE, MAX_T, MAX_ROWS = -5, -5, (-4, -2)
        VALUES_MM, VALUES_SPREAD = -13, -11
        VALUE_PRODUCTS = (7, 11, 15, 15)
        HEADS_OUT, HEADS_T, HEADS_NORM, HEADS_BACK, ADD = 15, 19, 21, 24, 26
        NORMALISE2, SECOND_T, SPLIT2 = 27, 28, 28
        ROUTER, ROUTER_READ = 33, 34
        TICKS = range(NORMALISE, NH * (NB - 1) + ROUTER_READ + 1)

        def at(t, offset, work, *args):
            b, rest = divmod(t - offset, NH)
            if rest == 0 and 0 <= b < NB:
                work(b, *args)

        ROUTED = (slice(0, NB - 2), slice(NB - 2, NB))
        ROUTE, FIRST_PRODUCTS, FIRST_WEIGHED = 119, 125, 129
        QKV_ORDER = [(e, b) for part in ROUTED for e in range(2) for b in range(part.start, part.stop)]
        EARLY = 2 * (NB - 2)
        QKV_ORDER += [(e, b) for e in range(2, NE - 2) for b in range(NB)]
        QKV_ORDER += [(e, b) for b in range(NB) for e in (NE - 2, NE - 1)]
        QKV_AT = {pair: n for n, pair in enumerate(QKV_ORDER)}

        def qkv_bank(n):
            return (0, 1, 6, 7, 2, 3, 4)[n % 7] if n < 2 * NB else (2, 3, 6, 7)[n % 4]

        RING = (5, 6, 7, 2, 3, 4, 0, 1)

        def last_qkv(t, work):
            m, rest = divmod(t - LAST_QKV, LAST_QKV_STEP)
            if rest == 0 and 0 <= m < 2 * NB:
                work(QKV_AT[(NE - 2, 0)] + m)

        def products_with(e):
            return QKV_AT[(e, NB - 1)] + 1

        WARMING = 15
        V_PAD_MADE, CONSTS = 8, 12

        TAIL_PERIOD = 20
        QK_T, SCORES, ROWS, PAT_T, AO = 1, 6, 7, 9, 10
        WEIGHTS = (8, 9, 17, 17)
        WEIGHTED = (11, 14, 15, 21)
        OUTPUTS = (21, 27, 29, 35)
        ADD_OUTPUT, KEYS, KEYS_T, EXPONENTS = 32, 34, 38, 43
        SUMS, QUOTIENT, Y_T, ADD_WKV, NORMALISE4 = 46, 49, 54, 51, 52
        XN4_T, SPLIT4, LOGITS, GATE, COMBINE, COMB_T, BIAS = 56, 54, 59, 61, 65, 66, 70
        LAST = (64, 64, 71, 75)
        LAST_READ, LAST_OUT = (68, 69, 72, 79), 84
        LAST_QKV, LAST_QKV_STEP = -9, 2
        TAIL_TICKS = range(LAST_QKV, TAIL_PERIOD * (NB - 1) + LAST_OUT + 1)

        def tail_at(t, offset, work, *args):
            b, rest = divmod(t - offset, TAIL_PERIOD)
            if rest == 0 and 0 <= b < NB:
                work(b, *args)

        ST_PARITY = {}
        for t in TICKS:
            for use, offset in [*enumerate(STACK + MAX_ROWS), (6, VALUES_MM)]:
                at(t, offset, lambda b, u: ST_PARITY.setdefault((b, u), len(ST_PARITY) % 2), use)

        def st_bank(b, use):
            return bank[6 + ST_PARITY[(b, use)]][:]

        def side_part(n):
            if n % 2 == 0:
                k = n // 2
                return (o_hi[:, 2 * k:2 * k + 2, :], o_lo[:, 2 * k:2 * k + 2, :],
                        wo[2 * k:2 * k + 2].rearrange("e h c -> h e c"))
            k = n // 2
            hi, lo = (t.rearrange("p c e t -> p (c e) t")[:, 2 * k:2 * k + 2, :] for t in (w1_hi, w1_lo))
            return hi, lo, w1c[2 * k:2 * k + 2].rearrange("e h o -> h e o")

        def side_of(i, odd):
            if odd:
                hi, lo = (t.rearrange("p c e t -> p (c e) t")[:, bass.ds(i * 2, 2), :] for t in (w1_hi, w1_lo))
                return hi, lo, w1c[bass.ds(i * 2, 2)].rearrange("e h o -> h e o")
            return (o_hi[:, bass.ds(i * 2, 2), :], o_lo[:, bass.ds(i * 2, 2), :],
                    wo[bass.ds(i * 2, 2)].rearrange("e h c -> h e c"))

        def pairs(tile):
            return tile.rearrange("p (e c) -> p e c", e=2)

        @block.sync
        def _(sp):
            def load_side(n):
                sp.dma_start(pairs(s_raw[n % 2][:]), side_part(n)[2]).then_inc(s_in[n % 2], 16)

            def load_expert(e):
                sp.dma_start(w_raw[e % 2][:], wqkv[e].rearrange("(c p) n -> p c n", p=P)).then_inc(w_in[e % 2], 16)

            sp.dma_start(x_sb[:, 0, :], x[0]).then_inc(ld_x0, 16)
            for dst, src in ((wqT_sb, wqT), (wkT_sb, wkT)):
                sp.dma_start(dst[:], src).then_inc(ld_wts, 16)
            sp.dma_start(ctx_b[0][:], ctx[0]).then_inc(ctx_in[0], 16)
            for dst, src in ((bq_sb, bq), (bk_sb, bk)):
                sp.dma_start(dst[:], src).then_inc(ld_wts, 16)
            sp.dma_start(mask_bc[:, 0, :], mask[0].partition_broadcast(P)).then_inc(ld_mask0, 16)
            sp.wait_ge(mask8_clear, 1)
            for s in range(4):
                sp.dma_start(mask8[32 * s:32 * s + NB, :], mask).then_inc(ld_mask8, 16)
            sp.dma_start(x_sb[:, 1:NB, :], x[1:NB].rearrange("b p t -> p b t")).then_inc(ld_x, 16)
            sp.dma_start(mask_bc[:, 1:NB, :], mask[1:NB].partition_broadcast(P)).then_inc(ld_mask, 16)
            sp.dma_start(mask_col[:], maskT.rearrange("(c p) b -> p c b", p=P)).then_inc(ld_mask, 16)
            for dst, src in ((wvT_sb, wvT), (bv_sb, bv)):
                sp.dma_start(dst[:], src).then_inc(ld_values, 16)
            for dst, src in ((gx_sb[:], g_xattn.partition_broadcast(P)), (gf_sb[:], g_ffn.partition_broadcast(P)),
                             (gates_sb[:], gates.partition_broadcast(P)),
                             (sim_sb[:], sim.rearrange("(c p) e -> p c e", p=P))):
                sp.dma_start(dst, src).then_inc(ld_small, 16)
            sp.dma_start(ctx_b[1][:], ctx[1]).then_inc(ctx_in[1], 16)
            for dst, src in ((wg_sb[:], wg.rearrange("(c p) e -> p c e", p=P)), (b1_sb[:], b1),
                             (w_sb[:], wkv_w),
                             (u_sb[:], wkv_u),
                             (ctxT_sb[:], ctxT.rearrange("(c p) b t -> p c b t", p=P))):
                sp.dma_start(dst, src).then_inc(ld_late, 16)
            for n in range(2):
                load_expert(n)
                load_side(n)
            for b in range(NB):
                for quad in range(QUADS):
                    n = QUADS * b + quad
                    sp.wait_ge(k_stacked, 2 * b + quad // 2 + 1)
                    if n >= 8:
                        sp.wait_ge(p2_done, 4 * (n - 7))
                    else:
                        sp.wait_ge(kpad_clear, n // QUADS + 1)
                    for j in range(4):
                        sp.dma_start(k_pad[32 * j:32 * j + 32, n % 8, j, :].bitcast(F32),
                                     k_stack[32 * j:32 * j + 32, quad, :].bitcast(F32)).then_inc(kpad_in[n % 8], 16)
                if b + 2 < NB:
                    sp.wait_ge(v_mm, b + 1)
                    sp.dma_start(ctx_b[b % 2][:], ctx[b + 2]).then_inc(ctx_in[b % 2], 16)
            def wait_split(hi, lo, value):
                sp.wait_ge(hi, value)
                sp.wait_ge(lo, value)

            for e in range(2, 4):
                wait_split(whi_ready, wlo_ready, e - 1)
                load_expert(e)
            wait_split(shi_ready, slo_ready, 1)
            load_side(2)
            with sp.Fori(2, NE // 2) as i:
                for odd in range(2):
                    wait_split(whi_ready, wlo_ready, i * 2 + odd - 1)
                    sp.dma_start(w_raw[odd][:], wqkv[bass.ds(i * 2 + odd, 1)].rearrange("e (c p) n -> p (e c) n", p=P)
                                 ).then_inc(w_in[odd], 16)
                    wait_split(shi_ready, slo_ready, i * 2 + odd - 2)
                    sp.dma_start(pairs(s_raw[1 - odd][:]), side_of(i - 1 + odd, 1 - odd)[2]).then_inc(s_in[1 - odd], 16)
            wait_split(shi_ready, slo_ready, NE - 2)
            load_side(NE - 1)
            for b in range(NB):
                sp.wait_ge(xout_ready, b + 1)
                sp.dma_start(out[b], x_sb[:, b, :]).then_inc(out_done, 16)
            sp.wait_ge(out_done, 16 * NB)

        @block.gpsimd
        def _(eng):
            g = nc.gpsimd
            made = Tally(consts)
            g.memset(mask8[:], 0.0).then_inc(mask8_clear, 1)
            made.step(g.memset(ones[:], 1.0))
            made.step(g.memset(minus_half[:], -0.5))
            eng.wait_ge(consts, made.n)
            g.affine_select(out=ident[:], in_=ones[:], compare_op=ALU.is_equal, fill=0.0, base=0,
                            pattern=[[-1, P]], channel_multiplier=1).then_inc(ident_ready, 1)
            for t in (arena[:, 0:4 * QUADS * P].bitcast(F32), row_q[:], row_k[:]):
                g.memset(t, 0.0).then_inc(sel_clear, 1)
            eng.wait_ge(vef_ready, 1)
            g.tensor_tensor(rstd[:, 0:1], var_eps[:, 0:1], minus_half[:, 0:1], ALU.pow).then_inc(rstd_ready, 1)
            for i in range(2):
                g.memset(k_pad[:, QUADS * i:QUADS * (i + 1)].bitcast(F32), 0.0).then_inc(kpad_clear, 1)
            for i in range(2):
                made.step(g.memset(v_pad[i][:], 0.0))
            eng.wait_ge(consts, made.n)
            for i in range(2):
                by_pair = v_pad[i][:].rearrange("p c (g i) n -> p (c g) i n", i=2)
                for k in range(2):
                    made.step(g.memset(by_pair[:, :, k, 16 + k:17 + k], 1.0))
            eng.wait_ge(vef_ready, 2)
            g.tensor_tensor(rstd[:, 1:NB], var_eps[:, 1:NB], minus_half[:, 1:NB], ALU.pow).then_inc(rstd_ready, 1)
            made.step(g.memset(zeros[:], 0.0))
            made.step(g.iota(iota_e[:], pattern=[[1, NE]], base=0, channel_multiplier=0,
                             allow_small_or_imprecise_dtypes=True))
            eng.wait_ge(consts, made.n)
            made.step(g.affine_select(out=causal[:], in_=ones[:], compare_op=ALU.is_ge, fill=0.0, base=0,
                                      pattern=[[-1, P]], channel_multiplier=1))
            made.step(g.affine_select(out=causal_neg[:], in_=zeros[:], compare_op=ALU.is_ge, fill=-NEG_CAUSAL,
                                      base=0, pattern=[[-1, P]], channel_multiplier=1))
            assert made.n == CONSTS
            eng.wait_ge(simsum_ready, 1)
            g.tensor_tensor(sim_r[:], sim_sq[:, 0, :], minus_half[:], ALU.pow).then_inc(simr_ready, 1)

            def expert_lo(e):
                eng.wait_ge(w_in[e % 2], 16 * (e // 2 + 1))
                eng.wait_ge(whi_ready, e + 1)
                if e >= 2:
                    eng.wait_ge(moe_mm, products_with(e - 2))
                g.tensor_tensor(w_lo[e % 2][:], w_raw[e % 2][:], w_hi[e % 2][:].bitcast(F32),
                                ALU.subtract).then_inc(wlo_ready, 1)

            def side_lo(n):
                eng.wait_ge(s_in[n % 2], 16 * (n // 2 + 1))
                eng.wait_ge(shi_ready, n + 1)
                hi, lo, _ = side_part(n)
                g.tensor_tensor(lo, pairs(s_raw[n % 2][:]), hi.bitcast(F32), ALU.subtract).then_inc(slo_ready, 1)

            def second_root(b):
                eng.wait_ge(ve2_ready, b + 1)
                g.tensor_tensor(rstdf[:], vef[:], minus_half[:, 0:1], ALU.pow).then_inc(rstd2_ready, 1)

            for e in range(2):
                expert_lo(e)
            def norms(part):
                eng.wait_ge(nsq_ready, part + 1)
                rows = ROUTED[part]
                g.tensor_tensor(rnorm[:, rows], nsq[:, rows], minus_half[:, rows], ALU.pow).then_inc(rnorm_ready, 1)

            for t in TICKS:
                at(t, ADD, second_root)
                if t == ROUTE:
                    norms(0)
            norms(1)
            for e in range(4):
                if e >= 2:
                    expert_lo(e)
                side_lo(e)
            with eng.Fori(2, NE // 2) as i:
                for odd in range(2):
                    eng.wait_ge(w_in[odd], i * 16 + 16)
                    eng.wait_ge(whi_ready, i * 2 + odd + 1)
                    eng.wait_ge(moe_mm, i * (2 * NB) + NB * (odd - 1))
                    g.tensor_tensor(w_lo[odd][:], w_raw[odd][:], w_hi[odd][:].bitcast(F32),
                                    ALU.subtract).then_inc(wlo_ready, 1)
                    eng.wait_ge(s_in[odd], i * 16 + 16)
                    eng.wait_ge(shi_ready, i * 2 + odd + 1)
                    hi, lo, _ = side_of(i, odd)
                    g.tensor_tensor(lo, pairs(s_raw[odd][:]), hi.bitcast(F32), ALU.subtract).then_inc(slo_ready, 1)

            def weighted_lo(b, group):
                n = GROUPS * b + group
                cols = slice(group * GROUP * P, (group + 1) * GROUP * P)
                eng.wait_ge(wahi_ready, n + 1)
                if b >= 1:
                    eng.wait_ge(oproj_mm, n - GROUPS + 1)
                else:
                    eng.wait_ge(moe_mm, QKV_AT[(NE - 1, 2 * group + 1)] + 1)
                g.tensor_tensor(wa_lo[:, cols], wa_f[group // 2][:, group % 2 * GROUP * P:(group % 2 + 1) * GROUP * P],
                                wa_hi[:, cols].bitcast(F32), ALU.subtract).then_inc(walo_ready, 1)

            def root(b, col, ve, ready):
                eng.wait_ge(ve, b + 1)
                g.tensor_tensor(rstd[:, col:col + 1], var_eps[:, col:col + 1], minus_half[:, 0:1],
                                ALU.pow).then_inc(ready, 1)

            def times_values(b, exponentials, ready, dst, done, free):
                eng.wait_ge(ready, b + 1)
                if b >= 1 and free is not None:
                    eng.wait_ge(free, 2 * b - 1)
                g.tensor_tensor(dst[:].rearrange("p (c t) -> p c t", c=CC),
                                exponentials[:, 1, :].rearrange("p (c t) -> p c t", c=CC), ctxT_sb[:, :, b, :],
                                ALU.mult).then_inc(done, 1)

            def numerator(b):
                eng.wait_ge(sums_ready, 2 * b + 1)
                if b >= 1:
                    eng.wait_ge(y_ready, b)
                eng.wait_ge(sums_ready, 2 * b + 2)
                g.tensor_tensor(den[:], e1[:, 0, :], pq[:, 1, 0:T], ALU.mult).then_inc(den_ready, 1)
                g.tensor_tensor(num[:], e1[:, 0, :], pq[:, 0, 0:T], ALU.mult).then_inc(pool, 1)
                eng.wait_ge(pool, b + 1)
                eng.wait_ge(ev_ready, b + 1)
                g.tensor_tensor(num[:], num[:], ev[:], ALU.add).then_inc(num_ready, 1)

            def add_odd(b, k):
                eng.wait_ge(odd_ready, NE1 // 2 * b + k + 1)
                if k == 0:
                    eng.wait_ge(bias_ready, b + 1)
                    if b >= 1:
                        eng.wait_ge(xout_ready, b)
                    first = bias_term
                else:
                    first = odd_sum
                    eng.wait_ge(odd_added, NE1 // 2 * b + k)
                g.tensor_tensor(odd_sum, first, odd_out[k][:], ALU.add).then_inc(odd_added, 1)

            for t in TAIL_TICKS:
                for group, offset in enumerate(WEIGHTED):
                    tail_at(t, offset, weighted_lo, group)
                tail_at(t, ADD_OUTPUT, root, 0, ve3_ready, rstd3_ready)
                tail_at(t, EXPONENTS, times_values, e2, e2_ready, e2v, e2v_ready, sums_ready)
                tail_at(t, EXPONENTS, times_values, e1, e1_ready, ev, ev_ready, None)
                tail_at(t, SUMS, numerator)
                tail_at(t, ADD_WKV, root, 1, ve4_ready, rstd4_ready)
                for k in range(NE1 // 2):
                    tail_at(t, LAST_READ[1 + k // 2 * 2], add_odd, k)

        @block.scalar
        def _(act):
            a = nc.scalar
            act.wait_ge(ld_small, 64)
            a.activation(tgx[:], gx_sb[:], ACT.Tanh).then_inc(tanh_done, 1)
            a.activation(tgf[:], gf_sb[:], ACT.Tanh).then_inc(tanh_done, 1)
            a.activation(sgate[:], gates_sb[:], ACT.Exp, scale=-1.0).then_inc(sg_exp, 1)

            def expert_hi(e):
                act.wait_ge(w_in[e % 2], 16 * (e // 2 + 1))
                if e >= 2:
                    act.wait_ge(moe_mm, products_with(e - 2))
                a.activation(w_hi[e % 2][:], w_raw[e % 2][:], ACT.Copy).then_inc(whi_ready, 1)

            def side_hi(n):
                act.wait_ge(s_in[n % 2], 16 * (n // 2 + 1))
                a.activation(side_part(n)[0], pairs(s_raw[n % 2][:]), ACT.Copy).then_inc(shi_ready, 1)

            def exponential(n):
                if n % 4 == 0 and n >= 8:
                    act.wait_ge(av_done, n // 4 - 1)
                act.wait_ge(p2_done, n + 1)
                a.activation(probs[:, n % 8, :, :], bank[2 + n % 2][:].rearrange("p (c t) -> p c t", c=CC),
                             ACT.Exp).then_inc(exp_done, 1)

            def stack_copy(b, use):
                half = use % 2
                done, stacked, dst = ((q_mm, q_stacked, q_stack[b % 2]) if use < 2 else (k_mm, k_stacked, k_stack))
                if use == 0 and b >= 2:
                    act.wait_ge(q_max_ready, 2 * (b - 1))
                if use >= 2 and b >= 1:
                    for n in range(QUADS * (b - 1) + 2 * half, QUADS * (b - 1) + 2 * half + 2):
                        act.wait_ge(kpad_in[n % 8], 64 * (n // 8 + 1))
                act.wait_ge(done, 2 * b + half + 1)
                a.activation(dst[:, 2 * half:2 * half + 2, :],
                             st_bank(b, use).rearrange("p (q t) -> p q t", q=2), ACT.Copy).then_inc(stacked, 1)

            def spread_values(b):
                act.wait_ge(v_mm, b + 1)
                if b == 0:
                    act.wait_ge(consts, V_PAD_MADE)
                    act.wait_ge(ld_mask, 32)
                if b >= 2:
                    act.wait_ge(av_done, 4 * (b - 1))
                vp = v_pad[b % 2][:].rearrange("p c (g i) n -> p c g i n", i=2)
                src = st_bank(b, 6)[:, 0:CC * P].rearrange("p (c g i n) -> p c g i n", c=CC, i=2, n=HD)
                for c in range(CC):
                    for i in range(2):
                        a.activation(vp[:, c, :, i, HD * i:HD * (i + 1)], src[:, c, :, i, :], ACT.Copy,
                                     scale=mask_col[:, c, b:b + 1]).then_inc(v_ready, 1)

            def second_hi(b):
                act.wait_ge(xn2_T, b + 1)
                a.activation(xT_hi[:, b, :, :], bank[5][:, 0:T].rearrange("p (c n) -> p c n", c=CC),
                             ACT.Copy).then_inc(xThi_ready, 1)

            def heads_out(b):
                act.wait_ge(av_done, 4 * (b + 1))
                if b >= 1:
                    act.wait_ge(o_T, b)
                a.activation(o_raw[:], bank[4][:].rearrange("p (f t) -> p f t", f=2), ACT.Copy).then_inc(o_read, 1)

            def copy_maxima(b):
                act.wait_ge(max_T, b + 1)
                if b >= 1:
                    act.wait_ge(max_mm, 2 * b)
                a.activation(max_rows[:], bank[5][0:2 * NH, 0:T], ACT.Copy).then_inc(max_copied, 1)

            def weight_exponentials(part):
                act.wait_ge(gated_ready, part + 1)
                a.activation(w_e[:, ROUTED[part]], gated[:, ROUTED[part]], ACT.Exp).then_inc(exp_w, 1)

            def square_second(b):
                act.wait_ge(xn2_ready, b + 1)
                a.activation(sq_junk[:], xn_f[:], ACT.Square, accum_out=nsq[:, b:b + 1]).then_inc(sq_done, 1)

            for t in TICKS:
                if 0 <= t < NH * NB:
                    exponential(t)
                at(t, VALUES_SPREAD, spread_values)
                at(t, SPLIT2, second_hi)
                for use, offset in enumerate(STACK):
                    at(t, offset, stack_copy, use)
                at(t, MAX_T, copy_maxima)
                at(t, HEADS_OUT, heads_out)
                at(t, NORMALISE2 + 1, square_second)
                if t in (6, 8):
                    expert_hi(t // 2 - 3)
                if t == ROUTE:
                    weight_exponentials(0)
            weight_exponentials(1)
            for e in range(4):
                if e >= 2:
                    expert_hi(e)
                side_hi(e)
            with act.Fori(2, NE // 2) as i:
                for odd in range(2):
                    act.wait_ge(w_in[odd], i * 16 + 16)
                    act.wait_ge(moe_mm, i * (2 * NB) + NB * (odd - 1))
                    a.activation(w_hi[odd][:], w_raw[odd][:], ACT.Copy).then_inc(whi_ready, 1)
                    act.wait_ge(s_in[odd], i * 16 + 16)
                    a.activation(side_of(i, odd)[0], pairs(s_raw[odd][:]), ACT.Copy).then_inc(shi_ready, 1)
            for half in range(2):
                act.wait_ge(wparts_T, half + 1)
                a.activation(wT[:, half * 4 * P:(half + 1) * 4 * P], bank[half][0:2 * NE, :],
                             ACT.Copy).then_inc(wT_ready, 1)

            def transposed_keys(b):
                act.wait_ge(kn_T, b + 1)
                if b >= 1:
                    act.wait_ge(arg2_ready, b)
                    act.wait_ge(arg1_ready, b)
                src = bank[6][:, 0:T].rearrange("p (c t) -> p c t", c=CC)
                a.activation(kT[:], src, ACT.Copy).then_inc(kT_ready, 1)
                for c in range(CC):
                    a.activation(uk[:, c, :], src[:, c, :], ACT.Identity, bias=u_sb[:, c:c + 1]).then_inc(uk_ready, 1)

            def transposed_qk(b):
                act.wait_ge(qk_T, b + 1)
                if b >= 1:
                    act.wait_ge(scored, b)
                a.activation(qkT[:], bank[4][:, 0:2 * P].rearrange("p (c t) -> p c t", c=2),
                             ACT.Copy).then_inc(qkT_ready, 1)

            def wkv_exponentials(b):
                act.wait_ge(arg2_ready, b + 1)
                if b >= 1:
                    act.wait_ge(e2v_ready, b)
                    act.wait_ge(sums_ready, 2 * b)
                a.activation(e2[:], arg2[:], ACT.Exp).then_inc(e2_ready, 1)
                act.wait_ge(arg1_ready, b + 1)
                if b >= 1:
                    act.wait_ge(num_ready, b)
                    act.wait_ge(y_ready, b)
                a.activation(e1[:], arg1[:], ACT.Exp).then_inc(e1_ready, 1)

            def last_exponentials(b):
                act.wait_ge(nm4_ready, b + 1)
                a.activation(ex1[:], lg1[:], ACT.Exp, bias=nm1[:], accum_out=s1[:]).then_inc(ex4_ready, 1)

            def row_exponentials(b):
                act.wait_ge(scr_ready, b + 1)
                a.activation(pat[:], scr[:], ACT.Exp, bias=row_nm[:], accum_out=row_s[:]).then_inc(pat_exp, 1)

            def transposed_rows(b):
                act.wait_ge(pat_T, b + 1)
                if b >= 1:
                    act.wait_ge(ao_mm, b)
                a.activation(patT[:], bank[4][:, 3 * P:4 * P], ACT.Copy).then_inc(patT_ready, 1)

            def attention_out(b):
                act.wait_ge(ao_mm, b + 1)
                if b >= 1:
                    act.wait_ge(wa_ready, GROUPS * b)
                a.activation(ao_f[:], bank[4][:, 0:P], ACT.Copy).then_inc(ao_ready, 1)

            def weighted_hi(b, group):
                n = GROUPS * b + group
                act.wait_ge(wa_ready, n + 1)
                if b >= 1:
                    act.wait_ge(oproj_mm, n - GROUPS + 1)
                    act.wait_ge(walo_ready, n - GROUPS + 1)
                else:
                    act.wait_ge(moe_mm, QKV_AT[(NE - 1, 2 * group + 1)] + 1)
                a.activation(wa_hi[:, group * GROUP * P:(group + 1) * GROUP * P],
                             wa_f[group // 2][:, group % 2 * GROUP * P:(group % 2 + 1) * GROUP * P],
                             ACT.Copy).then_inc(wahi_ready, 1)

            def last_hi(b):
                act.wait_ge(xn4_T, b + 1)
                if b >= 1:
                    act.wait_ge(l1_mm, NE1 // 2 * b)
                a.activation(x1_hi[:], bank[7][:, 0:T].rearrange("p (c t) -> p c t", c=CC),
                             ACT.Copy).then_inc(x4hi_ready, 1)

            def transposed_combine(b):
                act.wait_ge(comb_T, b + 1)
                if b >= 1:
                    act.wait_ge(bias_mm, b)
                a.activation(combT[:], bank[7][0:NE1, 0:P], ACT.Copy).then_inc(combT_ready, 1)

            def bias_out(b):
                act.wait_ge(bias_mm, b + 1)
                if b >= 1:
                    act.wait_ge(odd_added, NE1 // 2 * b)
                a.activation(bias_term, bank[7][:, 0:T], ACT.Copy).then_inc(bias_ready, 1)

            def odd_pair(b, k):
                act.wait_ge(comb_ready, b + 1)
                act.wait_ge(l1_mm, NE1 // 2 * b + k + 1)
                for i in range(2):
                    m = k - 1 + i
                    if b >= 1:
                        act.wait_ge(odd_added, NE1 // 2 * (b - 1) + m + 1)
                    a.activation(odd_out[m][:], bank[3][:, i * T:(i + 1) * T], ACT.Copy,
                                 scale=comb[:, 2 * k + i:2 * k + i + 1]).then_inc(odd_ready, 1)

            for t in TAIL_TICKS:
                tail_at(t, QK_T, transposed_qk)
                tail_at(t, SCORES, row_exponentials)
                tail_at(t, PAT_T, transposed_rows)
                tail_at(t, AO, attention_out)
                tail_at(t, SPLIT4, last_hi)
                tail_at(t, KEYS_T, transposed_keys)
                for group, offset in enumerate(WEIGHTED):
                    tail_at(t, offset, weighted_hi, group)
                tail_at(t, EXPONENTS, wkv_exponentials)
                tail_at(t, GATE, last_exponentials)
                tail_at(t, COMB_T, transposed_combine)
                tail_at(t, BIAS, bias_out)
                for k, offset in enumerate(LAST_READ):
                    if k % 2:
                        tail_at(t, offset, odd_pair, k)

        @block.vector
        def _(eng):
            v = nc.vector
            d = Tally(dve)

            def then(instruction):
                eng.wait_ge(dve, d.step(instruction))

            eng.wait_ge(ld_x0, 16)
            then(v.bn_stats(bn6[:, 0, :], x_sb[:, 0, :]))
            then(v.bn_aggr(mv[:, 0, :], bn6[:, 0, :]))
            v.tensor_scalar(var_eps[:, 0:1], mv[:, 0, 1:2], EPS, None, ALU.add).then_inc(vef_ready, 1)
            eng.wait_ge(ld_wts, 64)
            v.tensor_scalar(wqT_sb[:], wqT_sb[:], XATTN_SCALE, None, ALU.mult).then_inc(wq_scaled, 1)
            d.step(v.tensor_scalar(bq_sb[:], bq_sb[:], XATTN_SCALE, None, ALU.mult))

            def selections():
                eng.wait_ge(ident_ready, 1)
                eng.wait_ge(sel_clear, 3)
                for t, parts in ((sel_k_hi, (0, 2)), (sel_k_lo, (1,)), (sel_q_hi, (0, 1)), (sel_q_lo, (2,))):
                    for quad in range(QUADS):
                        half, odd = divmod(quad, 2)
                        src = ident[:, 64 * half:64 * half + 64].rearrange("p (j n) -> p j n", n=16)[
                            :, :, HD * odd:HD * (odd + 1)]
                        dst = t[:, quad, :].rearrange("p (j n) -> p j n", j=4)
                        for part in parts:
                            d.step(v.tensor_copy(dst[:, :, HD * part:HD * (part + 1)], src))
                by_head_q = row_q[:].rearrange("p (j n) -> p j n", j=4)
                by_head_k = row_k[:].rearrange("p (j n) -> p j n", j=4)
                for s, row, end in ((0, 24, 26), (1, 26, 27), (2, 27, 28), (3, 28, 29)):
                    d.step(v.memset(by_head_q[32 * s:32 * s + 32, :, row:end], 1.0))
                for s, row, end in ((0, 24, 25), (0, 26, 27), (1, 25, 26), (2, 27, 31)):
                    d.step(v.memset(by_head_k[32 * s:32 * s + 32, :, row:end], 1.0))
                for s in range(4):
                    d.step(v.tensor_copy(batch_row[32 * s:32 * s + 32, :],
                                         ident[32 * s:32 * s + 32, 32 * s:32 * s + NB]))
                eng.wait_ge(ld_mask8, 64)
                d.step(v.tensor_scalar(aux_f[0:64, 0, :], mask8[0:64, :], -NEG_MASK, None, ALU.mult))
                d.step(v.tensor_scalar(aux_f[64:128, 0, :], mask8[64:128, :], 1.0, NEG_MASK, ALU.subtract, ALU.mult))
                n = d.step(v.tensor_scalar(aux_f[:, 1, :], mask8[:], -1.0, 1.0, ALU.mult, ALU.add))
                eng.wait_ge(dve, n)
                for dst, k in ((aux_q, 0), (aux_k, 1)):
                    n = d.step(v.tensor_copy(dst[:], aux_f[:, k, :]))
                eng.wait_ge(dve, n)
                for p0, dst, k in ((32, aux_q, 0), (96, aux_q, 0), (32, aux_k, 1)):
                    d.step(v.tensor_tensor(dst[p0:p0 + 32, :], aux_f[p0:p0 + 32, k, :],
                                           dst[p0:p0 + 32, :].bitcast(F32), ALU.subtract))
                d.step(v.tensor_scalar(aux_k[64:96, :], aux_f[64:96, 1, :], 0.0, 1.0, ALU.mult, ALU.add))
                d.step(v.tensor_scalar(aux_k[96:128, :], aux_f[96:128, 1, :], 0.0, None, ALU.mult))

            def batch_selections(b0, b1):
                for dst, rows in ((sel_aux_k, row_k), (sel_aux_q, row_q)):
                    n = d.step(v.tensor_tensor(dst[:, b0:b1, :],
                                               batch_row[:, b0:b1].unsqueeze(2).to_broadcast([P, b1 - b0, P]),
                                               rows[:].unsqueeze(1).to_broadcast([P, b1 - b0, P]), ALU.mult))
                return n

            def other_statistics():
                eng.wait_ge(ld_x, 16)
                for b in range(1, NB):
                    n = d.step(v.bn_stats(bn6[:, b, :], x_sb[:, b, :]))
                eng.wait_ge(dve, n)
                for b in range(1, NB):
                    n = d.step(v.bn_aggr(mv[:, b, :], bn6[:, b, :]))
                eng.wait_ge(dve, n)
                v.tensor_scalar(var_eps[:, 1:NB], mv[:, 1:NB, 1], EPS, None, ALU.add).then_inc(vef_ready, 1)

            def other_selections():
                then(v.memset(sel_max[:].bitcast(F32), 0.0))
                for quad in range(QUADS):
                    for part in range(2):
                        h0 = NH * part + head_of(quad, 0)
                        d.step(v.tensor_copy(sel_max[:, quad, 29 + part::32], ident[0:2 * NH, h0:h0 + 7:2]))
                eng.wait_ge(dve, batch_selections(1, NB))
                v.memset(pq[:, :, 0:1], 0.0).then_inc(setup_done, 1)

            def prepare(b):
                eng.wait_ge(rstd_ready, min(b, 1) + 1)
                if b >= 1:
                    eng.wait_ge(qk_mm, b)
                v.tensor_scalar(xn[:], x_sb[:, b, :], mv[:, b, 0:1], rstd[:, b:b + 1], ALU.subtract,
                                ALU.mult).then_inc(xn_ready, 1)

            def project(b):
                if b == 1:
                    eng.wait_ge(ld_mask, 32)
                if b == 0:
                    selections()
                    batch_selections(0, 1)
                    eng.wait_ge(ld_mask0, 16)
                eng.wait_ge(qk_mm, b + 1)
                v.scalar_tensor_tensor(q_f[:], bank[5][:, 0:T], bq_sb[:], mask_bc[:, b, :], ALU.add,
                                       ALU.mult).then_inc(dve, 1)
                d.n += 1
                nq = d.n
                v.scalar_tensor_tensor(k_f[:], bank[5][:, T:2 * T], bk_sb[:], mask_bc[:, b, :], ALU.add,
                                       ALU.mult).then_inc(kf_ready, 1)
                if b >= 1:
                    eng.wait_ge(q_mm, 2 * b)
                eng.wait_ge(dve, nq)
                nq = d.step(v.tensor_copy(q_hi[:], q_f[:]))
                eng.wait_ge(kf_ready, b + 1)
                nk = d.step(v.tensor_copy(k_hi[:], k_f[:]))
                eng.wait_ge(dve, nq)
                d.step(v.tensor_tensor(q_lo[:], q_f[:], q_hi[:].bitcast(F32), ALU.subtract))
                eng.wait_ge(dve, nk)
                v.tensor_tensor(k_lo[:], k_f[:], k_hi[:].bitcast(F32), ALU.subtract).then_inc(qk_split, 1)

            def maxima(n):
                h = head_of(n % NH // 4, n % 4)
                eng.wait_ge(p1_done, n + 1)
                if n % NH == 0 and n:
                    eng.wait_ge(negmax_ready, n // NH)
                v.tensor_reduce(mx[:, :, h], bank[n % 2][:].rearrange("p (c s) -> p c s", c=CC), axis=AX.X,
                                op=ALU.max).then_inc(p1_read, 1)

            def negate_maxima(b):
                eng.wait_ge(p1_read, NH * (b + 1))
                if b >= 1:
                    eng.wait_ge(max_T, b)
                then(v.tensor_scalar(neg_max[:, :, 0, :], mx[:], -1.0, None, ALU.mult))
                v.scalar_tensor_tensor(neg_max[:, :, 1, :], mx[:], -1.0, neg_max[:, :, 0, :].bitcast(F32), ALU.mult,
                                       ALU.subtract).then_inc(negmax_ready, 1)

            def add_maxima(b, half):
                if b >= 1:
                    eng.wait_ge(p2_done, NH * (b - 1) + 8 * (half + 1))
                eng.wait_ge(q_stacked, 2 * (b + 1))
                eng.wait_ge(max_mm, 2 * b + half + 1)
                s = slice(2 * half, 2 * half + 2)
                v.tensor_tensor(q_stack_max[:, s, :], st_bank(b, 4 + half).rearrange("p (q t) -> p q t", q=2),
                                q_stack[b % 2][:, s, :].bitcast(F32), ALU.add).then_inc(q_max_ready, 1)

            def normalise_heads(b):
                eng.wait_ge(o_T, b + 1)
                cols = bank[5][:].rearrange("p (g n) -> p g n", n=32)
                then(v.reciprocal(o_den[:].rearrange("p c (g i) -> p (c g) i", i=2), cols[:, :, 16:18]))
                then(v.tensor_tensor(o_den[:], o_den[:], mask_col[:, :, b:b + 1].to_broadcast([P, CC, NH]), ALU.mult))
                if b >= 1:
                    eng.wait_ge(o_back, b)
                v.tensor_tensor(o_tok[:].rearrange("p c (g i n) -> p (c g) i n", i=2, n=HD),
                                cols[:, :, 0:16].rearrange("p g (i n) -> p g i n", i=2),
                                o_den[:].rearrange("p c (g i) -> p (c g) i", i=2).unsqueeze(3).to_broadcast(
                                    [P, CC * NH // 2, 2, HD]), ALU.mult).then_inc(otok_ready, 1)

            def add_attention(b):
                eng.wait_ge(tanh_done, 2)
                eng.wait_ge(o_back, b + 1)
                v.scalar_tensor_tensor(x_sb[:, b, :], bank[5][:, 0:T], tgx[:, 0:1], x_sb[:, b, :], ALU.mult,
                                       ALU.add).then_inc(x1_ready, 1)
                eng.wait_ge(x1_ready, b + 1)
                then(v.bn_stats(bn6f[:], x_sb[:, b, :]))
                then(v.bn_aggr(mvf[:], bn6f[:]))
                if b >= 1:
                    eng.wait_ge(rstd2_ready, b)
                v.tensor_scalar(vef[:], mvf[:, 1:2], EPS, None, ALU.add).then_inc(ve2_ready, 1)

            def normalise_second(b):
                eng.wait_ge(rstd2_ready, b + 1)
                if b >= 1:
                    eng.wait_ge(xn2_T, b)
                    eng.wait_ge(sq_done, b)
                v.tensor_scalar(xn_f[:], x_sb[:, b, :], mvf[:, 0:1], rstdf[:], ALU.subtract,
                                ALU.mult).then_inc(xn2_ready, 1)

            def split_second(b):
                eng.wait_ge(xThi_ready, b + 1)
                v.tensor_tensor(xT_lo[:, b, :, :], bank[5][:, 0:T].rearrange("p (c n) -> p c n", c=CC),
                                xT_hi[:, b, :, :].bitcast(F32), ALU.subtract).then_inc(xT_ready, 1)

            def other_constants():
                eng.wait_ge(consts, CONSTS)
                eng.wait_ge(ld_small, 64)
                v.tensor_tensor(sim_sq[:], sim_sb[:], sim_sb[:], ALU.mult).then_inc(simsq_ready, 1)
                eng.wait_ge(sg_exp, 1)
                then(v.tensor_scalar(sgate[:], sgate[:], 1.0, None, ALU.add))
                then(v.reciprocal(sgate[:], sgate[:]))
                eng.wait_ge(ld_late, 80)
                for c in range(CC):
                    d.step(v.tensor_scalar(w_full[:, c, :], ones[:], w_sb[:, c:c + 1], None, ALU.mult))
                d.step(v.memset(o_ext[:, :, 0:1], NEG_START))
                then(v.tensor_copy(wg_parts[:, :, 0, :], wg_sb[:]))
                then(v.tensor_tensor(wg_parts[:, :, 1, :], wg_sb[:], wg_parts[:, :, 0, :].bitcast(F32), ALU.subtract))

            def router_sums():
                eng.wait_ge(simsum_mm, 1)
                v.tensor_scalar(sim_sq[:, 0, :], bank[5][:, 0:NE], 1e-24, None, ALU.max).then_inc(simsum_ready, 1)

            def router_columns():
                eng.wait_ge(simr_ready, 1)
                then(v.tensor_tensor(simn[:], sim_sb[:], sim_r[:].unsqueeze(1).to_broadcast([P, CC, NE]), ALU.mult))
                then(v.tensor_copy(sim_parts[:, :, 0, :], simn[:]))
                v.tensor_tensor(sim_parts[:, :, 1, :], simn[:], sim_parts[:, :, 0, :].bitcast(F32),
                                ALU.subtract).then_inc(simsum_ready, 1)

            def attention_ticks():
                for t in TICKS:
                    at(t, NEGATE, negate_maxima)
                    if 0 <= t + PEAK_LEAD < NH * NB:
                        maxima(t + PEAK_LEAD)
                    at(t, NORMALISE, prepare)
                    at(t, SPLIT, project)
                    for half, offset in enumerate(MAX_ROWS):
                        at(t, offset + 1, add_maxima, half)
                    at(t, HEADS_NORM, normalise_heads)
                    at(t, ADD, add_attention)
                    at(t, NORMALISE2, normalise_second)
                    at(t, SPLIT2, split_second)
                    if t == SPLIT:
                        other_statistics()
                    if t == SPLIT + 1:
                        other_selections()
                    if t == ROUTE:
                        route(0)
                    if 0 <= t - FIRST_WEIGHED < EARLY:
                        weigh_product(t - FIRST_WEIGHED)
                    at(t, ROUTER_READ, read_logits)
                    if t == 2:
                        other_constants()
                    if t == 5:
                        router_sums()
                    if t == 10:
                        router_columns()

            def read_logits(b):
                eng.wait_ge(routed, b + 1)
                v.tensor_reduce(lg[:, b, :], bank[5][:, 0:2 * NE].rearrange("p (k e) -> p e k", k=2), axis=AX.X,
                                op=ALU.add).then_inc(lg_read, 1)

            def route(part):
                rows = ROUTED[part]
                nb = rows.stop - rows.start
                eng.wait_ge(sq_done, rows.stop)
                v.tensor_scalar(nsq[:, rows], nsq[:, rows], 1e-24, None, ALU.max).then_inc(nsq_ready, 1)
                eng.wait_ge(rnorm_ready, part + 1)

                def each(column):
                    return column.unsqueeze(2).to_broadcast([P, nb, NE])

                l, w, p, f, w_g = lg[:, rows], w_e[:, rows], pos[:, rows], fb[:, rows], gated[:, rows]
                eng.wait_ge(lg_read, rows.stop)
                then(v.tensor_tensor(l, l, each(rnorm[:, rows]), ALU.mult))
                then(v.tensor_tensor(l, l, sgate[:].unsqueeze(1).to_broadcast([P, nb, NE]), ALU.subtract))
                for b in range(rows.start, rows.stop):
                    n = d.step(v.max(top8[:, b, :], lg[:, b, :]))
                eng.wait_ge(dve, n)
                for b in range(rows.start, rows.stop):
                    n = d.step(v.max_index(topi[:, b, :], top8[:, b, :], lg[:, b, :]))
                d.step(v.tensor_scalar(w_g, l, 0.0, None, ALU.max))
                then(v.tensor_scalar(gmax[:, rows], top8[:, rows, 0], 0.0, None, ALU.max))
                v.tensor_tensor(w_g, w_g, each(gmax[:, rows]), ALU.subtract).then_inc(gated_ready, 1)
                then(v.tensor_copy(topi_f[:, rows], topi[:, rows]))
                iota_b = iota_e[:].unsqueeze(1).to_broadcast([P, nb, NE])
                d.step(v.tensor_tensor(f, iota_b, topi_f[:, rows, 0:1].to_broadcast([P, nb, NE]), ALU.is_equal))
                d.step(v.tensor_scalar(inact[:, rows], top8[:, rows, 0], 0.0, None, ALU.is_le))
                then(v.tensor_tensor(p, iota_b, topi_f[:, rows, 1:2].to_broadcast([P, nb, NE]), ALU.is_equal))
                then(v.tensor_tensor(f, f, p, ALU.add))
                d.step(v.tensor_scalar(p, l, 0.0, None, ALU.is_gt))
                then(v.tensor_tensor(f, f, each(inact[:, rows]), ALU.mult))
                then(v.tensor_tensor(p, p, f, ALU.add))
                eng.wait_ge(exp_w, part + 1)
                then(v.tensor_tensor(w, w, p, ALU.mult))
                then(v.tensor_reduce(esum[:, rows], w, axis=AX.X, op=ALU.add))
                then(v.reciprocal(ersum[:, rows], esum[:, rows]))
                then(v.tensor_tensor(w, w, each(ersum[:, rows]), ALU.mult))

            def weigh_product(n):
                e, b = QKV_ORDER[n]
                eng.wait_ge(moe_mm, n + 1)
                src = bank[qkv_bank(n)][:, 0:QKV]
                if n == 0:
                    eng.wait_ge(av_done, QUADS * NB)
                if e == 0:
                    v.tensor_scalar(qkv[:, b, :], src, w_e[:, b, e:e + 1], None, ALU.mult).then_inc(moe_read, 1)
                else:
                    eng.wait_ge(moe_read, QKV_AT[(e - 1, b)] + 1)
                    v.scalar_tensor_tensor(qkv[:, b, :], src, w_e[:, b, e:e + 1], qkv[:, b, :], ALU.mult,
                                           ALU.add).then_inc(moe_read, 1)

            attention_ticks()

            route(1)
            for n in range(EARLY, EARLY + 4):
                weigh_product(n)
            then(v.tensor_scalar(w_et[:], w_e[:], tgf[:, 0:1], None, ALU.mult))
            then(v.tensor_copy(w_parts[:, :, 0, :], w_et[:]))
            v.tensor_tensor(w_parts[:, :, 1, :], w_et[:], w_parts[:, :, 0, :].bitcast(F32),
                            ALU.subtract).then_inc(wparts_ready, 1)
            for e in range(0, NE, 2):
                for i in range(2):
                    n = d.step(v.tensor_tensor(weight_rows(e + i),
                                               ident[0:2 * NE, e + i:e + i + 1].to_broadcast([2 * NE, P]),
                                               ident[0:2 * NE, NE + e + i:NE + e + i + 1].to_broadcast([2 * NE, P]),
                                               ALU.add))
            eng.wait_ge(dve, n)
            v.memset(row_m[:], 0.0).then_inc(rows_ready, 1)

            with eng.Fori(1, NE // 2 - 1) as i:
                for odd in range(2):
                    for b in range(NB):
                        m = NB * odd + b
                        eng.wait_ge(moe_mm, i * (2 * NB) + m + 1)
                        eng.wait_ge(moe_read, i * (2 * NB) + m - NB + 1)
                        v.scalar_tensor_tensor(qkv[:, b, :], bank[RING[m % 8]][:, 0:QKV],
                                               w_e[:, b, bass.ds(i * 2 + odd, 1)], qkv[:, b, :], ALU.mult,
                                               ALU.add).then_inc(moe_read, 1)

            def flat(tile):
                return tile.rearrange("p (c t) -> p c t", c=CC)

            def weighted(b, group):
                n = GROUPS * b + group
                eng.wait_ge(wb_mm, n + 1)
                eng.wait_ge(ao_ready, b + 1)
                if b >= 1:
                    eng.wait_ge(walo_ready, n - GROUPS + 1)
                v.tensor_tensor(wa_f[group // 2][:, group % 2 * GROUP * P:(group % 2 + 1) * GROUP * P].rearrange(
                    "p (e t) -> p e t", e=GROUP), bank[n % 2][:].rearrange("p (e t) -> p e t", e=GROUP),
                    ao_f[:].unsqueeze(1).to_broadcast([P, GROUP, P]), ALU.mult).then_inc(wa_ready, 1)

            def statistics(b, col, ready):
                then(v.bn_stats(bn6f[:], x_sb[:, b, :]))
                then(v.bn_aggr(mv[:, col, :], bn6f[:]))
                v.tensor_scalar(var_eps[:, col:col + 1], mv[:, col, 1:2], EPS, None, ALU.add).then_inc(ready, 1)

            def add_output(b):
                eng.wait_ge(oproj_mm, GROUPS * (b + 1))
                v.tensor_tensor(x_sb[:, b, :], bank[5][:, 0:T], x_sb[:, b, :], ALU.add).then_inc(x2_ready, 1)
                eng.wait_ge(x2_ready, b + 1)
                statistics(b, 0, ve3_ready)

            def keys(b):
                eng.wait_ge(rstd3_ready, b + 1)
                if b >= 1:
                    eng.wait_ge(kn_T, b)
                v.tensor_scalar(kn[:], x_sb[:, b, :], mv[:, 0, 0:1], rstd[:, 0:1], ALU.subtract,
                                ALU.mult).then_inc(kn_ready, 1)

            def wkv_exponents(b):
                o_prev, o_next = o_ext[:, :, 0:P], o_ext[:, :, 1:P + 1]
                eng.wait_ge(kT_ready, b + 1)
                for c in range(CC):
                    d.step(v.tensor_tensor_scan(o_ext[:, c, 1:P + 1], w_full[:, c, :], kT[:, c, :], NEG_START,
                                                op0=ALU.add, op1=ALU.max))
                eng.wait_ge(dve, d.n)
                if b >= 1:
                    eng.wait_ge(e2_ready, b)
                    eng.wait_ge(e1_ready, b)
                for c in range(CC):
                    n_2 = d.step(v.scalar_tensor_tensor(arg2[:, 0, c * P:(c + 1) * P], o_prev[:, c, :],
                                                        w_sb[:, c:c + 1], o_next[:, c, :], ALU.add, ALU.subtract))
                eng.wait_ge(dve, n_2)
                v.tensor_tensor(flat(arg2[:, 1, :]), kT[:], o_next, ALU.subtract).then_inc(arg2_ready, 1)
                eng.wait_ge(uk_ready, CC * (b + 1))
                then(v.tensor_tensor(no[:], o_prev, uk[:], ALU.max))
                then(v.tensor_tensor(flat(arg1[:, 0, :]), o_prev, no[:], ALU.subtract))
                v.tensor_tensor(flat(arg1[:, 1, :]), uk[:], no[:], ALU.subtract).then_inc(arg1_ready, 1)
                eng.wait_ge(arg2_ready, b + 1)

            def wkv_sums(b):
                eng.wait_ge(e2v_ready, b + 1)
                eng.wait_ge(e2_ready, b + 1)
                if b >= 1:
                    eng.wait_ge(num_ready, b)
                v.tensor_tensor_scan(pq[:, 0, 1:T + 1], e2[:, 0, :], e2v[:], 0.0, op0=ALU.mult,
                                     op1=ALU.add).then_inc(sums_ready, 1)
                v.tensor_tensor_scan(pq[:, 1, 1:T + 1], e2[:, 0, :], e2[:, 1, :], 0.0, op0=ALU.mult,
                                     op1=ALU.add).then_inc(sums_ready, 1)

            def wkv_quotient(b):
                eng.wait_ge(sums_ready, 2 * (b + 1))
                eng.wait_ge(e1_ready, b + 1)
                eng.wait_ge(den_ready, b + 1)
                then(v.tensor_tensor(den[:], den[:], e1[:, 1, :], ALU.add))
                then(v.reciprocal(den[:], den[:]))
                eng.wait_ge(num_ready, b + 1)
                if b >= 1:
                    eng.wait_ge(y_T, b)
                v.tensor_tensor(yT[:], flat(num[:]), flat(den[:]), ALU.mult).then_inc(y_ready, 1)

            def add_wkv(b):
                eng.wait_ge(y_T, b + 1)
                v.scalar_tensor_tensor(x_sb[:, b, :], bank[6][:, 0:T], tgx[:, 1:2], x_sb[:, b, :], ALU.mult,
                                       ALU.add).then_inc(x3_ready, 1)
                eng.wait_ge(x3_ready, b + 1)
                statistics(b, 1, ve4_ready)

            def normalise_last(b):
                eng.wait_ge(rstd4_ready, b + 1)
                v.tensor_scalar(xn_1[:], x_sb[:, b, :], mv[:, 1, 0:1], rstd[:, 1:2], ALU.subtract,
                                ALU.mult).then_inc(xn4_ready, 1)

            def split_last(b):
                eng.wait_ge(x4hi_ready, b + 1)
                v.tensor_tensor(x1_lo[:], flat(bank[7][:, 0:T]), x1_hi[:].bitcast(F32),
                                ALU.subtract).then_inc(x4_split, 1)

            def gate_last(b):
                eng.wait_ge(lg4_mm, b + 1)
                then(v.tensor_reduce(lg1[:], bank[7][:, 0:2 * NE1].rearrange("p (k e) -> p e k", k=2), axis=AX.X,
                                     op=ALU.add))
                then(v.max(m8[:], lg1[:]))
                d.step(v.max_index(i8[:], m8[:], lg1[:]))
                v.tensor_scalar(nm1[:], m8[:, 0:1], -1.0, None, ALU.mult).then_inc(nm4_ready, 1)

            def combine_last(b):
                eng.wait_ge(dve, d.n)
                if b >= 1:
                    eng.wait_ge(odd_ready, NE1 // 2 * b)
                then(v.tensor_copy(i8f[:], i8[:]))
                then(v.tensor_scalar(comb[:], iota_e[:, 0:NE1], i8f[:, 0:1], None, ALU.is_equal))
                eng.wait_ge(ex4_ready, b + 1)
                then(v.reciprocal(r1[:], s1[:]))
                then(v.tensor_tensor(r1[:], r1[:], tgf[:, 1:2], ALU.mult))
                v.tensor_scalar(comb[:], comb[:], r1[:], None, ALU.mult).then_inc(comb_ready, 1)

            def even_pair(b, k):
                eng.wait_ge(l1_mm, NE1 // 2 * b + k + 1)
                for i in range(2):
                    if k + i:
                        eng.wait_ge(l1_even, NE1 // 2 * b + k + i)
                    else:
                        eng.wait_ge(comb_ready, b + 1)
                    v.scalar_tensor_tensor(x_sb[:, b, :], bank[2][:, i * T:(i + 1) * T],
                                           comb[:, 2 * k + i:2 * k + i + 1], x_sb[:, b, :], ALU.mult,
                                           ALU.add).then_inc(l1_even, 1)

            def last_out(b):
                eng.wait_ge(l1_even, NE1 // 2 * (b + 1))
                eng.wait_ge(odd_added, NE1 // 2 * (b + 1))
                v.tensor_tensor(x_sb[:, b, :], x_sb[:, b, :], odd_sum, ALU.add).then_inc(xout_ready, 1)

            def mask_scores(b):
                eng.wait_ge(scored, b + 1)
                then(v.scalar_tensor_tensor(scr[:], bank[4][:, 2 * P:3 * P], FFN_SCALE, causal[:], ALU.mult, ALU.mult))
                then(v.tensor_tensor_reduce(out=scr[:], in0=scr[:], in1=causal_neg[:], scale=1.0, scalar=-3.0e38,
                                            op0=ALU.add, op1=ALU.max, accum_out=row_m[:]))
                v.tensor_scalar(row_nm[:], row_m[:], -1.0, None, ALU.mult).then_inc(scr_ready, 1)

            def normalise_rows(b):
                eng.wait_ge(pat_exp, b + 1)
                then(v.reciprocal(row_r[:], row_s[:]))
                v.tensor_scalar(pat[:], pat[:], row_r[:], None, ALU.mult).then_inc(pat_ready, 1)

            for t in TAIL_TICKS:
                last_qkv(t, weigh_product)
                for group, offset in enumerate(WEIGHTED):
                    tail_at(t, offset, weighted, group)
                tail_at(t, SCORES, mask_scores)
                tail_at(t, ROWS, normalise_rows)
                tail_at(t, ADD_OUTPUT, add_output)
                tail_at(t, KEYS, keys)
                tail_at(t, EXPONENTS, wkv_exponents)
                tail_at(t, SUMS, wkv_sums)
                tail_at(t, QUOTIENT, wkv_quotient)
                tail_at(t, ADD_WKV, add_wkv)
                tail_at(t, NORMALISE4, normalise_last)
                tail_at(t, SPLIT4, split_last)
                tail_at(t, GATE, gate_last)
                tail_at(t, COMBINE, combine_last)
                for k, offset in enumerate(LAST_READ):
                    if k % 2 == 0:
                        tail_at(t, offset, even_pair, k)
                tail_at(t, LAST_OUT, last_out)

        @block.tensor
        def _(pe):
            banks = [Bank(b) for b in bank]
            stack_uses = [0]

            def stack_bank(b, use, reader, value):
                assert ST_PARITY[(b, use)] == stack_uses[0] % 2
                stack_uses[0] += 1
                return banks[6 + ST_PARITY[(b, use)]].take(pe, reader, value)

            def mm(out_, lhsT, rhs, start, stop):
                return nc.tensor.matmul(out_, lhsT, rhs, start=start, stop=stop)

            def split_product(out_, terms):
                steps = [s for lh, ll, rh, rl in terms for s in ((lh, rh), (lh, rl), (ll, rh))]
                for n, (l, r) in enumerate(steps):
                    last = mm(out_, l, r, n == 0, n == len(steps) - 1)
                return last

            def narrow_product(ps, n, terms):
                for k, (lh, ll, parts) in enumerate(terms):
                    mm(ps[:, 0:2 * n], lh, parts.rearrange("p k e -> p (k e)"), k == 0, False)
                    last = mm(ps[:, 0:n], ll, parts[:, 0, :], False, k == len(terms) - 1)
                return last

            def project(b):
                pe.wait_ge(wq_scaled, 1)
                pe.wait_ge(ld_wts, 64)
                pe.wait_ge(xn_ready, b + 1)
                pe.wait_ge(ctx_in[b % 2], 16 * (b // 2 + 1))
                ps = banks[5].take(pe, kf_ready, b + 1)
                mm(ps[:, 0:T], wqT_sb[:], xn[:], True, True)
                mm(ps[:, T:2 * T], wkT_sb[:], ctx_b[b % 2][:], True, True).then_inc(qk_mm, 1)
                if b == 0:
                    for _ in range(WARMING):
                        mm(bank[0][:, 0:T], wkT_sb[:], ctx_b[0][:], True, True)

            def project_values(b):
                pe.wait_ge(ld_values, 32)
                ps = stack_bank(b, 6, v_ready, 2 * CC * (b + 1))
                for c in range(CC):
                    mm(ps[:, c * P:(c + 1) * P], ctx_b[b % 2][:, c * P:(c + 1) * P], wvT_sb[:], True, False)
                    last = mm(ps[:, c * P:(c + 1) * P], ones[0:1, :], bv_sb[:], False, True)
                last.then_inc(v_mm, 1)

            def stack(b, use):
                if use % 2 == 0:
                    pe.wait_ge(qk_split, b + 1)
                    if b == 1:
                        pe.wait_ge(setup_done, 1)
                hi, lo, s_hi, s_lo, aux, s_aux, done, stacked = (
                    (q_hi, q_lo, sel_q_hi, sel_q_lo, aux_q, sel_aux_q, q_mm, q_stacked) if use < 2 else
                    (k_hi, k_lo, sel_k_hi, sel_k_lo, aux_k, sel_aux_k, k_mm, k_stacked))
                half = use % 2
                ps = stack_bank(b, use, stacked, 2 * b + half + 1)
                for n in range(2):
                    quad, cols = 2 * half + n, slice(n * T, (n + 1) * T)
                    mm(ps[:, cols], s_hi[:, quad, :], hi[:], True, False)
                    mm(ps[:, cols], s_lo[:, quad, :], lo[:], False, False)
                    last = mm(ps[:, cols], s_aux[:, b, :], aux[:], False, True)
                last.then_inc(done, 1)

            def scores_for_maxima(n):
                b, quad, j = n // NH, n % NH // 4, n % 4
                if n % NH == 0:
                    pe.wait_ge(q_stacked, 2 * (b + 1))
                if j == 0:
                    q = QUADS * b + quad
                    pe.wait_ge(kpad_in[q % 8], 64 * (q // 8 + 1))
                ps = banks[n % 2].take(pe, p1_read, n + 1)
                for c in range(CC):
                    last = mm(ps[:, c * T:(c + 1) * T], q_stack[b % 2][:, quad, c * P:(c + 1) * P],
                              k_pad[:, n // 4 % 8, j, :], True, True)
                last.then_inc(p1_done, 1)

            def scores_transposed(n):
                b, quad, j = n // NH, n % NH // 4, n % 4
                if n % 8 == 0:
                    pe.wait_ge(q_max_ready, n // 8 + 1)
                ps = banks[2 + n % 2].take(pe, exp_done, n + 1)
                for c in range(CC):
                    last = mm(ps[:, c * T:(c + 1) * T], k_pad[:, n // 4 % 8, j, c * P:(c + 1) * P],
                              q_stack_max[:, quad, :], True, True)
                last.then_inc(p2_done, 1)

            def values(b, quad):
                half, first = quad // 2, quad % 2 == 0
                if quad == 0:
                    pe.wait_ge(v_ready, 2 * CC * (b + 1))
                    banks[4].take(pe, o_read, b + 1)
                pe.wait_ge(exp_done, NH * b + 4 * quad + 4)
                for c in range(CC):
                    for j in range(4):
                        last = mm(bank[4][32 * j:32 * j + 32, half * T:(half + 1) * T],
                                  v_pad[b % 2][:, c, head_of(quad, j), :],
                                  probs[:, (4 * quad + j) % 8, c, :], first and c == 0, not first and c == CC - 1)
                last.then_inc(av_done, 1)

            def transpose_maxima(b):
                pe.wait_ge(negmax_ready, b + 1)
                ps = banks[5].take(pe, max_copied, b + 1)
                for c in range(CC):
                    last = nc.tensor.transpose(
                        ps[0:2 * NH, c * P:(c + 1) * P],
                        neg_max[:, c, :, :].rearrange("p k h -> p (k h)").bitcast(F32), ident[:])
                last.then_inc(max_T, 1)

            def maxima_rows(b, half):
                pe.wait_ge(max_copied, b + 1)
                ps = stack_bank(b, 4 + half, q_max_ready, 2 * b + half + 1)
                for n in range(2):
                    last = mm(ps[:, n * T:(n + 1) * T], sel_max[:, 2 * half + n, :], max_rows[:], True, True)
                last.then_inc(max_mm, 1)

            def transpose_heads(b):
                pe.wait_ge(o_read, b + 1)
                ps = banks[5].take(pe, otok_ready, b + 1)
                for c in range(CC):
                    for f in range(2):
                        last = nc.tensor.transpose(ps[:, (2 * c + f) * P:(2 * c + f + 1) * P],
                                                   o_raw[:, f, c * P:(c + 1) * P], ident[:])
                last.then_inc(o_T, 1)

            def transpose_back(b):
                pe.wait_ge(otok_ready, b + 1)
                ps = banks[5].take(pe, x1_ready, b + 1)
                for c in range(CC):
                    last = nc.tensor.transpose(ps[:, c * P:(c + 1) * P], o_tok[:, c, :], ident[:])
                last.then_inc(o_back, 1)

            def transpose_second(b):
                pe.wait_ge(xn2_ready, b + 1)
                ps = banks[5].take(pe, xT_ready, b + 1)
                for c in range(CC):
                    last = nc.tensor.transpose(ps[:, c * P:(c + 1) * P], xn_f[:, c * P:(c + 1) * P], ident[:])
                last.then_inc(xn2_T, 1)

            def router_columns():
                pe.wait_ge(simsq_ready, 1)
                ps = banks[5].take(pe, simsum_ready, 1)
                for c in range(CC):
                    last = mm(ps[:, 0:NE], ones[:], sim_sq[:, c, :], c == 0, c == CC - 1)
                last.then_inc(simsum_mm, 1)

            def router_logits(b):
                pe.wait_ge(xT_ready, b + 1)
                if b == 0:
                    pe.wait_ge(simsum_ready, 2)
                ps = banks[5].take(pe, lg_read, b + 1)
                narrow_product(ps, NE, [(xT_hi[:, b, c, :], xT_lo[:, b, c, :], sim_parts[:, c]) for c in range(CC)]
                               ).then_inc(routed, 1)

            def qkv_product(n):
                e, b = QKV_ORDER[n]
                pe.wait_ge(whi_ready, e + 1)
                pe.wait_ge(wlo_ready, e + 1)
                ps = banks[qkv_bank(n)].take(pe, moe_read, n + 1)
                split_product(ps[:, 0:QKV],
                              [(xT_hi[:, b, c, :], xT_lo[:, b, c, :], w_hi[e % 2][:, c, :], w_lo[e % 2][:, c, :])
                               for c in range(CC)]).then_inc(moe_mm, 1)

            for t in TICKS:
                if 0 <= t + PEAK_LEAD < NH * NB:
                    scores_for_maxima(t + PEAK_LEAD)
                if 0 <= t < NH * NB:
                    scores_transposed(t)
                for quad, offset in enumerate(VALUE_PRODUCTS):
                    at(t, offset, values, quad)
                at(t, PROJECT, project)
                at(t, MAX_T, transpose_maxima)
                for use, offset in [*enumerate(STACK + MAX_ROWS), (6, VALUES_MM)]:
                    at(t, offset, project_values if use == 6 else maxima_rows if use > 3 else stack,
                       *(() if use == 6 else (use - 4,) if use > 3 else (use,)))
                at(t, HEADS_T, transpose_heads)
                at(t, HEADS_BACK, transpose_back)
                at(t, SECOND_T, transpose_second)
                if t == 4:
                    router_columns()
                at(t, ROUTER, router_logits)
                if 0 <= t - FIRST_PRODUCTS < EARLY:
                    qkv_product(t - FIRST_PRODUCTS)

            for n in range(EARLY, 2 * NB):
                qkv_product(n)
            pe.wait_ge(lg_read, NB)
            with pe.Fori(1, NE // 2 - 1) as i:
                for odd in range(2):
                    pe.wait_ge(whi_ready, i * 2 + odd + 1)
                    pe.wait_ge(wlo_ready, i * 2 + odd + 1)
                    for b in range(NB):
                        m = NB * odd + b
                        pe.wait_ge(moe_read, i * (2 * NB) + m - 7)
                        split_product(bank[RING[m % 8]][:, 0:QKV],
                                      [(xT_hi[:, b, c, :], xT_lo[:, b, c, :], w_hi[odd][:, c, :], w_lo[odd][:, c, :])
                                       for c in range(CC)]).then_inc(moe_mm, 1)
            for k in range(8):
                banks[RING[k]].reader = (moe_read, QKV_AT[(NE - 2, 0)] - 7 + k)
            pe.wait_ge(wparts_ready, 1)
            for half in range(2):
                ps = banks[half].take(pe, wT_ready, half + 1)
                for k in range(4):
                    last = nc.tensor.transpose(
                        ps[0:2 * NE, k * P:(k + 1) * P],
                        w_parts[:, 4 * half + k].rearrange("p k e -> p (k e)").bitcast(F32), ident[:])
                last.then_inc(wparts_T, 1)

            def weights_on_all(b, group):
                n = GROUPS * b + group
                if n == 0:
                    pe.wait_ge(wT_ready, 2)
                    pe.wait_ge(rows_ready, 1)
                ps = banks[n % 2].take(pe, wa_ready, n + 1)
                for i in range(GROUP):
                    last = mm(ps[:, i * P:(i + 1) * P], weight_rows(GROUP * group + i), wT[:, b * P:(b + 1) * P],
                              True, True)
                last.then_inc(wb_mm, 1)

            def output_experts(b, group):
                n = GROUPS * b + group
                pe.wait_ge(walo_ready, n + 1)
                if n == 0:
                    pe.wait_ge(slo_ready, NE)
                if group == 0:
                    banks[5].take(pe, x2_ready, b + 1)
                for i in range(GROUP):
                    e = GROUP * group + i
                    hi, lo = (t[:, e * P:(e + 1) * P] for t in (wa_hi, wa_lo))
                    for step, (l, r) in enumerate(((hi, o_hi), (hi, o_lo), (lo, o_hi))):
                        last = mm(bank[5][:, 0:T], l, r[:, e, :], e == 0 and step == 0, e == NE - 1 and step == 2)
                last.then_inc(oproj_mm, 1)

            def transposes(ps, parts, done):
                for n, part in enumerate(parts):
                    last = nc.tensor.transpose(ps[:, n * P:(n + 1) * P], part, ident[:])
                last.then_inc(done, 1)

            def transpose_qk(b):
                pe.wait_ge(moe_read, QKV_AT[(NE - 1, b)] + 1)
                transposes(banks[4].take(pe, qkT_ready, b + 1), [qkv[:, b, n * P:(n + 1) * P] for n in range(2)], qk_T)

            def causal_scores(b):
                pe.wait_ge(qkT_ready, b + 1)
                ps = banks[4].take(pe, scr_ready, b + 1)
                mm(ps[:, 2 * P:3 * P], qkT[:, 0, :], qkT[:, 1, :], True, True).then_inc(scored, 1)

            def transpose_rows(b):
                pe.wait_ge(pat_ready, b + 1)
                transposes(banks[4].take(pe, patT_ready, b + 1)[:, 3 * P:4 * P], [pat[:]], pat_T)

            def attend(b):
                pe.wait_ge(patT_ready, b + 1)
                ps = banks[4].take(pe, ao_ready, b + 1)
                mm(ps[:, 0:P], qkv[:, b, 2 * HID:3 * HID], patT[:], True, True).then_inc(ao_mm, 1)

            def transpose_keys(b):
                pe.wait_ge(kn_ready, b + 1)
                transposes(banks[6].take(pe, uk_ready, CC * (b + 1)), [kn[:, c * P:(c + 1) * P] for c in range(CC)],
                           kn_T)

            def transpose_y(b):
                pe.wait_ge(y_ready, b + 1)
                transposes(banks[6].take(pe, x3_ready, b + 1), [yT[:, c, :] for c in range(CC)], y_T)

            def transpose_last(b):
                pe.wait_ge(xn4_ready, b + 1)
                transposes(banks[7].take(pe, x4_split, b + 1), [xn_1[:, c * P:(c + 1) * P] for c in range(CC)], xn4_T)

            def last_logits(b):
                pe.wait_ge(x4_split, b + 1)
                ps = banks[7].take(pe, nm4_ready, b + 1)
                narrow_product(ps, NE1, [(x1_hi[:, c, :], x1_lo[:, c, :], wg_parts[:, c]) for c in range(CC)]
                               ).then_inc(lg4_mm, 1)

            def transpose_combine(b):
                pe.wait_ge(comb_ready, b + 1)
                ps = banks[7].take(pe, combT_ready, b + 1)
                nc.tensor.transpose(ps[0:NE1, 0:P], comb[:], ident[:]).then_inc(comb_T, 1)

            def last_bias(b):
                pe.wait_ge(combT_ready, b + 1)
                ps = banks[7].take(pe, bias_ready, b + 1)
                mm(ps[:, 0:T], combT[:], b1_sb[:], True, True).then_inc(bias_mm, 1)

            def last_experts(b, k):
                if k == 0:
                    pe.wait_ge(x4_split, b + 1)
                ps = banks[2 + k % 2].take(pe, odd_ready if k % 2 else l1_even, NE1 // 2 * b + 2 * (k // 2 + 1))
                two = slice(2 * k, 2 * k + 2)
                split_product(ps[:].rearrange("p (e c) -> p e c", e=2),
                              [(x1_hi[:, c, :], x1_lo[:, c, :], w1_hi[:, c, two, :], w1_lo[:, c, two, :])
                               for c in range(CC)]).then_inc(l1_mm, 1)

            for t in TAIL_TICKS:
                last_qkv(t, qkv_product)
                tail_at(t, QK_T, transpose_qk)
                tail_at(t, SCORES, causal_scores)
                tail_at(t, PAT_T, transpose_rows)
                tail_at(t, AO, attend)
                tail_at(t, KEYS_T, transpose_keys)
                tail_at(t, Y_T, transpose_y)
                tail_at(t, XN4_T, transpose_last)
                tail_at(t, LOGITS, last_logits)
                tail_at(t, COMB_T, transpose_combine)
                tail_at(t, BIAS, last_bias)
                for group, offset in enumerate(WEIGHTS):
                    tail_at(t, offset, weights_on_all, group)
                for group, offset in enumerate(OUTPUTS):
                    tail_at(t, offset, output_experts, group)
                for k, offset in enumerate(LAST):
                    tail_at(t, offset, last_experts, k)


_OUT = ((8, 128, 256), "float32")


def kernel(**inputs):
    import numpy as _np
    import concourse.bacc as _bacc
    from concourse import mybir as _mybir
    from concourse.bass_utils import run_bass_kernel_spmd as _run

    a = {k: _np.asarray(v) for k, v in inputs.items()}
    nb = a["x"].shape[0]
    laid = {
        "x": a["x"],
        "ctx": a["ctx_2048"],
        "ctxT": a["ctx_2048"].transpose(2, 0, 1),
        "mask": a["mask_Bx1x2048_fk1"].reshape(nb, -1),
        "maskT": a["mask_Bx1x2048_fk1"].reshape(nb, -1).T,
        "g_xattn": a["g_xattn"],
        "g_ffn": a["g_ffn"],
        "wqT": a["L0_xattn_Wq"].T,
        "wkT": a["L0_xattn_Wk"].T,
        "wvT": a["L0_xattn_Wv"].T,
        "bq": a["L0_xattn_bq"].reshape(-1, 1),
        "bk": a["L0_xattn_bk"].reshape(-1, 1),
        "bv": a["L0_xattn_bv"].reshape(1, -1),
        "sim": a["L0_ffn_sim_matrix"],
        "gates": a["L0_ffn_gates"],
        "wqkv": _np.concatenate([a["L0_ffn_q_proj"], a["L0_ffn_k_proj"], a["L0_ffn_v_proj"]], axis=2),
        "wo": a["L0_ffn_o_proj"],
        "wkv_w": a["L1_xattn_w"].reshape(-1, 128).T,
        "wkv_u": a["L1_xattn_u"].reshape(-1, 128).T,
        "wg": a["L1_ffn_wg"],
        "w1c": a["L1_ffn_W"].transpose(2, 0, 1).reshape(2, 128, 8, 256).transpose(0, 2, 1, 3).reshape(16, 128, 256),
        "b1": a["L1_ffn_b"],
    }
    nc = _bacc.Bacc("TRN2", target_bir_lowering=False, num_devices=1)
    arrays, args = {}, []
    for name, value in laid.items():
        value = _np.ascontiguousarray(value)
        arrays[f"in_{name}_dram"] = value
        args.append(nc.dram_tensor(f"in_{name}_dram", value.shape, _mybir.dt.from_np(value.dtype),
                                   kind="ExternalInput").ap())
    args.append(nc.dram_tensor("out_dram", _OUT[0], _mybir.dt.from_np(_np.dtype(_OUT[1])),
                               kind="ExternalOutput").ap())
    flamingo_two_layers(nc, *args)
    r = _run(nc, [arrays], core_ids=[0])
    return r.results[0]["out_dram"]
```
